# Optimizing a Trainium2 kernel written in Bass

```python
import numpy as np
import jax
import jax.numpy as jnp

def _softmax(x, axis=-1):
    return jax.nn.softmax(x, axis=axis)

def _gelu(x):
    return jax.nn.gelu(x, approximate=True)

def _silu(x):
    return jax.nn.silu(x)

def _sigmoid(x):
    return jax.nn.sigmoid(x)

def _layernorm(x, axis=-1, eps=1e-05):
    m = jnp.mean(x, axis=axis, keepdims=True)
    v = jnp.var(x, axis=axis, keepdims=True)
    return (x - m) / jnp.sqrt(v + eps)

def _scatter_add(tgt, idx, src, axis=0):
    return tgt.at[idx].add(src)

def _segment_sum(src, seg, n):
    return jax.ops.segment_sum(src, seg, n)
kernel_name = 'mk_adj_ffn_d2_adj_r2_a1138b'

def setup_inputs(seed: int=0):
    np.random.seed(seed)
    _w = jnp.asarray

    def _rec_inputs():
        import jax
        import jax.numpy as jnp
        _gk = jax.random.key(seed)
        x = -0.0002928 + 1 * jax.random.normal(jax.random.fold_in(_gk, 1), (128, 64, 128), jnp.float32)
        _a = jax.random.bernoulli(jax.random.fold_in(_gk, 2), 0.125, (128, 64, 64))
        _a = jnp.logical_or(_a, jnp.swapaxes(_a, -1, -2))
        _a = jnp.logical_or(_a, jnp.eye(64, dtype=bool))
        adj = _a.astype(jnp.int32)
        return (x, adj)
    x, adj = _rec_inputs()

    def _L0_gnn_setup():
        import jax, jax.numpy as jnp
        import numpy as np
        NEG_BIG = -9000000000000000.0
        key = jax.random.key(seed)
        k1, k2, k3, k4 = jax.random.split(key, 4)
        B, N, FIN, FOUT = (8, 1024, 128, 128)
        inp = jax.random.normal(k1, (B, N, FIN), dtype=jnp.float32)
        adj = jax.random.randint(k2, (B, N, N), 0, 2, dtype=jnp.int32)
        W = jax.random.normal(k3, (FIN, FOUT), dtype=jnp.float32) * (1.414 / np.sqrt(FIN))
        a = jax.random.normal(k4, (2 * FOUT, 1), dtype=jnp.float32) * 0.1
        return {'input': inp, 'adj': adj, 'W': W, 'a': a}
    _L0_gnn_all = _L0_gnn_setup()
    _L0_gnn_in = {k: v for k, v in _L0_gnn_all.items() if k in ('W', 'a')}
    del _L0_gnn_all

    def _L0_ffn_setup():
        import jax, jax.numpy as jnp
        import numpy as np
        B, S, D, H, E, K = (8, 4096, 128, 512, 8, 2)
        key = jax.random.key(seed)
        ks = jax.random.split(key, 7)
        s_in = 1.0 / np.sqrt(D)
        s_hid = 1.0 / np.sqrt(H)
        return {'x': jax.random.normal(ks[0], (B, S, D), dtype=jnp.float32), 'Wg': jax.random.uniform(ks[1], (E, D), jnp.float32, -s_in, s_in), 'bg': jax.random.uniform(ks[2], (E,), jnp.float32, -s_in, s_in), 'W1': jax.random.uniform(ks[3], (E, H, D), jnp.float32, -s_in, s_in), 'b1': jax.random.uniform(ks[4], (E, H), jnp.float32, -s_in, s_in), 'W2': jax.random.uniform(ks[5], (E, D, H), jnp.float32, -s_hid, s_hid), 'b2': jax.random.uniform(ks[6], (E, D), jnp.float32, -s_hid, s_hid)}
    _L0_ffn_all = _L0_ffn_setup()
    _L0_ffn_in = {k: v for k, v in _L0_ffn_all.items() if k in ('Wg', 'bg', 'W1', 'b1', 'W2', 'b2')}
    del _L0_ffn_all

    def _L1_gnn_setup():
        import jax, jax.numpy as jnp
        import numpy as np
        OUT = 128
        NUM_LAYERS = 3

        def _gru_cell(inp, h, w_ih, w_hh, b_ih, b_hh):
            gi = inp @ w_ih.T + b_ih
            gh = h @ w_hh.T + b_hh
            i_r, i_z, i_n = jnp.split(gi, 3, axis=-1)
            h_r, h_z, h_n = jnp.split(gh, 3, axis=-1)
            r = jax.nn.sigmoid(i_r + h_r)
            z = jax.nn.sigmoid(i_z + h_z)
            n = jnp.tanh(i_n + r * h_n)
            return (1.0 - z) * n + z * h
        key = jax.random.key(seed)
        ks = jax.random.split(key, 8)
        B, N, D = (32, 256, 128)
        x = jax.random.normal(ks[0], (B, N, D), dtype=jnp.float32)
        adj = jax.random.randint(ks[1], (B, N, N), 0, 2, dtype=jnp.int32)
        s = 1.0 / np.sqrt(OUT)
        weight = jax.random.uniform(ks[2], (NUM_LAYERS, OUT, OUT), jnp.float32, -s, s)
        w_ih = jax.random.uniform(ks[3], (3 * OUT, OUT), jnp.float32, -s, s)
        w_hh = jax.random.uniform(ks[4], (3 * OUT, OUT), jnp.float32, -s, s)
        b_ih = jax.random.uniform(ks[5], (3 * OUT,), jnp.float32, -s, s)
        b_hh = jax.random.uniform(ks[6], (3 * OUT,), jnp.float32, -s, s)
        return {'x': x, 'adj': adj, 'weight': weight, 'w_ih': w_ih, 'w_hh': w_hh, 'b_ih': b_ih, 'b_hh': b_hh}
    _L1_gnn_all = _L1_gnn_setup()
    _L1_gnn_in = {k: v for k, v in _L1_gnn_all.items() if k in ('weight', 'w_ih', 'w_hh', 'b_ih', 'b_hh')}
    del _L1_gnn_all

    def _L1_ffn_setup():
        import jax, jax.numpy as jnp
        import numpy as np
        D_MODEL = 128
        N_EXPERTS = 16
        HIDDEN = 256
        SCALE = 0.02
        key = jax.random.key(seed)
        ks = jax.random.split(key, 5)
        x = jax.random.normal(ks[0], (4, 4096, D_MODEL), dtype=jnp.float32)
        gate_w = jax.random.normal(ks[1], (D_MODEL, N_EXPERTS), dtype=jnp.float32) * SCALE
        gate_b = jnp.zeros((N_EXPERTS,), dtype=jnp.float32)
        w1 = jax.random.normal(ks[2], (N_EXPERTS, D_MODEL, HIDDEN), dtype=jnp.float32) * SCALE
        w2 = jax.random.normal(ks[3], (N_EXPERTS, D_MODEL, HIDDEN), dtype=jnp.float32) * SCALE
        w3 = jax.random.normal(ks[4], (N_EXPERTS, HIDDEN, D_MODEL), dtype=jnp.float32) * SCALE
        return {'x': x, 'gate_w': gate_w, 'gate_b': gate_b, 'w1': w1, 'w2': w2, 'w3': w3}
    _L1_ffn_all = _L1_ffn_setup()
    _L1_ffn_in = {k: v for k, v in _L1_ffn_all.items() if k in ('gate_w', 'gate_b', 'w1', 'w2', 'w3')}
    del _L1_ffn_all
    return {'x': x, 'adj': adj, 'L0_gnn_W': _L0_gnn_in['W'], 'L0_gnn_a': _L0_gnn_in['a'], 'L0_ffn_Wg': _L0_ffn_in['Wg'], 'L0_ffn_bg': _L0_ffn_in['bg'], 'L0_ffn_W1': _L0_ffn_in['W1'], 'L0_ffn_b1': _L0_ffn_in['b1'], 'L0_ffn_W2': _L0_ffn_in['W2'], 'L0_ffn_b2': _L0_ffn_in['b2'], 'L1_gnn_weight': _L1_gnn_in['weight'], 'L1_gnn_w_ih': _L1_gnn_in['w_ih'], 'L1_gnn_w_hh': _L1_gnn_in['w_hh'], 'L1_gnn_b_ih': _L1_gnn_in['b_ih'], 'L1_gnn_b_hh': _L1_gnn_in['b_hh'], 'L1_ffn_gate_w': _L1_ffn_in['gate_w'], 'L1_ffn_gate_b': _L1_ffn_in['gate_b'], 'L1_ffn_w1': _L1_ffn_in['w1'], 'L1_ffn_w2': _L1_ffn_in['w2'], 'L1_ffn_w3': _L1_ffn_in['w3']}

def reference(x, adj, L0_gnn_W, L0_gnn_a, L0_ffn_Wg, L0_ffn_bg, L0_ffn_W1, L0_ffn_b1, L0_ffn_W2, L0_ffn_b2, L1_gnn_weight, L1_gnn_w_ih, L1_gnn_w_hh, L1_gnn_b_ih, L1_gnn_b_hh, L1_ffn_gate_w, L1_ffn_gate_b, L1_ffn_w1, L1_ffn_w2, L1_ffn_w3):
    import jax
    import jax.numpy as jnp

    def _L0_gnn_ref(input, adj, W, a):
        import jax, jax.numpy as jnp
        import numpy as np
        NEG_BIG = -9000000000000000.0
        alpha = 0.2
        h = jnp.matmul(input, W)
        F = h.shape[-1]
        a1, a2 = (a[:F, 0], a[F:, 0])
        s1 = jnp.einsum('bnf,f->bn', h, a1)
        s2 = jnp.einsum('bnf,f->bn', h, a2)
        e = s1[:, :, None] + s2[:, None, :]
        e = jax.nn.leaky_relu(e, negative_slope=alpha)
        e = jnp.where(adj > 0, e, NEG_BIG)
        attention = jax.nn.softmax(e, axis=2)
        h_prime = jnp.matmul(attention, h)
        return jax.nn.elu(h_prime)

    def _L0_ffn_ref(x, Wg, bg, W1, b1, W2, b2):
        import jax, jax.numpy as jnp
        import numpy as np
        B, S, D, H, E, K = (8, 4096, 128, 512, 8, 2)
        gate_scores = jnp.einsum('bsd,ed->bse', x, Wg) + bg
        topk_scores, topk_idx = jax.lax.top_k(gate_scores, K)
        topk_probs = jax.nn.softmax(topk_scores, axis=-1)
        combine = jnp.sum(topk_probs[..., None] * jax.nn.one_hot(topk_idx, E, dtype=x.dtype), axis=-2)
        out = jnp.zeros_like(x)
        for e in range(E):
            h = jax.nn.relu(jnp.einsum('bsd,hd->bsh', x, W1[e]) + b1[e])
            y = jnp.einsum('bsh,dh->bsd', h, W2[e]) + b2[e]
            out = out + combine[..., e:e + 1] * y
        return out

    def _L1_gnn_ref(x, adj, weight, w_ih, w_hh, b_ih, b_hh):
        import jax, jax.numpy as jnp
        import numpy as np
        OUT = 128
        NUM_LAYERS = 3

        def _gru_cell(inp, h, w_ih, w_hh, b_ih, b_hh):
            gi = inp @ w_ih.T + b_ih
            gh = h @ w_hh.T + b_hh
            i_r, i_z, i_n = jnp.split(gi, 3, axis=-1)
            h_r, h_z, h_n = jnp.split(gh, 3, axis=-1)
            r = jax.nn.sigmoid(i_r + h_r)
            z = jax.nn.sigmoid(i_z + h_z)
            n = jnp.tanh(i_n + r * h_n)
            return (1.0 - z) * n + z * h
        A = (adj != 0).astype(x.dtype)
        h = x
        L = weight.shape[0]
        for i in range(L):
            m = jnp.einsum('bnd,de->bne', h, weight[i])
            aggr = jnp.einsum('bst,bsd->btd', A, m)
            h = _gru_cell(aggr, h, w_ih, w_hh, b_ih, b_hh)
        return h

    def _L1_ffn_ref(x, gate_w, gate_b, w1, w2, w3):
        import jax, jax.numpy as jnp
        import numpy as np
        D_MODEL = 128
        N_EXPERTS = 16
        HIDDEN = 256
        SCALE = 0.02
        n_experts = w1.shape[0]
        logits = jnp.einsum('bsd,de->bse', x, gate_w) + gate_b
        probs = jax.nn.softmax(logits, axis=-1)
        top_probs, top_idx = jax.lax.top_k(probs, 2)
        top_probs = top_probs / jnp.sum(top_probs, axis=-1, keepdims=True)
        dispatch = jnp.sum(jax.nn.one_hot(top_idx, n_experts, dtype=x.dtype) * top_probs[..., None], axis=-2)
        h1 = jnp.einsum('bsd,edh->bseh', x, w1)
        h2 = jnp.einsum('bsd,edh->bseh', x, w2)
        hidden = jax.nn.silu(h1) * h2
        expert_out = jnp.einsum('bseh,eho->bseo', hidden, w3)
        return jnp.einsum('bseo,bse->bso', expert_out, dispatch)
    x = x + _L0_gnn_ref(_layernorm(x, axis=-1), adj, L0_gnn_W, L0_gnn_a)
    x = x + _L0_ffn_ref(_layernorm(x, axis=-1), L0_ffn_Wg, L0_ffn_bg, L0_ffn_W1, L0_ffn_b1, L0_ffn_W2, L0_ffn_b2)
    x = x + _L1_gnn_ref(_layernorm(x, axis=-1), adj, L1_gnn_weight, L1_gnn_w_ih, L1_gnn_w_hh, L1_gnn_b_ih, L1_gnn_b_hh)
    x = x + _L1_ffn_ref(_layernorm(x, axis=-1), L1_ffn_gate_w, L1_ffn_gate_b, L1_ffn_w1, L1_ffn_w2, L1_ffn_w3)
    return x

_drawn_inputs = setup_inputs


def setup_inputs(seed=0):
    import zlib

    import numpy as np

    out = dict(_drawn_inputs(seed))
    spreads = {'L1_ffn_gate_b': (0.0, 0.8)}
    factors = {'L0_ffn_b1': 2.709,
     'L1_ffn_gate_w': 8.0,
     'L1_ffn_w1': 8.0,
     'L1_ffn_w2': 8.0,
     'L1_ffn_w3': 8.0}
    for name, (base, spread) in spreads.items():
        noise = np.random.default_rng([zlib.crc32(name.encode()), seed]).standard_normal(out[name].shape)
        drawn = base * np.exp(spread * noise) if base else spread * noise
        out[name] = jnp.asarray(drawn.astype(out[name].dtype))
    for name, factor in factors.items():
        out[name] = (out[name] * factor).astype(out[name].dtype)
    return out
```

```python
import concourse.bass as bass
from concourse import mybir
from contextlib import ExitStack

F32 = mybir.dt.float32
BF16 = mybir.dt.bfloat16
I32 = mybir.dt.int32
U32 = mybir.dt.uint32
ALU = mybir.AluOpType
ACT = mybir.ActivationFunctionType
AX = mybir.AxisListType

P = 128
GRAPHS, N, D = 128, 64, 128
TOKENS = GRAPHS * N
NT = TOKENS // P
G = 4
NG = NT // G
GN = G * P
UNROLL = 8
NEG = -9.0e15
EPS = 1e-5
E0, H0 = 8, 512
E1, H1 = 16, 256
TOPK = 2
REGION = TOKENS + P
ROW = D + 1


class Steps:

    def __init__(self, sem, names):
        self.sem, self.names = sem, names.split()

    def upto(self, name, s):
        return s * len(self.names) + (self.names.index(name) + 1)


def wait(eng, steps, name, s):
    if type(s) is int and s < 0:
        return
    eng.wait_ge(steps.sem, steps.upto(name, s))


def alone(eng, c):
    eng.nop(nofuse=True)


class At:

    def __init__(self, i, j):
        self.s = 2 * i + j if type(i) is int else (i * 2 + j if j >= 0 else i * 2 - (-j))
        self.b = j % 2
        k = j // 2
        self.half = i + k if type(i) is int or k >= 0 else i - (-k)

    def back(self, n):
        return self.s - n


def tiles_of(experts):
    most = (TOKENS * TOPK - experts) // P + experts
    return -(-most // UNROLL) * UNROLL


def routing_names():
    return "scores top where wheref hot0 hot1 both ranked carried slot0 slot1 slots gap den p0 p1"


def program(nc, x, adj, gat_w, gat_wT, gat_a2, gate0_w, gate0_b, w1, b1, w2, b2,
            gnn_wT, w_ihT, w_hhT, b_ih, b_hh, gate1_w, gate1_b, w12, w3, out):
    with ExitStack() as ctx:
        def sb(name, shape, dt=F32):
            return ctx.enter_context(nc.sbuf_tensor(name, shape, dt))

        c = Shared()
        c.queue0 = nc.dram_tensor("queue0", (E0 * (REGION + P), ROW), F32, kind="Internal").ap()
        c.queue1 = nc.dram_tensor("queue1", (E1 * (REGION + P), ROW), F32, kind="Internal").ap()
        c.result0 = nc.dram_tensor("result0", (TOPK * TOKENS + 2 * E0 * P, D), F32, kind="Internal").ap()
        c.result1 = nc.dram_tensor("result1", (TOPK * TOKENS + 2 * E1 * P, D), F32, kind="Internal").ap()
        c.x = sb("x_res", [P, NT, D])
        c.ident = sb("ident", [P, P])
        c.before = sb("before", [P, P], BF16)
        c.ones = sb("ones", [P, P], BF16)
        c.iota_e = sb("iota_e", [P, E1 + 1])
        c.region = sb("region", [P, E1 + 1])
        c.carry = sb("carry", [P, E1])
        c.ids = sb("ids", [P, TOPK, NT], I32)
        c.prob = sb("prob", [P, TOPK, NT])
        c.half_neg = sb("half_neg", [P, G])
        c.pad = sb("pad", [P, 2 * E1, ROW])
        c.iota_j = sb("iota_j", [1, tiles_of(E1)])
        c.tile_row = sb("tile_row", [1, tiles_of(E1)], I32)
        c.tile_expert = sb("tile_expert", [1, tiles_of(E1)], I32)
        c.carry_i = sb("carry_i", [1, E1], I32)
        c.constants_made = ctx.enter_context(nc.semaphore("constants_made"))
        make_constants(nc, c)
        with ExitStack() as stage:
            up = stage.enter_context(nc.sbuf_tensor("w1_sb", [D, E0 * H0], F32))
            down = stage.enter_context(nc.sbuf_tensor("w2_sb", [P, E0 * H0], F32))
            up_b = stage.enter_context(nc.sbuf_tensor("b1_sb", [P, E0 * H0], F32))
            down_b = stage.enter_context(nc.sbuf_tensor("b2_sb", [P, E0 * D], F32))
            weights = ((up[:], w1), (down[:], w2), (up_b[:], b1.partition_broadcast(P)),
                       (down_b[:], b2.partition_broadcast(P)))
            gat_and_routing(nc, c, x, adj, gat_w, gat_wT, gat_a2, gate0_w, gate0_b, weights)
            tile_table(nc, c, E0)
            experts(nc, c, 0, c.queue0, c.result0, E0, H0 // P, up, down, up_b, down_b)
        with ExitStack() as stage:
            up = stage.enter_context(nc.sbuf_tensor("w12_sb", [D, E1 * 2 * H1], F32))
            down = stage.enter_context(nc.sbuf_tensor("w3_sb", [P, E1 * H1], F32))
            gru_and_routing(nc, c, adj, gnn_wT, w_ihT, w_hhT, b_ih, b_hh, gate1_w, gate1_b,
                            ((up[:], w12), (down[:], w3)))
            tile_table(nc, c, E1)
            experts(nc, c, 1, c.queue1, c.result1, E1, H1 // P, up, down, None, None)
        combine_out(nc, c, out)


class Shared:
    pass


def make_constants(nc, c):
    with ExitStack() as ctx:
        made = ctx.enter_context(nc.semaphore("filled"))
        block = ctx.enter_context(nc.Block())

        @block.gpsimd
        def _(pool):
            pool.memset(c.ident[:], 0.0).then_inc(made, 1)
            pool.memset(c.before[:], 1.0).then_inc(made, 1)
            pool.memset(c.ones[:], 1.0)
            pool.memset(c.half_neg[:], -0.5)
            pool.memset(c.pad[:, :, 0:D], 0.0)
            pool.iota(c.iota_e[:], pattern=[[1, E1 + 1]], base=0, channel_multiplier=0,
                      allow_small_or_imprecise_dtypes=True)
            pool.iota(c.region[:], pattern=[[REGION, E1 + 1]], base=0, channel_multiplier=0,
                      allow_small_or_imprecise_dtypes=True)
            pool.iota(c.iota_j[:], pattern=[[1, tiles_of(E1)]], base=0, channel_multiplier=0,
                      allow_small_or_imprecise_dtypes=True)
            for k in range(TOPK):
                pool.iota(c.ids[:, k, :], pattern=[[TOPK * P, NT]], base=k, channel_multiplier=TOPK)
            pool.iota(c.pad[:, :, D:ROW].bitcast(I32), pattern=[[P, 2 * E1], [1, 1]],
                      base=TOPK * TOKENS, channel_multiplier=1)
            pool.wait_ge(made, 2)
            pool.affine_select(out=c.ident[:], in_=c.ident[:], compare_op=ALU.not_equal, fill=1.0,
                               base=0, pattern=[[-1, P]], channel_multiplier=1)
            pool.affine_select(out=c.before[:], in_=c.before[:], compare_op=ALU.is_gt, fill=0.0,
                               base=0, pattern=[[1, P]], channel_multiplier=-1).then_inc(c.constants_made, 1)


def bc(ap, n):
    return ap.unsqueeze(len(ap.shape)).to_broadcast([*ap.shape, n])


def norm_stats(v, c, src, stats):
    alone(v, c)
    for t in range(G):
        last = v.bn_stats(stats[:, t, :], src[:, t, :])
    return last


def route_vector(v, c, r, V, A, Q, at, experts_n, gate_b, QR):
    s, b = at.s, at.b
    wait(v, Q, "scored", s)
    v.tensor_tensor(r.score[:, :, 0:experts_n], r.ps_score[:, 0:G * experts_n].rearrange("p (t e) -> p t e", t=G),
                    gate_b[:, None, :].to_broadcast([P, G, experts_n]), ALU.add).then_inc(V.sem, 1)
    wait(v, V, "scores", s)
    alone(v, c)
    for t in range(G):
        last = v.max(r.top[:, t, :], r.score[:, t, 0:experts_n])
    last.then_inc(V.sem, 1)
    wait(v, V, "top", s)
    alone(v, c)
    for t in range(G):
        last = v.max_index(r.where[:, t, :], r.top[:, t, :], r.score[:, t, 0:experts_n])
    last.then_inc(V.sem, 1)
    wait(v, V, "where", s)
    v.tensor_copy(r.wheref[:], r.where[:, :, 0:TOPK]).then_inc(V.sem, 1)
    wait(v, V, "wheref", s)
    iota = c.iota_e[:, None, 0:experts_n].to_broadcast([P, G, experts_n])
    for k in range(TOPK):
        v.tensor_tensor(r.hot[k][:], iota, bc(r.wheref[:, :, k], experts_n), ALU.is_equal).then_inc(V.sem, 1)
    wait(v, V, "hot1", s)
    wait(v, QR, "ranked", at.back(1))
    v.tensor_tensor(r.both[:], r.hot[0][:], r.hot[1][:], ALU.add).then_inc(V.sem, 1)


def route_vector_2(v, c, r, V, A, Q, at, experts_n, sigmoid=False):
    s, b = at.s, at.b
    carry = c.carry[:, 0:experts_n]
    wait(v, Q, "ranked", s)
    wait(v, V, "carried", at.back(1))
    v.tensor_tensor(r.rank[:], r.ps_rank[:, 0:G * experts_n].rearrange("p (t e) -> p t e", t=G),
                    carry[:, None, :].to_broadcast([P, G, experts_n]), ALU.add).then_inc(V.sem, 1)
    wait(v, V, "ranked", s)
    v.tensor_tensor(carry, r.ps_rank[:, G * experts_n:(G + 1) * experts_n], carry, ALU.add).then_inc(V.sem, 1)
    for k in range(TOPK):
        v.tensor_tensor(r.pick[k][:], r.hot[k][:], r.rank[:], ALU.mult).then_inc(r.picked, 1)
    for k in range(TOPK):
        v.wait_ge(r.picked, s * TOPK + (k + 1))
        v.tensor_reduce(r.slotf[:, k, :], r.pick[k][:], AX.X, ALU.add).then_inc(V.sem, 1)
    wait(v, V, "slot1", s)
    v.tensor_copy(r.slots[b][:], r.slotf[:]).then_inc(V.sem, 1)
    if sigmoid:
        wait(v, A, "p1", at.back(1))
    v.tensor_tensor(r.gap[:], r.top[:, :, 1], r.top[:, :, 0], ALU.subtract).then_inc(V.sem, 1)
    if sigmoid:
        return
    wait(v, A, "gap_exp", s)
    v.tensor_scalar(r.den[:], r.egap[:], 1.0, None, ALU.add).then_inc(V.sem, 1)
    wait(v, V, "den", s)
    v.reciprocal(c.prob[:, 0, bass.ds(s * G, G)], r.den[:]).then_inc(V.sem, 1)
    wait(v, V, "p0", s)
    v.tensor_tensor(c.prob[:, 1, bass.ds(s * G, G)], r.egap[:], c.prob[:, 0, bass.ds(s * G, G)],
                    ALU.mult).then_inc(V.sem, 1)


def route_tensor(pe, c, r, V, VR, Q, at, experts_n):
    wait(pe, V, "both", at.s)
    wait(pe, VR, "carried", at.back(1))
    for t in range(G + 1):
        cols = r.ps_rank[:, t * experts_n:(t + 1) * experts_n]
        for u in range(min(t, G - 1) + 1):
            last = pe.matmul(cols, c.before[:] if u == t else c.ones[:], r.both[:, u, :],
                             start=(u == 0), stop=(u == min(t, G - 1)))
    last.then_inc(Q.sem, 1)


def route_buffers(sb, pb, sem, prefix, experts_n):
    r = Shared()
    r.score = sb(prefix + "score", [P, G, experts_n])
    r.top = sb(prefix + "top", [P, G, 8])
    r.where = sb(prefix + "where", [P, G, 8], U32)
    r.wheref = sb(prefix + "wheref", [P, G, TOPK])
    r.hot = [sb(prefix + f"hot{k}", [P, G, experts_n]) for k in range(TOPK)]
    r.both = sb(prefix + "both", [P, G, experts_n], BF16)
    r.rank = sb(prefix + "rank", [P, G, experts_n])
    r.pick = [sb(prefix + f"pick{k}", [P, G, experts_n]) for k in range(TOPK)]
    r.slotf = sb(prefix + "slotf", [P, TOPK, G])
    r.slots = [sb(prefix + f"slots{b}", [P, TOPK, G], U32) for b in range(2)]
    r.gap = sb(prefix + "gap", [P, G])
    r.egap = sb(prefix + "egap", [P, G])
    r.den = sb(prefix + "den", [P, G])
    r.rows = [[sb(prefix + f"rows{k}_{b}", [P, G, ROW]) for b in range(2)] for k in range(TOPK)]
    r.picked = sem(prefix + "picked")
    r.queued = [sem(prefix + f"queued{b}") for b in range(2)]
    return r


def queue_rows(pool, c, r, V, A, queue, at):
    wait(pool, V, "slots", at.s)
    wait(pool, A, "rows_copied", at.s)
    alone(pool, c)
    for k in range(TOPK):
        for t in range(G):
            pool.indirect_dma_start(
                out=queue, out_offset=bass.IndirectOffsetOnAxis(ap=r.slots[at.b][:, k, t:t + 1], axis=0),
                in_=r.rows[k][at.b][:, t, :], in_offset=None).then_inc(r.queued[at.b], 16)


def pipelined(eng, body, groups):
    body(At(0, 0), True, False)
    body(At(0, 1), True, True)
    with eng.Fori(1, groups // 2) as i:
        body(At(i, 0), True, True)
        body(At(i, 1), True, True)
    body(At(groups // 2, 0), False, True)


def prev(at):
    p = At.__new__(At)
    p.s, p.b = at.s - 1, 1 - at.b
    p.half = at.half - 1 if at.b == 0 else at.half
    return p


def gat_and_routing(nc, c, x, adj, gat_w, gat_wT, gat_a2, gate_w, gate_b, weights):
    with ExitStack() as ctx:
        def sb(name, shape, dt=F32):
            return ctx.enter_context(nc.sbuf_tensor("a_" + name, shape, dt))

        def pb(name, shape, dt=F32):
            return ctx.enter_context(nc.psum_tensor("a_" + name, shape, dt))

        def sem(name):
            return ctx.enter_context(nc.semaphore("a_" + name))

        w_sb = sb("w", [D, D])
        wT_sb = sb("wT", [D, D])
        a2_sb = sb("a2", [D, 2])
        wa_sb = sb("wa", [D, 2])
        wa2_wide = sb("wa2_wide", [D, N])
        gw_sb = sb("gw", [D, E0])
        gb_sb = sb("gb", [P, E0])
        adj_sb = [sb(f"adj{b}", [P, G, N], I32) for b in range(2)]
        neg = sb("neg", [P, G, N])
        stats = [sb(f"stats{k}", [P, G, 6]) for k in range(2)]
        mv = [sb(f"mv{k}", [P, G, 2]) for k in range(2)]
        vare = [sb(f"vare{k}", [P, G]) for k in range(2)]
        rstd = [sb(f"rstd{k}", [P, G]) for k in range(2)]
        xn = sb("xn", [P, G, D])
        xnT = sb("xnT", [P, GN])
        h = [sb(f"h{b}", [P, G, D]) for b in range(2)]
        s1 = sb("s1", [P, G])
        e = sb("e", [P, G, N])
        rowmax = sb("rowmax", [P, G])
        pbd = [sb(f"pbd{b}", [P, G, P]) for b in range(2)]
        rowsum = sb("rowsum", [P, G])
        rinv = [sb(f"rinv{b}", [P, G]) for b in range(2)]
        pT = [sb(f"pT{b}", [P, GN]) for b in range(2)]
        z = sb("z", [P, G, D])
        zmin = sb("zmin", [P, G, D])
        zexp = sb("zexp", [P, G, D])
        xz = sb("xz", [P, G, D])
        rT = sb("rT", [P, GN])
        r = route_buffers(sb, pb, sem, "r_", E0)

        ps_t = pb("ps_t", [P, GN])
        ps_h = pb("ps_h", [P, GN])
        ps_s = pb("ps_s", [P, GN])
        ps_p = pb("ps_p", [P, GN])
        ps_o = pb("ps_o", [P, GN])
        ps_r = pb("ps_r", [P, GN])
        r.ps_score = pb("ps_score", [P, GN])[:, :]
        r.ps_rank = pb("ps_rank", [P, GN])[:, :]

        loaded = sem("weights_loaded")
        arrived = [sem(f"arrived{b}") for b in range(2)]
        ready = sem("weights_ready")
        V1 = Steps(sem("v_attend"), "stats agg vare normed neg s1 e lrelu masked max centred sum rinv")
        V2 = Steps(sem("v_update"), "z zmin xz x1 stats agg vare normed ids " + routing_names())
        A1 = Steps(sem("a_attend"), "xnT h exp pT")
        A2 = Steps(sem("a_update"), "zexp rT rows_copied gap_exp")
        Q1 = Steps(sem("q_attend"), "turned hs probs_turned")
        Q2 = Steps(sem("q_update"), "mixed turned scored ranked")
        G1 = Steps(sem("g_attend"), "rstd")
        G2 = Steps(sem("g_update"), "rstd")

        block = ctx.enter_context(nc.Block())

        @block.sync
        def _(sp):
            for dst, src in ((w_sb[:], gat_w), (wT_sb[:], gat_wT), (a2_sb[:], gat_a2), (gw_sb[:], gate_w),
                             (gb_sb[:], gate_b.partition_broadcast(P))):
                sp.dma_start(dst, src).then_inc(loaded, 16)

            def load(at, first):
                if not first:
                    sp.wait_ge(arrived[at.b], 32 * at.half)
                    alone(sp, c)
                    wait(sp, V1, "neg", at.back(2))
                    alone(sp, c)
                rows = x[bass.ds(at.s * GN, GN), :]
                sp.dma_start(c.x[:, bass.ds(at.s * G, G), :],
                             rows.rearrange("(t p) d -> p t d", p=P)).then_inc(arrived[at.b], 16)
                sp.dma_start(adj_sb[at.b][:], adj[bass.ds(at.s * GN, GN), :]
                             .rearrange("(t p) d -> p t d", p=P)).then_inc(arrived[at.b], 16)

            load(At(0, 0), True)
            load(At(0, 1), True)
            with sp.Fori(1, NG // 2) as i:
                load(At(i, 0), False)
                load(At(i, 1), False)
            for dst, src in weights:
                sp.dma_start(dst, src).then_inc(loaded, 16)
            sp.wait_ge(loaded, 16 * (5 + len(weights)))
            for b in range(2):
                sp.wait_ge(r.queued[b], 16 * TOPK * G * (NG // 2))

        @block.gpsimd
        def _(pool):
            def body(at, new, old):
                if new:
                    wait(pool, V1, "vare", at.s)
                    pool.tensor_tensor(rstd[0][:], vare[0][:], c.half_neg[:], ALU.pow).then_inc(G1.sem, 1)
                if old:
                    p = prev(at)
                    wait(pool, V2, "vare", p.s)
                    pool.tensor_tensor(rstd[1][:], vare[1][:], c.half_neg[:], ALU.pow).then_inc(G2.sem, 1)
                    queue_rows(pool, c, r, V2, A2, c.queue0, p)

            pipelined(pool, body, NG)

        @block.vector
        def _(v):
            v.tensor_copy(c.carry[:], c.region[:, 0:E1])
            for b in range(2):
                v.memset(pbd[b][:], 0.0)
            v.wait_ge(ready, 1)
            v.tensor_copy(wa_sb[:], ps_t[:, 0:2]).then_inc(ready, 1)
            v.wait_ge(ready, 2)
            v.tensor_copy(wa2_wide[:], wa_sb[:, 1:2].to_broadcast([D, N])).then_inc(ready, 1)

            def update_1(p):
                xs = c.x[:, bass.ds(p.s * G, G), :]
                wait(v, Q2, "mixed", p.s)
                wait(v, V1, "rinv", p.s)
                v.tensor_tensor(z[:], ps_o[:].rearrange("p (t d) -> p t d", t=G), bc(rinv[p.b][:], D),
                                ALU.mult).then_inc(V2.sem, 1)
                wait(v, V2, "z", p.s)
                v.tensor_scalar(zmin[:], z[:], 0.0, None, ALU.min).then_inc(V2.sem, 1)
                v.scalar_tensor_tensor(out=xz[:], in0=z[:], scalar=0.0, in1=xs, op0=ALU.max,
                                       op1=ALU.add).then_inc(V2.sem, 1)

            def update_2(p):
                xs = c.x[:, bass.ds(p.s * G, G), :]
                wait(v, V2, "xz", p.s)
                wait(v, A2, "zexp", p.s)
                v.scalar_tensor_tensor(out=xs, in0=zexp[:], scalar=-1.0, in1=xz[:], op0=ALU.add,
                                       op1=ALU.add).then_inc(V2.sem, 1)
                wait(v, V2, "x1", p.s)
                norm_stats(v, c, xs, stats[1]).then_inc(V2.sem, 1)
                wait(v, V2, "stats", p.s)
                alone(v, c)
                for t in range(G):
                    last = v.bn_aggr(mv[1][:, t, :], stats[1][:, t, :])
                last.then_inc(V2.sem, 1)
                wait(v, V2, "agg", p.s)
                v.tensor_scalar(vare[1][:], mv[1][:, :, 1], EPS, None, ALU.add).then_inc(V2.sem, 1)

            def update_3(p):
                wait(v, G2, "rstd", p.s)
                if type(p.s) is not int or p.s >= 2:
                    v.wait_ge(r.queued[p.b], 16 * TOPK * G * p.half)
                for t in range(G):
                    last = v.tensor_scalar(r.rows[0][p.b][:, t, 0:D], c.x[:, p.s * G + t, :],
                                           mv[1][:, t, 0:1], rstd[1][:, t:t + 1], ALU.subtract, ALU.mult)
                last.then_inc(V2.sem, 1)
                for k in range(TOPK):
                    last = v.tensor_copy(r.rows[k][p.b][:, :, D:ROW].bitcast(I32),
                                         c.ids[:, k, bass.ds(p.s * G, G)].unsqueeze(2))
                last.then_inc(V2.sem, 1)

            def attend_1(at):
                v.wait_ge(arrived[at.b], 32 * at.half + 32)
                norm_stats(v, c, c.x[:, bass.ds(at.s * G, G), :], stats[0]).then_inc(V1.sem, 1)
                wait(v, V1, "stats", at.s)
                alone(v, c)
                for t in range(G):
                    last = v.bn_aggr(mv[0][:, t, :], stats[0][:, t, :])
                last.then_inc(V1.sem, 1)
                wait(v, V1, "agg", at.s)
                v.tensor_scalar(vare[0][:], mv[0][:, :, 1], EPS, None, ALU.add).then_inc(V1.sem, 1)

            def attend_2(at):
                wait(v, G1, "rstd", at.s)
                wait(v, Q1, "turned", at.back(1))
                for t in range(G):
                    last = v.tensor_scalar(xn[:, t, :], c.x[:, at.s * G + t, :], mv[0][:, t, 0:1],
                                           rstd[0][:, t:t + 1], ALU.subtract, ALU.mult)
                last.then_inc(V1.sem, 1)
                v.tensor_scalar(neg[:], adj_sb[at.b][:], 0.0, NEG, ALU.is_le, ALU.mult).then_inc(V1.sem, 1)

            def attend_3(at):
                wait(v, Q1, "hs", at.s)
                v.tensor_copy(s1[:], ps_s[:, G * N:G * N + G]).then_inc(V1.sem, 1)
                wait(v, V1, "s1", at.s)
                if type(at.s) is not int or at.s >= 1:
                    wait(v, A1, "exp", at.back(1))
                v.tensor_tensor(e[:], ps_s[:, 0:G * N].rearrange("p (t n) -> p t n", t=G), bc(s1[:], N),
                                ALU.add).then_inc(V1.sem, 1)
                wait(v, V1, "e", at.s)
                v.scalar_tensor_tensor(out=e[:], in0=e[:], scalar=0.2, in1=e[:], op0=ALU.mult,
                                       op1=ALU.max).then_inc(V1.sem, 1)
                wait(v, V1, "lrelu", at.s)
                v.tensor_tensor(e[:], e[:], neg[:], ALU.add).then_inc(V1.sem, 1)
                wait(v, V1, "masked", at.s)
                v.tensor_reduce(rowmax[:], e[:], AX.X, ALU.max).then_inc(V1.sem, 1)
                wait(v, V1, "max", at.s)
                v.tensor_tensor(e[:], e[:], bc(rowmax[:], N), ALU.subtract).then_inc(V1.sem, 1)

            def attend_4(at):
                wait(v, A1, "exp", at.s)
                v.tensor_reduce(rowsum[:], pbd[at.b][:], AX.X, ALU.add).then_inc(V1.sem, 1)
                wait(v, V1, "sum", at.s)
                v.reciprocal(rinv[at.b][:], rowsum[:]).then_inc(V1.sem, 1)

            def body(at, new, old):
                p = prev(at) if old else None
                if old:
                    update_1(p)
                if new:
                    attend_1(at)
                if old:
                    update_2(p)
                if new:
                    attend_2(at)
                if old:
                    update_3(p)
                if new:
                    attend_3(at)
                if old:
                    route_vector(v, c, r, V2, A2, Q2, p, E0, gb_sb[:], Q2)
                if new:
                    attend_4(at)
                if old:
                    route_vector_2(v, c, r, V2, A2, Q2, p, E0)

            pipelined(v, body, NG)

        @block.scalar
        def _(act):
            act.wait_ge(ready, 3)

            def body(at, new, old):
                p = prev(at) if old else None
                if old:
                    wait(act, V2, "zmin", p.s)
                    act.activation(zexp[:], zmin[:], ACT.Exp).then_inc(A2.sem, 1)
                if new:
                    wait(act, Q1, "turned", at.s)
                    wait(act, Q1, "hs", at.back(1))
                    act.activation(xnT[:], ps_t[:], ACT.Copy).then_inc(A1.sem, 1)
                    wait(act, Q1, "hs", at.s)
                    act.activation(h[at.b][:].rearrange("p t d -> p (t d)"), ps_h[:], ACT.Copy).then_inc(A1.sem, 1)
                if old:
                    wait(act, Q2, "turned", p.s)
                    act.activation(rT[:], ps_r[:], ACT.Copy).then_inc(A2.sem, 1)
                    act.activation(r.rows[1][p.b][:, :, 0:D], r.rows[0][p.b][:, :, 0:D], ACT.Copy).then_inc(A2.sem, 1)
                if new:
                    wait(act, V1, "centred", at.s)
                    for q in range(2):
                        rows = slice(q * N, (q + 1) * N)
                        last = act.activation(pbd[at.b][rows, :, q * N:(q + 1) * N], e[rows, :, :], ACT.Exp)
                    last.then_inc(A1.sem, 1)
                    wait(act, Q1, "probs_turned", at.s)
                    act.activation(pT[at.b][:], ps_p[:], ACT.Copy).then_inc(A1.sem, 1)
                if old:
                    wait(act, V2, "gap", p.s)
                    act.activation(r.egap[:], r.gap[:], ACT.Exp).then_inc(A2.sem, 1)

            pipelined(act, body, NG)

        @block.tensor
        def _(pe):
            pe.wait_ge(loaded, 16 * 5)
            pe.matmul(ps_t[:, 0:2], wT_sb[:], a2_sb[:], start=True, stop=True).then_inc(ready, 1)
            pe.wait_ge(ready, 3)

            def body(at, new, old):
                p = prev(at) if old else None
                if old:
                    wait(pe, A1, "pT", p.s)
                    wait(pe, V2, "z", p.back(1))
                    for t in range(G):
                        last = pe.matmul(ps_o[:, t * P:(t + 1) * P], pT[p.b][:, t * P:(t + 1) * P],
                                         h[p.b][:, t, :], start=True, stop=True)
                    last.then_inc(Q2.sem, 1)
                if new:
                    wait(pe, V1, "normed", at.s)
                    wait(pe, A1, "xnT", at.back(1))
                    for t in range(G):
                        last = pe.transpose(ps_t[:, t * P:(t + 1) * P], xn[:, t, :], c.ident[:])
                    last.then_inc(Q1.sem, 1)
                    wait(pe, A1, "xnT", at.s)
                    wait(pe, A1, "h", at.back(1))
                    wait(pe, V1, "e", at.back(1))
                    for t in range(G):
                        pe.matmul(ps_h[:, t * P:(t + 1) * P], xnT[:, t * P:(t + 1) * P], w_sb[:],
                                  start=True, stop=True)
                    for t in range(G):
                        pe.matmul(ps_s[:, G * N + t:G * N + t + 1], xnT[:, t * P:(t + 1) * P], wa_sb[:, 0:1],
                                  start=True, stop=True)
                    for q in range(2):
                        last = pe.matmul(ps_s[q * N:(q + 1) * N, 0:G * N], wa2_wide[:],
                                         xnT[:].rearrange("p (t q n) -> p t q n", t=G, q=2)[:, :, q, :],
                                         start=True, stop=True)
                    last.then_inc(Q1.sem, 1)
                if old:
                    wait(pe, V2, "normed", p.s)
                    wait(pe, A2, "rT", p.back(1))
                    for t in range(G):
                        last = pe.transpose(ps_r[:, t * P:(t + 1) * P], r.rows[0][p.b][:, t, 0:D], c.ident[:])
                    last.then_inc(Q2.sem, 1)
                    wait(pe, A2, "rT", p.s)
                    wait(pe, V2, "scores", p.back(1))
                    for t in range(G):
                        last = pe.matmul(r.ps_score[:, t * E0:(t + 1) * E0], rT[:, t * P:(t + 1) * P], gw_sb[:],
                                         start=True, stop=True)
                    last.then_inc(Q2.sem, 1)
                if new:
                    wait(pe, A1, "exp", at.s)
                    wait(pe, A1, "pT", at.back(1))
                    for t in range(G):
                        last = pe.transpose(ps_p[:, t * P:(t + 1) * P], pbd[at.b][:, t, :], c.ident[:])
                    last.then_inc(Q1.sem, 1)
                if old:
                    route_tensor(pe, c, r, V2, V2, Q2, p, E0)

            pipelined(pe, body, NG)


def gru_and_routing(nc, c, adj, gnn_wT, w_ihT, w_hhT, b_ih, b_hh, gate_w, gate_b, weights):
    pairs, layers = NG // 2, 3
    with ExitStack() as ctx:
        def sb(name, shape, dt=F32):
            return ctx.enter_context(nc.sbuf_tensor("g_" + name, shape, dt))

        def pb(name, shape, dt=F32):
            return ctx.enter_context(nc.psum_tensor("g_" + name, shape, dt))

        def sem(name):
            return ctx.enter_context(nc.semaphore("g_" + name))

        two = range(2)
        wT_sb = sb("wT", [D, layers * D])
        wi_sb = sb("wi", [D, 3 * D])
        wh_sb = sb("wh", [D, 3 * D])
        wv_sb = sb("wv", [D, layers, 3 * D])
        bi_sb = sb("bi", [D, 3])
        bh_sb = sb("bh", [D, 3])
        bsum = sb("bsum", [D, 3])
        gw_sb = sb("gw", [D, E1])
        gb_sb = sb("gb", [P, E1])
        y = [sb(f"y{b}", [P, G, TOPK, D]) for b in two]
        adj_sb = [sb(f"adj{b}", [P, G, N], I32) for b in two]
        edges = [sb(f"edges{b}", [P, G, P]) for b in two]
        stats = [sb(f"stats{k}", [P, G, 6]) for k in two]
        mv = [sb(f"mv{k}", [P, G, 2]) for k in two]
        vare = [sb(f"vare{k}", [P, G]) for k in two]
        rstd = [sb(f"rstd{k}", [P, G]) for k in two]
        xn = sb("xn", [P, G, D])
        state = [[sb(f"state{l}_{b}", [D, GN]) for b in two] for l in range(layers + 1)]
        tok = [sb(f"tok{b}", [P, G, D]) for b in two]
        agg = [sb(f"agg{b}", [D, GN]) for b in two]
        rg = [sb(f"rg{b}", [D, GN]) for b in two]
        zg = [sb(f"zg{b}", [D, GN]) for b in two]
        cand = [sb(f"cand{b}", [D, GN]) for b in two]
        new = [sb(f"new{b}", [D, GN]) for b in two]
        rT = sb("rT", [P, GN])
        r = route_buffers(sb, pb, sem, "q_", E1)

        ps_r, ps_z = pb("ps_r", [P, GN]), pb("ps_z", [P, GN])
        ps_n = [pb(f"ps_n{b}", [P, GN]) for b in two]
        ps_hn = [pb(f"ps_hn{b}", [P, GN]) for b in two]
        ps_m = pb("ps_m", [P, GN])
        ps_q = pb("ps_q", [P, GN])
        r.ps_score = ps_q[:, 0:G * E1]
        r.ps_rank = ps_q[:, G * E1:G * E1 + (G + 1) * E1]

        loaded, ready = sem("weights_loaded"), sem("weights_ready")
        arrived = [sem(f"arrived{b}") for b in two]
        s_turned, s_agged, s_gates = sem("turned"), sem("agged"), sem("gates")
        s_tok, s_aggT, s_sig, s_new = sem("tok"), sem("aggT"), sem("sigmoids"), sem("new")
        VR = Steps(sem("v_run"), "reset cand diff scaled state")
        VH = Steps(sem("v_head"), "add0 x2 stats agg vare normed")
        VE = Steps(sem("v_edges"), "edges")
        QH, AH, GH = Steps(sem("q_head"), "turned"), Steps(sem("a_head"), "state"), Steps(sem("g_head"), "rstd")
        VT = Steps(sem("v_tail"), "x3 stats agg vare normed ids")
        VS = Steps(sem("v_scores"), "scores top where wheref hot0 hot1 both")
        VK = Steps(sem("v_ranks"), "ranked carried slot0 slot1 slots gap")
        QT1, QT2, QT3, QT4 = (Steps(sem(f"q_tail{k}"), n) for k, n in enumerate(("back", "turned", "scored", "ranked")))
        AT1, AT2 = Steps(sem("a_tail_rows"), "rT rows_copied"), Steps(sem("a_tail_probs"), "p0 p1")
        GT = Steps(sem("g_tail"), "rstd")

        block = ctx.enter_context(nc.Block())

        def run_steps(eng, body):
            body(-1, True, False, False)
            body(0, True, True, False)
            body(1, True, True, True)
            with eng.Fori(2, pairs - 1) as n:
                body(n, True, True, True)
            body(pairs - 1, False, True, True)
            body(pairs, False, False, True)

        def u_of(n, layer, b):
            return n * 6 + (2 * layer + b)

        def after(eng, s, u, back=0):
            if type(u) is int and u - back < 0:
                return
            eng.wait_ge(s, u + (1 - back))

        def after_step(eng, steps, name, u, back=0):
            if type(u) is int and u - back < 0:
                return
            eng.wait_ge(steps.sem, u * 5 + (steps.names.index(name) + 1 - 5 * back))

        def group(n, b):
            return At(n, b)

        @block.sync
        def _(sp):
            first = ((wT_sb[:], gnn_wT), (wi_sb[:], w_ihT), (wh_sb[:], w_hhT), (bi_sb[:], b_ih), (bh_sb[:], b_hh),
                     (gw_sb[:], gate_w), (gb_sb[:], gate_b.partition_broadcast(P)))
            for dst, src in first:
                sp.dma_start(dst, src).then_inc(loaded, 16)

            def load(at):
                if type(at.s) is not int or at.s >= 2:
                    sp.wait_ge(arrived[at.b], 32 * at.half)
                    alone(sp, c)
                    wait(sp, VH, "x2", at.back(2))
                    alone(sp, c)
                    wait(sp, VE, "edges", at.back(2))
                    alone(sp, c)
                sp.dma_start(y[at.b][:], results_of(c.result0, at.s)).then_inc(arrived[at.b], 16)
                sp.dma_start(adj_sb[at.b][:], adj[bass.ds(at.s * GN, GN), :]
                             .rearrange("(t p) d -> p t d", p=P)).then_inc(arrived[at.b], 16)

            load(At(0, 0))
            load(At(0, 1))
            for dst, src in weights:
                sp.dma_start(dst, src).then_inc(loaded, 16)
            with sp.Fori(1, pairs) as i:
                load(At(i, 0))
                load(At(i, 1))
            sp.wait_ge(loaded, 16 * (len(first) + len(weights)))
            for b in two:
                sp.wait_ge(r.queued[b], 16 * TOPK * G * pairs)

        @block.gpsimd
        def _(pool):
            def head(at):
                wait(pool, VH, "vare", at.s)
                pool.tensor_tensor(rstd[0][:], vare[0][:], c.half_neg[:], ALU.pow).then_inc(GH.sem, 1)

            def tail(at):
                wait(pool, VT, "vare", at.s)
                pool.tensor_tensor(rstd[1][:], vare[1][:], c.half_neg[:], ALU.pow).then_inc(GT.sem, 1)

            def body(n, has_head, has_run, has_tail):
                if has_tail:
                    tail(group(n - 1, 0))
                    tail(group(n - 1, 1))
                if has_head:
                    head(group(n + 1, 0))
                if has_tail:
                    queue_rows(pool, c, r, VK, AT1, c.queue1, group(n - 1, 0))
                if has_head:
                    head(group(n + 1, 1))
                if has_tail:
                    queue_rows(pool, c, r, VK, AT1, c.queue1, group(n - 1, 1))

            run_steps(pool, body)

        @block.tensor
        def _(pe):
            pe.wait_ge(loaded, 16 * (7 + len(weights)))
            for l in range(layers):
                last = pe.matmul((ps_r, ps_z, ps_m)[l][:, 0:3 * D], wT_sb[:, l * D:(l + 1) * D], wi_sb[:],
                                 start=True, stop=True)
            last.then_inc(ready, 1)
            pe.wait_ge(ready, 2)

            def run(n, l, b):
                u = u_of(n, l, b)
                h = state[l][b]
                at = group(n, b)
                if l == 0:
                    wait(pe, AH, "state", at.s)
                else:
                    after_step(pe, VR, "state", u, 2)
                after_step(pe, VR, "cand", u, 2)
                for t in range(G):
                    last = pe.transpose(ps_n[b][:, t * P:(t + 1) * P], h[:, t * P:(t + 1) * P], c.ident[:])
                last.then_inc(s_turned, 1)
                pe.matmul(ps_hn[b][:], wh_sb[:, 2 * D:3 * D], h[:], start=True, stop=True)
                after(pe, s_tok, u)
                if l == 0:
                    wait(pe, VE, "edges", at.s)
                for t in range(G):
                    last = pe.matmul(ps_n[b][:, t * P:(t + 1) * P], tok[b][:, t, :], edges[b][:, t, :],
                                     start=True, stop=True)
                last.then_inc(s_agged, 1)
                after(pe, s_sig, u, 1)
                pe.matmul(ps_r[:], wh_sb[:, 0:D], h[:], start=True, stop=False)
                pe.matmul(ps_z[:], wh_sb[:, D:2 * D], h[:], start=True, stop=False)
                after(pe, s_aggT, u)
                pe.matmul(ps_r[:], wv_sb[:, l, 0:D], agg[b][:], start=False, stop=True)
                pe.matmul(ps_z[:], wv_sb[:, l, D:2 * D], agg[b][:], start=False, stop=True)
                pe.matmul(ps_n[b][:], wv_sb[:, l, 2 * D:3 * D], agg[b][:], start=True,
                          stop=True).then_inc(s_gates, 1)

            def head(at):
                wait(pe, VH, "normed", at.s)
                for t in range(G):
                    last = pe.transpose(ps_m[:, t * P:(t + 1) * P], xn[:, t, :], c.ident[:])
                last.then_inc(QH.sem, 1)

            def tail_back(n, b):
                after_step(pe, VR, "state", u_of(n - 1, 2, b))
                for t in range(G):
                    last = pe.transpose(ps_m[:, t * P:(t + 1) * P], state[layers][b][:, t * P:(t + 1) * P],
                                        c.ident[:])
                last.then_inc(QT1.sem, 1)

            def tail_turn(at):
                wait(pe, VT, "normed", at.s)
                for t in range(G):
                    last = pe.transpose(ps_m[:, t * P:(t + 1) * P], r.rows[0][at.b][:, t, 0:D], c.ident[:])
                last.then_inc(QT2.sem, 1)

            def tail_score(at):
                wait(pe, AT1, "rT", at.s)
                wait(pe, VK, "carried", at.back(1))
                for t in range(G):
                    last = pe.matmul(r.ps_score[:, t * E1:(t + 1) * E1], rT[:, t * P:(t + 1) * P], gw_sb[:],
                                     start=True, stop=True)
                last.then_inc(QT3.sem, 1)

            def body(n, has_head, has_run, has_tail):
                pa = [group(n - 1, b) for b in two] if has_tail else None
                nx = [group(n + 1, b) for b in two] if has_head else None
                if has_run:
                    run(n, 0, 0)
                if has_tail:
                    if has_head:
                        wait(pe, AH, "state", At(n, 1).s)
                    tail_back(n, 0)
                if has_run:
                    run(n, 0, 1)
                if has_tail:
                    wait(pe, VT, "x3", pa[0].s)
                    tail_back(n, 1)
                    wait(pe, VT, "x3", pa[1].s)
                    tail_turn(pa[0])
                if has_run:
                    run(n, 1, 0)
                if has_tail:
                    tail_score(pa[0])
                    tail_turn(pa[1])
                if has_run:
                    run(n, 1, 1)
                if has_tail:
                    wait(pe, VS, "both", pa[0].s)
                    tail_rank(pa[0])
                if has_run:
                    run(n, 2, 0)
                if has_head:
                    if has_tail:
                        wait(pe, AT1, "rT", pa[1].s)
                    head(nx[0])
                if has_tail:
                    wait(pe, VK, "carried", pa[0].s)
                    tail_score(pa[1])
                if has_run:
                    run(n, 2, 1)
                if has_tail:
                    tail_rank(pa[1])
                if has_head:
                    wait(pe, AH, "state", nx[0].s)
                    head(nx[1])
                    if not has_tail:
                        wait(pe, AH, "state", nx[1].s)

            def tail_rank(at):
                route_tensor(pe, c, r, VS, VK, QT4, at, E1)

            run_steps(pe, body)

        @block.scalar
        def _(act):
            def tok_out(n, l, b):
                u = u_of(n, l, b)
                after(act, s_turned, u)
                act.activation(tok[b][:].rearrange("p t d -> p (t d)"), ps_n[b][:], ACT.Copy).then_inc(s_tok, 1)

            def agg_out(n, l, b):
                u = u_of(n, l, b)
                after(act, s_agged, u)
                act.activation(agg[b][:], ps_n[b][:], ACT.Copy).then_inc(s_aggT, 1)

            def sigmoids(n, l, b):
                u = u_of(n, l, b)
                after(act, s_gates, u)
                after_step(act, VR, "scaled", u, 2)
                act.activation(rg[b][:], ps_r[:], ACT.Sigmoid, bias=bsum[:, 0:1])
                act.activation(zg[b][:], ps_z[:], ACT.Sigmoid, bias=bsum[:, 1:2]).then_inc(s_sig, 1)

            def new_out(n, l, b):
                u = u_of(n, l, b)
                after_step(act, VR, "cand", u)
                act.activation(new[b][:], cand[b][:], ACT.Tanh, bias=bi_sb[:, 2:3]).then_inc(s_new, 1)

            def tail_rows(at):
                wait(act, QT2, "turned", at.s)
                wait(act, QT3, "scored", at.back(1))
                act.activation(rT[:], ps_m[:], ACT.Copy).then_inc(AT1.sem, 1)
                act.activation(r.rows[1][at.b][:, :, 0:D], r.rows[0][at.b][:, :, 0:D], ACT.Copy).then_inc(AT1.sem, 1)

            def tail_probs(at):
                wait(act, VK, "gap", at.s)
                act.activation(c.prob[:, 0, bass.ds(at.s * G, G)], r.gap[:], ACT.Sigmoid, scale=-1.0).then_inc(AT2.sem, 1)
                act.activation(c.prob[:, 1, bass.ds(at.s * G, G)], r.gap[:], ACT.Sigmoid).then_inc(AT2.sem, 1)

            def head(at):
                wait(act, QH, "turned", at.s)
                act.activation(state[0][at.b][:], ps_m[:], ACT.Copy).then_inc(AH.sem, 1)

            def body(n, has_head, has_run, has_tail):
                pa = [group(n - 1, b) for b in two] if has_tail else None
                nx = [group(n + 1, b) for b in two] if has_head else None
                order = [(l, b) for l in range(layers) for b in two]
                for k, (l, b) in enumerate(order):
                    if has_run:
                        tok_out(n, l, b)
                        if k:
                            new_out(n, *order[k - 1])
                    if has_tail and k == 2:
                        tail_rows(pa[0])
                    if has_tail and k == 3:
                        tail_rows(pa[1])
                    if has_run:
                        agg_out(n, l, b)
                        sigmoids(n, l, b)
                    if has_tail and k == 4:
                        tail_probs(pa[0])
                    if has_head and k == 4:
                        head(nx[0])
                if has_run:
                    new_out(n, *order[-1])
                if has_tail:
                    tail_probs(pa[1])
                if has_head:
                    head(nx[1])

            run_steps(act, body)

        @block.vector
        def _(v):
            for b in two:
                v.memset(edges[b][:], 0.0)
            v.tensor_copy(c.carry[:], c.region[:, 0:E1])
            v.wait_ge(ready, 1)
            for l in range(layers):
                v.tensor_copy(wv_sb[:, l, :], (ps_r, ps_z, ps_m)[l][:, 0:3 * D])
            v.tensor_tensor(bsum[:], bi_sb[:], bh_sb[:], ALU.add).then_inc(ready, 1)

            def gates_1(n, l, b):
                u = u_of(n, l, b)
                after(v, s_sig, u)
                v.scalar_tensor_tensor(out=cand[b][:], in0=ps_hn[b][:], scalar=bh_sb[:, 2:3], in1=rg[b][:],
                                       op0=ALU.add, op1=ALU.mult).then_inc(VR.sem, 1)
                after_step(v, VR, "reset", u)
                v.tensor_tensor(cand[b][:], ps_n[b][:], cand[b][:], ALU.add).then_inc(VR.sem, 1)

            def gates_2(n, l, b):
                u = u_of(n, l, b)
                after(v, s_new, u)
                v.tensor_tensor(rg[b][:], state[l][b][:], new[b][:], ALU.subtract).then_inc(VR.sem, 1)
                after_step(v, VR, "diff", u)
                v.tensor_tensor(rg[b][:], rg[b][:], zg[b][:], ALU.mult).then_inc(VR.sem, 1)
                after_step(v, VR, "scaled", u)
                if l == layers - 1:
                    if type(n) is not int or n >= 1:
                        wait(v, QT1, "back", group(n - 1, b).s)
                v.tensor_tensor(state[l + 1][b][:], rg[b][:], new[b][:], ALU.add).then_inc(VR.sem, 1)

            def normalise(dst, at, k):
                for t in range(G):
                    last = v.tensor_scalar(dst[:, t, 0:D], c.x[:, at.s * G + t, :], mv[k][:, t, 0:1],
                                           rstd[k][:, t:t + 1], ALU.subtract, ALU.mult)
                return last

            def statistics(S, at, k):
                norm_stats(v, c, c.x[:, bass.ds(at.s * G, G), :], stats[k]).then_inc(S.sem, 1)
                wait(v, S, "stats", at.s)
                alone(v, c)
                for t in range(G):
                    last = v.bn_aggr(mv[k][:, t, :], stats[k][:, t, :])
                last.then_inc(S.sem, 1)
                wait(v, S, "agg", at.s)
                v.tensor_scalar(vare[k][:], mv[k][:, :, 1], EPS, None, ALU.add).then_inc(S.sem, 1)

            def head_1(at):
                v.wait_ge(arrived[at.b], 32 * at.half + 32)
                for k, name in enumerate(("add0", "x2")):
                    for t in range(G):
                        last = combine(v, c, y[at.b], t, k, at.s, None)
                    last.then_inc(VH.sem, 1)
                    wait(v, VH, name, at.s)
                statistics(VH, at, 0)

            def head_2(at):
                wait(v, GH, "rstd", at.s)
                wait(v, QH, "turned", at.back(1))
                normalise(xn, at, 0).then_inc(VH.sem, 1)

            def make_edges(at):
                v.wait_ge(arrived[at.b], 32 * at.half + 32)
                for q in two:
                    rows = slice(q * N, (q + 1) * N)
                    last = v.tensor_scalar(edges[at.b][rows, :, q * N:(q + 1) * N], adj_sb[at.b][rows, :, :], 0.0,
                                           None, ALU.not_equal)
                last.then_inc(VE.sem, 1)

            def tail_1(at):
                wait(v, QT1, "back", at.s)
                xs = c.x[:, bass.ds(at.s * G, G), :]
                v.tensor_tensor(xs, ps_m[:].rearrange("p (t d) -> p t d", t=G), xs, ALU.add).then_inc(VT.sem, 1)
                wait(v, VT, "x3", at.s)
                statistics(VT, at, 1)

            def tail_2(at):
                wait(v, GT, "rstd", at.s)
                if type(at.s) is not int or at.s >= 2:
                    v.wait_ge(r.queued[at.b], 16 * TOPK * G * at.half)
                normalise(r.rows[0][at.b], at, 1).then_inc(VT.sem, 1)
                for k in range(TOPK):
                    last = v.tensor_copy(r.rows[k][at.b][:, :, D:ROW].bitcast(I32),
                                         c.ids[:, k, bass.ds(at.s * G, G)].unsqueeze(2))
                last.then_inc(VT.sem, 1)

            def body(n, has_head, has_run, has_tail):
                pa = [group(n - 1, b) for b in two] if has_tail else None
                nx = [group(n + 1, b) for b in two] if has_head else None
                if has_run:
                    gates_1(n, 0, 0)
                if has_tail:
                    tail_1(pa[0])
                if has_run:
                    gates_2(n, 0, 0)
                if has_tail:
                    tail_2(pa[0])
                if has_run:
                    gates_1(n, 0, 1)
                if has_tail:
                    tail_1(pa[1])
                if has_run:
                    gates_2(n, 0, 1)
                if has_tail:
                    tail_2(pa[1])
                if has_run:
                    gates_1(n, 1, 0)
                    gates_2(n, 1, 0)
                if has_tail:
                    route_vector(v, c, r, VS, None, QT3, pa[0], E1, gb_sb[:], QT4)
                if has_run:
                    gates_1(n, 1, 1)
                    gates_2(n, 1, 1)
                if has_tail:
                    route_vector_2(v, c, r, VK, AT2, QT4, pa[0], E1, True)
                if has_head:
                    head_1(nx[0])
                    head_2(nx[0])
                if has_run:
                    gates_1(n, 2, 0)
                    gates_2(n, 2, 0)
                if has_head:
                    make_edges(nx[0])
                if has_tail:
                    route_vector(v, c, r, VS, None, QT3, pa[1], E1, gb_sb[:], QT4)
                if has_head:
                    head_1(nx[1])
                    head_2(nx[1])
                if has_run:
                    gates_1(n, 2, 1)
                    gates_2(n, 2, 1)
                if has_tail:
                    route_vector_2(v, c, r, VK, AT2, QT4, pa[1], E1, True)
                if has_head:
                    make_edges(nx[1])

            run_steps(v, body)


def tile_table(nc, c, experts_n):
    tiles = tiles_of(experts_n)
    with ExitStack() as ctx:
        def sb(name, shape, dt=F32):
            return ctx.enter_context(nc.sbuf_tensor(f"t{experts_n}_" + name, shape, dt))

        held = sb("held", [1, experts_n])
        held_i = sb("held_i", [1, experts_n], I32)
        count_i = sb("count_i", [1, experts_n], I32)
        count = sb("count", [1, experts_n])
        unit = sb("unit", [1, experts_n])
        upto = sb("upto", [1, experts_n + 1])
        base = sb("base", [1, experts_n + 1])
        passed = sb("passed", [1, tiles, experts_n])
        expert = sb("expert", [1, tiles])
        is_it = sb("is_it", [1, tiles, experts_n + 1])
        row = sb("row", [1, tiles])
        done = ctx.enter_context(nc.semaphore(f"t{experts_n}_table_step"))
        block = ctx.enter_context(nc.Block())

        @block.vector
        def _(v):
            count_of = [0]

            def link(instruction):
                count_of[0] += 1
                instruction.then_inc(done, 1)
                v.wait_ge(done, count_of[0])

            last = experts_n - 1
            region = c.region[0:1, 0:experts_n]
            v.tensor_copy(c.carry_i[0:1, 0:experts_n], c.carry[0:1, 0:experts_n])
            v.memset(unit[:], 1.0)
            v.memset(upto[0:1, 0:1], 0.0)
            link(v.scalar_tensor_tensor(out=held[:], in0=c.carry[0:1, 0:experts_n], scalar=float(P - 1),
                                        in1=region, op0=ALU.add, op1=ALU.subtract))
            link(v.tensor_copy(held_i[:], held[:]))
            link(v.tensor_scalar(count_i[:], held_i[:], P.bit_length() - 1, None, ALU.arith_shift_right))
            link(v.tensor_copy(count[:], count_i[:]))
            link(v.tensor_tensor_scan(upto[0:1, 1:experts_n + 1], unit[:], count[:], 0.0, ALU.mult, ALU.add))
            link(v.scalar_tensor_tensor(out=base[:], in0=upto[:], scalar=-float(P),
                                        in1=c.region[0:1, 0:experts_n + 1], op0=ALU.mult, op1=ALU.add))
            link(v.tensor_tensor(passed[:], upto[0:1, None, 1:experts_n + 1].to_broadcast([1, tiles, experts_n]),
                                 bc(c.iota_j[0:1, 0:tiles], experts_n), ALU.is_le))
            link(v.tensor_reduce(expert[:], passed[:], AX.X, ALU.add))
            link(v.tensor_tensor(is_it[:], c.iota_e[0:1, None, 0:experts_n + 1].to_broadcast([1, tiles, experts_n + 1]),
                                 bc(expert[:], experts_n + 1), ALU.is_equal))
            link(v.tensor_tensor(is_it[:], is_it[:], base[0:1, None, :].to_broadcast([1, tiles, experts_n + 1]),
                                 ALU.mult))
            link(v.tensor_reduce(row[:], is_it[:], AX.X, ALU.add))
            link(v.scalar_tensor_tensor(out=c.tile_row[0:1, 0:tiles], in0=c.iota_j[0:1, 0:tiles],
                                        scalar=float(P), in1=row[:], op0=ALU.mult, op1=ALU.add))
            link(v.tensor_scalar(c.tile_expert[0:1, 0:tiles], expert[:], float(last), None, ALU.min))


class Tile:

    def __init__(self, i, k):
        self.i, self.k = i + k // UNROLL if k >= 0 or type(i) is int else i - (-(k // UNROLL)), k % UNROLL
        self.j = self.i * UNROLL + self.k

    def done(self, back=0):
        return self.j + (1 - back) if back <= 1 else self.j - (back - 1)

    def first(self, n):
        return type(self.i) is int and self.j < n


def experts(nc, c, layer, queue, result, experts_n, chunks, up, down, up_b, down_b):
    tiles = tiles_of(experts_n)
    wide = 512
    with ExitStack() as ctx:
        def sb(name, shape, dt=F32):
            return ctx.enter_context(nc.sbuf_tensor(f"e{layer}_" + name, shape, dt))

        def pb(name, shape, dt=F32):
            return ctx.enter_context(nc.psum_tensor(f"e{layer}_" + name, shape, dt))

        def sem(name):
            return ctx.enter_context(nc.semaphore(f"e{layer}_" + name))

        xq = [sb(f"xq{k}", [P, ROW]) for k in range(UNROLL)]
        xT = [sb(f"xT{b}", [P, P]) for b in range(2)]
        h = [sb(f"h{b}", [P, chunks * P]) for b in range(2)]
        th = sb("th", [P, H1])
        gated = [sb(f"gated{b}", [P, H1]) for b in range(2)]
        hT = [sb(f"hT{b}", [P, chunks * P]) for b in range(2)]
        y = [sb(f"y{k}", [P, D]) for k in range(4)]
        ps_x = [pb(f"ps_x{b}", [P, 512]) for b in range(2)]
        ps_h = [pb(f"ps_h{b}", [P, wide]) for b in range(2)]
        ps_hT = [pb(f"ps_hT{b}", [P, 512]) for b in range(2)]
        ps_y = [pb(f"ps_y{b}", [P, 512]) for b in range(2)]
        padded = sem("padded")
        arrived = [sem(f"arrived{k}") for k in range(UNROLL)]
        x_turned, xT_copied, h_made, h_ready = sem("x_turned"), sem("xT_copied"), sem("h_made"), sem("h_ready")
        h_tanh, h_gated = sem("h_tanh"), sem("h_gated")
        h_turned, hT_copied, y_made, y_copied = sem("h_turned"), sem("hT_copied"), sem("y_made"), sem("y_copied")
        sent = [sem(f"sent{k}") for k in range(4)]

        def steps(eng, body):
            def step(i, k):
                lagged = [Tile(i, k - lag) for lag in range(4)]
                if type(i) is int:
                    lagged = [t if 0 <= t.j < tiles else None for t in lagged]
                body(*lagged)

            for k in range(UNROLL):
                step(0, k)
            with eng.Fori(1, tiles // UNROLL) as i:
                for k in range(UNROLL):
                    step(i, k)
            for k in range(3):
                step(tiles // UNROLL, k)

        def sent_of(t):
            return t.i * (UNROLL // 4) + (t.k // 4 + 1)

        block = ctx.enter_context(nc.Block())

        @block.sync
        def _(sp):
            sp.dma_start(queue[experts_n * REGION:experts_n * (REGION + P), :].rearrange("(u p) r -> p u r", p=P),
                         c.pad[:, experts_n:2 * experts_n, :]).then_inc(padded, 16)
            for e in range(experts_n):
                at = sp.value_load(c.carry_i[0:1, e:e + 1], min_val=e * REGION, max_val=e * REGION + TOKENS)
                sp.dma_start(queue[bass.ds(at, P), :], c.pad[:, e, :]).then_inc(padded, 16)
            sp.wait_ge(padded, 16 * (experts_n + 1))

            def load(t):
                at = sp.value_load(c.tile_row[0:1, bass.ds(t.j, 1)], min_val=0,
                                   max_val=experts_n * (REGION + P) - P)
                if not t.first(UNROLL):
                    sp.wait_ge(sent[t.k % 4], (sent_of(t) - 2) * 16)
                    alone(sp, c)
                    sp.wait_ge(x_turned, t.done(UNROLL))
                    alone(sp, c)
                sp.dma_start(xq[t.k][:], queue[bass.ds(at, P), :]).then_inc(arrived[t.k], 16)

            for k in range(UNROLL):
                load(Tile(0, k))
            with sp.Fori(1, tiles // UNROLL) as i:
                for k in range(UNROLL):
                    load(Tile(i, k))

        @block.gpsimd
        def _(pool):
            def send(t):
                if t is None:
                    return
                pool.wait_ge(y_copied, t.done())
                alone(pool, c)
                pool.indirect_dma_start(
                    out=result, out_offset=bass.IndirectOffsetOnAxis(ap=xq[t.k][:, D:ROW].bitcast(U32), axis=0),
                    in_=y[t.k % 4][:], in_offset=None).then_inc(sent[t.k % 4], 16)

            steps(pool, lambda t0, t1, t2, t3: send(t3))
            for k in range(4):
                pool.wait_ge(sent[k], 16 * tiles // 4)

        def expert_of(eng, t):
            return eng.value_load(c.tile_expert[0:1, bass.ds(t.j, 1)], min_val=0, max_val=experts_n - 1)

        @block.tensor
        def _(pe):
            def body(t0, t1, t2, t3):
                if t0:
                    pe.wait_ge(arrived[t0.k], 16 * (t0.i + 1))
                    if not t0.first(2):
                        pe.wait_ge(xT_copied, t0.done(2))
                    pe.transpose(ps_x[t0.k % 2][:, 0:P], xq[t0.k][:, 0:D], c.ident[:]).then_inc(x_turned, 1)
                if t1:
                    e = expert_of(pe, t1)
                    pe.wait_ge(xT_copied, t1.done())
                    if not t1.first(2):
                        pe.wait_ge(h_ready, t1.done(2))
                    pe.matmul(ps_h[t1.k % 2][:], xT[t1.k % 2][:], up[:, bass.ds(e * wide, wide)],
                              start=True, stop=True).then_inc(h_made, 1)
                if t2:
                    pe.wait_ge(h_ready, t2.done())
                    if not t2.first(2):
                        pe.wait_ge(hT_copied, t2.done(2))
                    for q in range(chunks):
                        last = pe.transpose(ps_hT[t2.k % 2][:, q * P:(q + 1) * P],
                                            h[t2.k % 2][:, q * P:(q + 1) * P], c.ident[:])
                    last.then_inc(h_turned, 1)
                if t3:
                    e = expert_of(pe, t3)
                    pe.wait_ge(hT_copied, t3.done())
                    if not t3.first(2):
                        pe.wait_ge(y_copied, t3.done(2))
                    for q in range(chunks):
                        last = pe.matmul(ps_y[t3.k % 2][:, 0:D], hT[t3.k % 2][:, q * P:(q + 1) * P],
                                         down[:, bass.ds(e * (chunks * P) + q * P, P)],
                                         start=(q == 0), stop=(q == chunks - 1))
                    last.then_inc(y_made, 1)

            steps(pe, body)

        @block.scalar
        def _(act):
            def body(t0, t1, t2, t3):
                if t0:
                    act.wait_ge(x_turned, t0.done())
                    if not t0.first(2):
                        act.wait_ge(h_made, t0.done(2))
                    act.activation(xT[t0.k % 2][:], ps_x[t0.k % 2][:, 0:P], ACT.Copy).then_inc(xT_copied, 1)
                if t1 and layer == 1:
                    act.wait_ge(h_made, t1.done())
                    if not t1.first(1):
                        act.wait_ge(h_gated, t1.done(1))
                    act.activation(th[:], ps_h[t1.k % 2][:, 0:H1], ACT.Tanh, scale=0.5).then_inc(h_tanh, 1)
                if t2:
                    act.wait_ge(h_turned, t2.done())
                    if not t2.first(2):
                        act.wait_ge(y_made, t2.done(2))
                    act.activation(hT[t2.k % 2][:], ps_hT[t2.k % 2][:, 0:chunks * P],
                                   ACT.Relu if layer == 0 else ACT.Copy).then_inc(hT_copied, 1)

            steps(act, body)

        @block.vector
        def _(v):
            def body(t0, t1, t2, t3):
                if t1 and layer == 0:
                    e = expert_of(v, t1)
                    v.wait_ge(h_made, t1.done())
                    if not t1.first(2):
                        v.wait_ge(h_turned, t1.done(2))
                    v.tensor_tensor(h[t1.k % 2][:], ps_h[t1.k % 2][:], up_b[:, bass.ds(e * wide, wide)],
                                    ALU.add).then_inc(h_ready, 1)
                if t1 and layer == 1:
                    v.wait_ge(h_tanh, t1.done())
                    v.scalar_tensor_tensor(out=gated[t1.k % 2][:], in0=th[:], scalar=1.0, in1=ps_h[t1.k % 2][:, 0:H1],
                                           op0=ALU.add, op1=ALU.mult).then_inc(h_gated, 1)
                    v.wait_ge(h_gated, t1.done())
                    if not t1.first(2):
                        v.wait_ge(h_turned, t1.done(2))
                    v.scalar_tensor_tensor(out=h[t1.k % 2][:], in0=gated[t1.k % 2][:], scalar=0.5,
                                           in1=ps_h[t1.k % 2][:, H1:2 * H1], op0=ALU.mult,
                                           op1=ALU.mult).then_inc(h_ready, 1)
                if t3:
                    if layer == 0:
                        e = expert_of(v, t3)
                    v.wait_ge(y_made, t3.done())
                    if not t3.first(4):
                        v.wait_ge(sent[t3.k % 4], (sent_of(t3) - 1) * 16)
                    if layer == 0:
                        v.tensor_tensor(y[t3.k % 4][:], ps_y[t3.k % 2][:, 0:D], down_b[:, bass.ds(e * D, D)],
                                        ALU.add).then_inc(y_copied, 1)
                    else:
                        v.tensor_copy(y[t3.k % 4][:], ps_y[t3.k % 2][:, 0:D]).then_inc(y_copied, 1)

            steps(v, body)


def combine(v, c, y, t, k, g, src):
    tile = g * G + t
    return v.scalar_tensor_tensor(out=c.x[:, tile, :], in0=y[:, t, k, :],
                                  scalar=c.prob[:, k, bass.ds(tile, 1)], in1=c.x[:, tile, :],
                                  op0=ALU.mult, op1=ALU.add)


def results_of(result, s):
    return result[bass.ds(s * (TOPK * GN), TOPK * GN), :].rearrange("(t p k) d -> p t k d", p=P, k=TOPK)


def combine_out(nc, c, out):
    with ExitStack() as ctx:
        def sem(name):
            return ctx.enter_context(nc.semaphore("o_" + name))

        y = [ctx.enter_context(nc.sbuf_tensor(f"o_y{b}", [P, G, TOPK, D], F32)) for b in range(4)]
        arrived = [sem(f"arrived{b}") for b in range(4)]
        first_added, added = sem("first_added"), sem("added")
        stored = sem("stored")
        block = ctx.enter_context(nc.Block())

        @block.sync
        def _(sp):
            for s in range(4):
                sp.dma_start(y[s][:], results_of(c.result1, s)).then_inc(arrived[s], 16)
            with sp.Fori(1, NG // 4) as i:
                for b in range(4):
                    sp.wait_ge(added, i * 4 + (b - 3))
                    alone(sp, c)
                    sp.dma_start(y[b][:], results_of(c.result1, i * 4 + b)).then_inc(arrived[b], 16)

        @block.vector
        def _(v):
            with v.Fori(0, NG // 4) as i:
                for b in range(4):
                    s = i * 4 + b
                    v.wait_ge(arrived[b], (i + 1) * 16)
                    for t in range(G):
                        last = combine(v, c, y[b], t, 0, s, None)
                    last.then_inc(first_added, 1)
                    v.wait_ge(first_added, s + 1)
                    for t in range(G):
                        last = combine(v, c, y[b], t, 1, s, None)
                    last.then_inc(added, 1)

        @block.scalar
        def _(act):
            with act.Fori(0, NG) as s:
                act.wait_ge(added, s + 1)
                act.dma_start(out[bass.ds(s * GN, GN), :].rearrange("(t p) d -> p t d", p=P),
                              c.x[:, bass.ds(s * G, G), :]).then_inc(stored, 16)
            act.wait_ge(stored, 16 * NG)


def lay_out(x, adj, L0_gnn_W, L0_gnn_a, L0_ffn_Wg, L0_ffn_bg, L0_ffn_W1, L0_ffn_b1, L0_ffn_W2, L0_ffn_b2,
            L1_gnn_weight, L1_gnn_w_ih, L1_gnn_w_hh, L1_gnn_b_ih, L1_gnn_b_hh, L1_ffn_gate_w, L1_ffn_gate_b,
            L1_ffn_w1, L1_ffn_w2, L1_ffn_w3):
    import numpy as np
    a = {
        "x": x.reshape(TOKENS, D),
        "adj": adj.reshape(TOKENS, N),
        "gat_w": L0_gnn_W,
        "gat_wT": L0_gnn_W.T,
        "gat_a2": L0_gnn_a.reshape(2, D).T,
        "gate0_w": L0_ffn_Wg.T,
        "gate0_b": L0_ffn_bg,
        "w1": L0_ffn_W1.transpose(2, 0, 1).reshape(D, E0 * H0),
        "b1": L0_ffn_b1.reshape(E0 * H0),
        "w2": L0_ffn_W2.reshape(E0, D, H0 // P, P).transpose(3, 0, 2, 1).reshape(P, E0 * H0),
        "b2": L0_ffn_b2.reshape(E0 * D),
        "gnn_wT": L1_gnn_weight.transpose(2, 0, 1).reshape(D, 3 * D),
        "w_ihT": L1_gnn_w_ih.T,
        "w_hhT": L1_gnn_w_hh.T,
        "b_ih": L1_gnn_b_ih.reshape(3, D).T,
        "b_hh": L1_gnn_b_hh.reshape(3, D).T,
        "gate1_w": L1_ffn_gate_w,
        "gate1_b": L1_ffn_gate_b,
        "w12": np.stack([L1_ffn_w1, L1_ffn_w2], axis=2).transpose(1, 0, 2, 3).reshape(D, E1 * 2 * H1),
        "w3": L1_ffn_w3.reshape(E1, H1 // P, P, D).transpose(2, 0, 1, 3).reshape(P, E1 * H1),
    }
    return {k: np.ascontiguousarray(v) for k, v in a.items()}


def kernel(**inputs):
    import numpy as np
    import concourse.bacc as bacc
    from concourse.bass_utils import run_bass_kernel_spmd

    arrays = lay_out(**{k: np.asarray(v) for k, v in inputs.items()})
    nc = bacc.Bacc("TRN2", target_bir_lowering=False, num_devices=1)
    args = [nc.dram_tensor(k, a.shape, mybir.dt.from_np(a.dtype), kind="ExternalInput").ap()
            for k, a in arrays.items()]
    args.append(nc.dram_tensor("out", (TOKENS, D), F32, kind="ExternalOutput").ap())
    program(nc, *args)
    r = run_bass_kernel_spmd(nc, [arrays], core_ids=[0])
    return r.results[0]["out"].reshape(GRAPHS, N, D)
```

```python
import concourse.bass as bass
from concourse import mybir
from contextlib import ExitStack

F32 = mybir.dt.float32
BF16 = mybir.dt.bfloat16
I32 = mybir.dt.int32
U32 = mybir.dt.uint32
ALU = mybir.AluOpType
ACT = mybir.ActivationFunctionType
AX = mybir.AxisListType

P = 128
GRAPHS, N, D = 128, 64, 128
TOKENS = GRAPHS * N
NT = TOKENS // P
G = 4
NG = NT // G
GN = G * P
UNROLL = 8
PACK, BITS = 4, 4
NEG = -9.0e15
EPS = 1e-5
E0, H0 = 8, 512
E1, H1 = 16, 256
TOPK = 2
REGION = TOKENS + P
ROW = D + 1


class Steps:

    def __init__(self, sem, names):
        self.sem, self.names = sem, names.split()

    def upto(self, name, s):
        return s * len(self.names) + (self.names.index(name) + 1)


def wait(eng, steps, name, s):
    if type(s) is int and s < 0:
        return
    eng.wait_ge(steps.sem, steps.upto(name, s))


def alone(eng, c):
    eng.nop(nofuse=True)


def behind(at, n):
    return type(at.s) is not int or at.s >= n


class At:

    def __init__(self, i, j):
        self.i, self.j = i, j
        self.s = 2 * i + j if type(i) is int else (i * 2 + j if j >= 0 else i * 2 - (-j))
        self.b = j % 2
        k = j // 2
        self.half = i + k if type(i) is int or k >= 0 else i - (-k)

    def back(self, n):
        return self.s - n


def prev(at):
    return At(at.i, at.j - 1)


def tiles_of(experts):
    most = (TOKENS * TOPK - experts) // P + experts
    return -(-most // UNROLL) * UNROLL


def program(nc, x, adj, gat_w, gat_wT, gat_a2, gate0_w, gate0_b, w1, b1, w2, b2,
            gnn_wT, w_ihT, w_hhT, b_ih, b_hh, gate1_w, gate1_b, w12, w3, out):
    with ExitStack() as ctx:
        def sb(name, shape, dt=F32):
            return ctx.enter_context(nc.sbuf_tensor(name, shape, dt))

        c = Shared()
        c.queue0 = nc.dram_tensor("queue0", (E0 * (REGION + P), ROW), F32, kind="Internal").ap()
        c.queue1 = nc.dram_tensor("queue1", (E1 * (REGION + P), ROW), F32, kind="Internal").ap()
        c.result0 = nc.dram_tensor("result0", (TOPK * TOKENS + 2 * E0 * P, D), F32, kind="Internal").ap()
        c.result1 = nc.dram_tensor("result1", (TOPK * TOKENS + 2 * E1 * P, D), F32, kind="Internal").ap()
        c.x = sb("x_res", [P, NT, D])
        c.ident = sb("ident", [P, P])
        c.before = sb("before", [P, P], BF16)
        c.ones = sb("ones", [P, P], BF16)
        c.iota_e = sb("iota_e", [P, E1 + 1])
        c.region = sb("region", [P, E1 + 1])
        c.carry = sb("carry", [P, E1])
        c.ids = sb("ids", [P, TOPK, NT], I32)
        c.prob = sb("prob", [P, TOPK, NT])
        c.half_neg = sb("half_neg", [P, G])
        c.pad = sb("pad", [P, 2 * E1, ROW])
        c.iota_j = sb("iota_j", [1, tiles_of(E1)])
        c.digit = sb("digit", [1, PACK])
        c.tile_row = sb("tile_row", [1, tiles_of(E1)], I32)
        c.tile_experts = sb("tile_experts", [1, tiles_of(E1) // PACK], I32)
        c.carry_i = sb("carry_i", [1, E1], I32)
        c.filled = ctx.enter_context(nc.semaphore("filled"))
        c.constants_made = ctx.enter_context(nc.semaphore("constants_made"))
        with ExitStack() as stage:
            up = stage.enter_context(nc.sbuf_tensor("w1_sb", [D, E0 * H0], F32))
            down = stage.enter_context(nc.sbuf_tensor("w2_sb", [P, E0 * H0], F32))
            up_b = stage.enter_context(nc.sbuf_tensor("b1_sb", [P, E0 * H0], F32))
            down_b = stage.enter_context(nc.sbuf_tensor("b2_sb", [P, E0 * D], F32))
            weights = ((up, w1), (down, w2), (up_b, b1.partition_broadcast(P)),
                       (down_b, b2.partition_broadcast(P)))
            gat_and_routing(nc, c, x, adj, gat_w, gat_wT, gat_a2, gate0_w, gate0_b, weights)
            tile_table(nc, c, E0)
            experts(nc, c, 0, c.queue0, c.result0, E0, H0 // P, up, down, up_b, down_b)
        with ExitStack() as stage:
            up = stage.enter_context(nc.sbuf_tensor("w12_sb", [D, E1 * 2 * H1], F32))
            down = stage.enter_context(nc.sbuf_tensor("w3_sb", [P, E1 * H1], F32))
            gru_and_routing(nc, c, adj, gnn_wT, w_ihT, w_hhT, b_ih, b_hh, gate1_w, gate1_b,
                            ((up, w12), (down, w3)))
            tile_table(nc, c, E1)
            experts(nc, c, 1, c.queue1, c.result1, E1, H1 // P, up, down, None, None)
        combine_out(nc, c, out)


class Shared:
    pass


def make_constants(pool, c):
    pool.memset(c.ident[:], 0.0).then_inc(c.filled, 1)
    pool.memset(c.before[:], 1.0).then_inc(c.filled, 1)
    pool.memset(c.ones[:], 1.0)
    pool.memset(c.half_neg[:], -0.5)
    for q in range(PACK):
        pool.memset(c.digit[0:1, q:q + 1], float(1 << (BITS * q)))
    pool.iota(c.iota_e[:], pattern=[[1, E1 + 1]], base=0, channel_multiplier=0,
              allow_small_or_imprecise_dtypes=True)
    pool.iota(c.region[:], pattern=[[REGION, E1 + 1]], base=0, channel_multiplier=0,
              allow_small_or_imprecise_dtypes=True)
    pool.iota(c.iota_j[:], pattern=[[1, tiles_of(E1)]], base=0, channel_multiplier=0,
              allow_small_or_imprecise_dtypes=True)
    for k in range(TOPK):
        pool.iota(c.ids[:, k, :], pattern=[[TOPK * P, NT]], base=k, channel_multiplier=TOPK)
    pool.wait_ge(c.filled, 2)
    pool.affine_select(out=c.ident[:], in_=c.ident[:], compare_op=ALU.not_equal, fill=1.0,
                       base=0, pattern=[[-1, P]], channel_multiplier=1)
    pool.affine_select(out=c.before[:], in_=c.before[:], compare_op=ALU.is_gt, fill=0.0,
                       base=0, pattern=[[1, P]], channel_multiplier=-1).then_inc(c.constants_made, 1)
    pool.memset(c.pad[:, :, 0:D], 0.0)
    pool.iota(c.pad[:, :, D:ROW].bitcast(I32), pattern=[[P, 2 * E1], [1, 1]],
              base=TOPK * TOKENS, channel_multiplier=1)


def bc(ap, n):
    return ap.unsqueeze(len(ap.shape)).to_broadcast([*ap.shape, n])


def norm_buffers(sb, name):
    m = Shared()
    m.stats = sb(name + "_stats", [P, G, 6])
    m.mv = sb(name + "_mv", [P, G, 2])
    m.vare = sb(name + "_vare", [P, G])
    m.minus_mean = sb(name + "_minus_mean", [P, G])
    m.rstd = sb(name + "_rstd", [P, G])
    m.shift = sb(name + "_shift", [P, G])
    return m


def statistics(v, c, m, V, Gs, at):
    statistics_1(v, c, m, V, at)
    statistics_2(v, c, m, V, at)
    statistics_3(v, c, m, V, Gs, at)


def statistics_1(v, c, m, V, at):
    alone(v, c)
    for t in range(G):
        last = v.bn_stats(m.stats[:, t, :], c.x[:, at.s * G + t, :])
    last.then_inc(V.sem, 1)


def statistics_2(v, c, m, V, at):
    wait(v, V, "stats", at.s)
    alone(v, c)
    for t in range(G):
        last = v.bn_aggr(m.mv[:, t, :], m.stats[:, t, :])
    last.then_inc(V.sem, 1)


def statistics_3(v, c, m, V, Gs, at):
    wait(v, V, "agg", at.s)
    wait(v, Gs, "shift", at.back(1))
    v.tensor_scalar(m.minus_mean[:], m.mv[:, :, 0], -1.0, None, ALU.mult)
    v.tensor_scalar(m.vare[:], m.mv[:, :, 1], EPS, None, ALU.add).then_inc(V.sem, 1)


def rstd_and_shift(pool, c, m, V, Gs, A, at):
    wait(pool, V, "vare", at.s)
    wait(pool, A, "normed", at.back(1))
    pool.tensor_tensor(m.rstd[:], m.vare[:], c.half_neg[:], ALU.pow).then_inc(Gs.sem, 1)
    wait(pool, Gs, "rstd", at.s)
    pool.tensor_tensor(m.shift[:], m.minus_mean[:], m.rstd[:], ALU.mult).then_inc(Gs.sem, 1)


def normalise(act, c, m, Gs, A, dst, at):
    wait(act, Gs, "shift", at.s)
    for t in range(G):
        last = act.activation(dst[:, t, 0:D], c.x[:, at.s * G + t, :], ACT.Identity,
                              bias=m.shift[:, t:t + 1], scale=m.rstd[:, t:t + 1])
    last.then_inc(A.sem, 1)


def route_vector(v, c, r, V, Q, at, experts_n, gate_b, QR):
    route_scores(v, r, V, Q, at, experts_n, gate_b)
    route_best(v, c, r, V, at, experts_n)
    route_hot(v, c, r, V, QR, at, experts_n)


def route_scores(v, r, V, Q, at, experts_n, gate_b):
    s = at.s
    wait(v, Q, "scored", s)
    v.tensor_tensor(r.score[:, :, 0:experts_n], r.ps_score[:, 0:G * experts_n].rearrange("p (t e) -> p t e", t=G),
                    gate_b[:, None, :].to_broadcast([P, G, experts_n]), ALU.add).then_inc(V.sem, 1)


def route_best(v, c, r, V, at, experts_n):
    s, b = at.s, at.b
    wait(v, V, "scores", s)
    alone(v, c)
    for t in range(G):
        last = v.max(r.top[b][:, t, :], r.score[:, t, 0:experts_n])
    last.then_inc(V.sem, 1)
    wait(v, V, "top", s)
    alone(v, c)
    for t in range(G):
        last = v.max_index(r.where[:, t, :], r.top[b][:, t, :], r.score[:, t, 0:experts_n])
    last.then_inc(V.sem, 1)


def route_hot(v, c, r, V, QR, at, experts_n):
    s, b = at.s, at.b
    wait(v, V, "where", s)
    v.tensor_copy(r.wheref[:], r.where[:, :, 0:TOPK]).then_inc(V.sem, 1)
    wait(v, V, "wheref", s)
    iota = c.iota_e[:, None, 0:experts_n].to_broadcast([P, G, experts_n])
    for k in range(TOPK):
        v.tensor_tensor(r.hot[k][b][:], iota, bc(r.wheref[:, :, k], experts_n), ALU.is_equal).then_inc(V.sem, 1)
    wait(v, V, "hot1", s)
    wait(v, QR, "ranked", at.back(2))
    v.tensor_tensor(r.both[b][:], r.hot[0][b][:], r.hot[1][b][:], ALU.add).then_inc(V.sem, 1)


def route_vector_2(v, c, r, V, A, Q, at, experts_n):
    route_ranks(v, c, r, V, Q, at, experts_n)
    route_slots(v, r, V, A, at)


def route_ranks(v, c, r, V, Q, at, experts_n):
    s, b = at.s, at.b
    carry = c.carry[:, 0:experts_n]
    wait(v, Q, "ranked", s)
    wait(v, V, "carried", at.back(1))
    v.tensor_tensor(r.rank[:], r.ps_rank[:, 0:G * experts_n].rearrange("p (t e) -> p t e", t=G),
                    carry[:, None, :].to_broadcast([P, G, experts_n]), ALU.add).then_inc(V.sem, 1)
    wait(v, V, "ranked", s)
    v.tensor_tensor(carry, r.ps_rank[:, G * experts_n:(G + 1) * experts_n], carry, ALU.add).then_inc(V.sem, 1)
    for k in range(TOPK):
        v.tensor_tensor(r.pick[k][:], r.hot[k][b][:], r.rank[:], ALU.mult).then_inc(r.picked, 1)


def route_slots(v, r, V, A, at):
    s, b = at.s, at.b
    for k in range(TOPK):
        v.wait_ge(r.picked, s * TOPK + (k + 1))
        v.tensor_reduce(r.slotf[:, k, :], r.pick[k][:], AX.X, ALU.add).then_inc(V.sem, 1)
    wait(v, V, "slot1", s)
    v.tensor_copy(r.slots[b][:], r.slotf[:]).then_inc(V.sem, 1)
    if A:
        wait(v, A, "p1", at.back(1))
    v.tensor_tensor(r.gap[:], r.top[b][:, :, 1], r.top[b][:, :, 0], ALU.subtract).then_inc(V.sem, 1)


def route_vector_3(v, c, r, V, A, at):
    s = at.s
    wait(v, A, "gap_exp", s)
    v.tensor_scalar(r.den[:], r.egap[:], 1.0, None, ALU.add).then_inc(V.sem, 1)
    wait(v, V, "den", s)
    v.reciprocal(c.prob[:, 0, bass.ds(s * G, G)], r.den[:]).then_inc(V.sem, 1)
    wait(v, V, "p0", s)
    v.tensor_tensor(c.prob[:, 1, bass.ds(s * G, G)], r.egap[:], c.prob[:, 0, bass.ds(s * G, G)],
                    ALU.mult).then_inc(V.sem, 1)


def route_tensor(pe, c, r, V, VR, Q, at, experts_n):
    wait(pe, V, "both", at.s)
    wait(pe, VR, "carried", at.back(1))
    for t in range(G + 1):
        cols = r.ps_rank[:, t * experts_n:(t + 1) * experts_n]
        for u in range(min(t, G - 1) + 1):
            last = pe.matmul(cols, c.before[:] if u == t else c.ones[:], r.both[at.b][:, u, :],
                             start=(u == 0), stop=(u == min(t, G - 1)))
    last.then_inc(Q.sem, 1)


def route_buffers(sb, pb, sem, prefix, experts_n):
    r = Shared()
    r.score = sb(prefix + "score", [P, G, experts_n])
    r.top = [sb(prefix + f"top{b}", [P, G, 8]) for b in range(2)]
    r.where = sb(prefix + "where", [P, G, 8], U32)
    r.wheref = sb(prefix + "wheref", [P, G, TOPK])
    r.hot = [[sb(prefix + f"hot{k}_{b}", [P, G, experts_n]) for b in range(2)] for k in range(TOPK)]
    r.both = [sb(prefix + f"both{b}", [P, G, experts_n], BF16) for b in range(2)]
    r.rank = sb(prefix + "rank", [P, G, experts_n])
    r.pick = [sb(prefix + f"pick{k}", [P, G, experts_n]) for k in range(TOPK)]
    r.slotf = sb(prefix + "slotf", [P, TOPK, G])
    r.slots = [sb(prefix + f"slots{b}", [P, TOPK, G], U32) for b in range(2)]
    r.gap = sb(prefix + "gap", [P, G])
    r.egap = sb(prefix + "egap", [P, G])
    r.den = sb(prefix + "den", [P, G])
    r.rows = [[sb(prefix + f"rows{k}_{b}", [P, G, ROW]) for b in range(2)] for k in range(TOPK)]
    r.picked = sem(prefix + "picked")
    r.queued = [sem(prefix + f"queued{b}") for b in range(2)]
    return r


def queue_rows(pool, c, r, V, A, queue, at, first=0, last=TOPK * G):
    wait(pool, V, "slots", at.s)
    wait(pool, A, "rows_copied", at.s)
    alone(pool, c)
    for k, t in [divmod(m, G) for m in range(first, last)]:
        pool.indirect_dma_start(
            out=queue, out_offset=bass.IndirectOffsetOnAxis(ap=r.slots[at.b][:, k, t:t + 1], axis=0),
            in_=r.rows[k][at.b][:, t, :], in_offset=None).then_inc(r.queued[at.b], 16)


def five_deep(eng, body):

    def step(i, j):
        groups = [At(i, j - lag) for lag in range(5)]
        if type(i) is int:
            groups = [g if 0 <= g.s < NG else None for g in groups]
        body(*groups)

    for n in range(6):
        step(n // 2, n % 2)
    with eng.Fori(3, NG // 2) as i:
        step(i, 0)
        step(i, 1)
    for n in range(4):
        step(NG // 2, n)


def load_share(sp, weights, s, loaded):
    for dst, src in weights:
        share = dst.shape[1] // NG
        sp.dma_start(dst[:, bass.ds(s * share, share)], src[:, bass.ds(s * share, share)]).then_inc(loaded, 16)


def gat_and_routing(nc, c, x, adj, gat_w, gat_wT, gat_a2, gate_w, gate_b, weights):
    with ExitStack() as ctx:
        def sb(name, shape, dt=F32):
            return ctx.enter_context(nc.sbuf_tensor("a_" + name, shape, dt))

        def pb(name, shape, dt=F32):
            return ctx.enter_context(nc.psum_tensor("a_" + name, shape, dt))

        def sem(name):
            return ctx.enter_context(nc.semaphore("a_" + name))

        w_sb = sb("w", [D, D + 1])
        wT_sb = sb("wT", [D, D])
        a2_sb = sb("a2", [D, 2])
        wa2_wide = sb("wa2_wide", [D, N])
        gw_sb = sb("gw", [D, E0])
        gb_sb = sb("gb", [P, E0])
        adj_sb = [sb(f"adj{b}", [P, G, N], I32) for b in range(2)]
        neg = sb("neg", [P, G, N])
        norm1, norm2 = norm_buffers(sb, "norm1"), norm_buffers(sb, "norm2")
        xn = sb("xn", [P, G, D])
        xnT = sb("xnT", [P, GN])
        h = sb("h", [P, G, D + 1])
        e = sb("e", [P, G, N])
        rowmax = sb("rowmax", [P, G])
        pbd = sb("pbd", [P, G, P])
        rowsum = sb("rowsum", [P, G])
        rinv = sb("rinv", [P, G])
        pT = sb("pT", [P, GN])
        z = sb("z", [P, G, D])
        zmin = sb("zmin", [P, G, D])
        zexp = sb("zexp", [P, G, D])
        xz = sb("xz", [P, G, D])
        rT = sb("rT", [P, GN])
        r = route_buffers(sb, pb, sem, "r_", E0)

        ps_t = pb("ps_t", [P, GN])
        ps_h = pb("ps_h", [P, 2, GN])
        ps_s = pb("ps_s", [P, G * N])
        ps_p = pb("ps_p", [P, GN])
        ps_o = pb("ps_o", [P, GN])
        ps_r = pb("ps_r", [P, GN])
        ps_q = pb("ps_q", [P, GN])
        r.ps_score = ps_q[:, 0:G * E0]
        r.ps_rank = ps_q[:, G * E0:G * E0 + (G + 1) * E0]

        loaded, next_loaded = sem("weights_loaded"), sem("next_weights_loaded")
        arrived = [sem(f"arrived{b}") for b in range(2)]
        ready = sem("weights_ready")
        VN1, VN2 = (Steps(sem(f"v_norm{k}"), "stats agg vare") for k in (1, 2))
        GN1, GN2 = (Steps(sem(f"g_norm{k}"), "rstd shift") for k in (1, 2))
        AN1, AN2 = (Steps(sem(f"a_norm{k}"), "normed") for k in (1, 2))
        VM = Steps(sem("v_mask"), "neg")
        VA = Steps(sem("v_attend"), "e lrelu masked max centred sum rinv")
        VU = Steps(sem("v_update"), "z zmin xz x1")
        VS = Steps(sem("v_scores"), "ids scores top where wheref hot0 hot1 both")
        VK = Steps(sem("v_ranks"), "ranked carried slot0 slot1 slots gap")
        VP = Steps(sem("v_weights"), "den p0 p1")
        AX1, AH1 = Steps(sem("a_turned"), "xnT"), Steps(sem("a_h"), "h")
        AA, AZ = Steps(sem("a_attend"), "exp pT"), Steps(sem("a_update"), "zexp")
        AR1, AR2 = Steps(sem("a_rows"), "rT rows_copied"), Steps(sem("a_weights"), "gap_exp")
        QX, QA = Steps(sem("q_project"), "turned hs"), Steps(sem("q_attend"), "probs_turned mixed")
        QR1, QR2 = Steps(sem("q_route"), "turned scored"), Steps(sem("q_ranks"), "ranked")

        block = ctx.enter_context(nc.Block())

        @block.sync
        def _(sp):
            for dst, src in ((w_sb[:, 0:D], gat_w), (wT_sb[:], gat_wT), (a2_sb[:], gat_a2), (gw_sb[:], gate_w),
                             (gb_sb[:], gate_b.partition_broadcast(P))):
                sp.dma_start(dst, src).then_inc(loaded, 16)

            def load(at, first):
                if not first:
                    sp.wait_ge(arrived[at.b], 32 * at.half)
                    alone(sp, c)
                    wait(sp, VM, "neg", at.back(2))
                    alone(sp, c)
                rows = x[bass.ds(at.s * GN, GN), :]
                sp.dma_start(c.x[:, bass.ds(at.s * G, G), :],
                             rows.rearrange("(t p) d -> p t d", p=P)).then_inc(arrived[at.b], 16)
                sp.dma_start(adj_sb[at.b][:], adj[bass.ds(at.s * GN, GN), :]
                             .rearrange("(t p) d -> p t d", p=P)).then_inc(arrived[at.b], 16)
                if behind(at, 2):
                    load_share(sp, weights, at.back(2), next_loaded)

            load(At(0, 0), True)
            load(At(0, 1), True)
            with sp.Fori(1, NG // 2) as i:
                load(At(i, 0), False)
                load(At(i, 1), False)
            for s in (NG - 2, NG - 1):
                load_share(sp, weights, s, next_loaded)
            sp.wait_ge(loaded, 16 * 5)
            sp.wait_ge(next_loaded, 16 * NG * len(weights))
            for b in range(2):
                sp.wait_ge(r.queued[b], 16 * TOPK * G * (NG // 2))

        @block.gpsimd
        def _(pool):
            make_constants(pool, c)

            def body(g0, g1, g2, g3, g4):
                if g4:
                    queue_rows(pool, c, r, VK, AR1, c.queue0, g4, 0, 3)
                if g0:
                    rstd_and_shift(pool, c, norm1, VN1, GN1, AN1, g0)
                if g4:
                    queue_rows(pool, c, r, VK, AR1, c.queue0, g4, 3, 5)
                if g2:
                    rstd_and_shift(pool, c, norm2, VN2, GN2, AN2, g2)
                if g4:
                    queue_rows(pool, c, r, VK, AR1, c.queue0, g4, 5, 8)

            five_deep(pool, body)

        @block.vector
        def _(v):
            v.wait_ge(c.constants_made, 1)
            v.tensor_copy(c.carry[:], c.region[:, 0:E1])
            v.memset(pbd[:], 0.0)
            v.wait_ge(ready, 1)
            v.tensor_copy(w_sb[:, D:D + 1], ps_t[:, 0:1])
            v.tensor_copy(wa2_wide[:], ps_t[:, 1:2].to_broadcast([D, N])).then_inc(ready, 1)

            def body(g0, g1, g2, g3, g4):
                if g2:
                    xs = c.x[:, bass.ds(g2.s * G, G), :]
                    wait(v, QA, "mixed", g2.s)
                    wait(v, VA, "rinv", g2.s)
                    v.tensor_tensor(z[:], ps_o[:].rearrange("p (t d) -> p t d", t=G), bc(rinv[:], D),
                                    ALU.mult).then_inc(VU.sem, 1)
                if g0:
                    v.wait_ge(arrived[g0.b], 32 * g0.half + 32)
                    statistics_1(v, c, norm1, VN1, g0)
                if g2:
                    wait(v, VU, "z", g2.s)
                    v.tensor_scalar(zmin[:], z[:], 0.0, None, ALU.min).then_inc(VU.sem, 1)
                if g0:
                    statistics_2(v, c, norm1, VN1, g0)
                if g2:
                    v.scalar_tensor_tensor(out=xz[:], in0=z[:], scalar=0.0, in1=xs,
                                           op0=ALU.max, op1=ALU.add).then_inc(VU.sem, 1)
                if g0:
                    statistics_3(v, c, norm1, VN1, GN1, g0)
                if g2:
                    wait(v, VU, "xz", g2.s)
                    wait(v, AZ, "zexp", g2.s)
                    v.scalar_tensor_tensor(out=xs, in0=zexp[:], scalar=-1.0, in1=xz[:],
                                           op0=ALU.add, op1=ALU.add).then_inc(VU.sem, 1)
                if g1:
                    wait(v, AH1, "h", g1.s)
                    wait(v, AA, "exp", g1.back(1))
                    v.tensor_tensor(e[:], ps_s[:].rearrange("p (t n) -> p t n", t=G), bc(h[:, :, D], N),
                                    ALU.add).then_inc(VA.sem, 1)
                if g2:
                    wait(v, VU, "x1", g2.s)
                    statistics_1(v, c, norm2, VN2, g2)
                if g1:
                    wait(v, VA, "e", g1.s)
                    v.scalar_tensor_tensor(out=e[:], in0=e[:], scalar=0.2, in1=e[:], op0=ALU.mult,
                                           op1=ALU.max).then_inc(VA.sem, 1)
                if g2:
                    statistics_2(v, c, norm2, VN2, g2)
                if g1:
                    wait(v, VA, "lrelu", g1.s)
                    wait(v, VM, "neg", g1.s)
                    v.tensor_tensor(e[:], e[:], neg[:], ALU.add).then_inc(VA.sem, 1)
                if g2:
                    statistics_3(v, c, norm2, VN2, GN2, g2)
                if g1:
                    wait(v, VA, "masked", g1.s)
                    v.tensor_reduce(rowmax[:], e[:], AX.X, ALU.max).then_inc(VA.sem, 1)
                if g0:
                    v.tensor_scalar(neg[:], adj_sb[g0.b][:], 0.0, NEG, ALU.is_le, ALU.mult).then_inc(VM.sem, 1)
                if g1:
                    wait(v, VA, "max", g1.s)
                    v.tensor_tensor(e[:], e[:], bc(rowmax[:], N), ALU.subtract).then_inc(VA.sem, 1)
                if g3:
                    if behind(g3, 2):
                        v.wait_ge(r.queued[g3.b], 16 * TOPK * G * g3.half)
                    for k in range(TOPK):
                        last = v.tensor_copy(r.rows[k][g3.b][:, :, D:ROW].bitcast(I32),
                                             c.ids[:, k, bass.ds(g3.s * G, G)].unsqueeze(2))
                    last.then_inc(VS.sem, 1)
                    route_scores(v, r, VS, QR1, g3, E0, gb_sb[:])
                    route_best(v, c, r, VS, g3, E0)
                    route_hot(v, c, r, VS, QR2, g3, E0)
                if g1:
                    wait(v, AA, "exp", g1.s)
                    v.tensor_reduce(rowsum[:], pbd[:], AX.X, ALU.add).then_inc(VA.sem, 1)
                    wait(v, VA, "sum", g1.s)
                    v.reciprocal(rinv[:], rowsum[:]).then_inc(VA.sem, 1)
                if g4:
                    route_vector_3(v, c, r, VP, AR2, g4)
                if g3:
                    route_ranks(v, c, r, VK, QR2, g3, E0)
                    route_slots(v, r, VK, None, g3)

            five_deep(v, body)

        @block.scalar
        def _(act):
            act.wait_ge(ready, 2)

            def body(g0, g1, g2, g3, g4):
                if g3:
                    if behind(g3, 2):
                        act.wait_ge(r.queued[g3.b], 16 * TOPK * G * g3.half)
                    normalise(act, c, norm2, GN2, AN2, r.rows[0][g3.b], g3)
                if g2:
                    wait(act, VU, "zmin", g2.s)
                    act.activation(zexp[:], zmin[:], ACT.Exp).then_inc(AZ.sem, 1)
                if g3:
                    wait(act, QR1, "turned", g3.s)
                    act.activation(rT[:], ps_r[:], ACT.Copy).then_inc(AR1.sem, 1)
                    act.activation(r.rows[1][g3.b][:, :, 0:D], r.rows[0][g3.b][:, :, 0:D],
                                   ACT.Copy).then_inc(AR1.sem, 1)
                if g0:
                    wait(act, QX, "turned", g0.back(1))
                    normalise(act, c, norm1, GN1, AN1, xn, g0)
                if g1:
                    wait(act, VA, "centred", g1.s)
                    for q in range(2):
                        rows = slice(q * N, (q + 1) * N)
                        last = act.activation(pbd[rows, :, q * N:(q + 1) * N], e[rows, :, :], ACT.Exp)
                    last.then_inc(AA.sem, 1)
                if g0:
                    wait(act, QX, "turned", g0.s)
                    act.activation(xnT[:], ps_t[:], ACT.Copy).then_inc(AX1.sem, 1)
                if g1:
                    wait(act, QA, "probs_turned", g1.s)
                    act.activation(pT[:], ps_p[:], ACT.Copy).then_inc(AA.sem, 1)
                if g0:
                    wait(act, QX, "hs", g0.s)
                    act.activation(h[:].rearrange("p (b j) d -> p b (j d)", b=2), ps_h[:, :, 0:2 * (D + 1)],
                                   ACT.Copy).then_inc(AH1.sem, 1)
                if g3:
                    wait(act, VK, "gap", g3.s)
                    act.activation(r.egap[:], r.gap[:], ACT.Exp).then_inc(AR2.sem, 1)

            five_deep(act, body)

        @block.tensor
        def _(pe):
            pe.wait_ge(c.constants_made, 1)
            pe.wait_ge(loaded, 16 * 5)
            pe.matmul(ps_t[:, 0:2], wT_sb[:], a2_sb[:], start=True, stop=True).then_inc(ready, 1)
            pe.wait_ge(ready, 2)

            def body(g0, g1, g2, g3, g4):
                if g3:
                    wait(pe, AN2, "normed", g3.s)
                    wait(pe, AR1, "rT", g3.back(1))
                    for t in range(G):
                        last = pe.transpose(ps_r[:, t * P:(t + 1) * P], r.rows[0][g3.b][:, t, 0:D], c.ident[:])
                    last.then_inc(QR1.sem, 1)
                    wait(pe, AR1, "rT", g3.s)
                    wait(pe, VK, "carried", g3.back(1))
                    for t in range(G):
                        last = pe.matmul(r.ps_score[:, t * E0:(t + 1) * E0], rT[:, t * P:(t + 1) * P], gw_sb[:],
                                         start=True, stop=True)
                    last.then_inc(QR1.sem, 1)
                if g0:
                    wait(pe, AN1, "normed", g0.s)
                    wait(pe, AX1, "xnT", g0.back(1))
                    for t in range(G):
                        last = pe.transpose(ps_t[:, t * P:(t + 1) * P], xn[:, t, :], c.ident[:])
                    last.then_inc(QX.sem, 1)
                if g1:
                    wait(pe, AA, "exp", g1.s)
                    wait(pe, AA, "pT", g1.back(1))
                    for t in range(G):
                        last = pe.transpose(ps_p[:, t * P:(t + 1) * P], pbd[:, t, :], c.ident[:])
                    last.then_inc(QA.sem, 1)
                if g3:
                    route_tensor(pe, c, r, VS, VK, QR2, g3, E0)
                if g1:
                    wait(pe, AA, "pT", g1.s)
                    wait(pe, AH1, "h", g1.s)
                    wait(pe, VU, "z", g1.back(1))
                    for t in range(G):
                        last = pe.matmul(ps_o[:, t * P:(t + 1) * P], pT[:, t * P:(t + 1) * P],
                                         h[:, t, 0:D], start=True, stop=True)
                    last.then_inc(QA.sem, 1)
                if g0:
                    wait(pe, AX1, "xnT", g0.s)
                    wait(pe, AH1, "h", g0.back(1))
                    wait(pe, VA, "e", g0.back(1))
                    for t in range(G):
                        pe.matmul(ps_h[:, t // 2, (t % 2) * (D + 1):(t % 2 + 1) * (D + 1)],
                                  xnT[:, t * P:(t + 1) * P], w_sb[:], start=True, stop=True)
                    for q in range(2):
                        last = pe.matmul(ps_s[q * N:(q + 1) * N, :], wa2_wide[:],
                                         xnT[:].rearrange("p (t q n) -> p t q n", t=G, q=2)[:, :, q, :],
                                         start=True, stop=True)
                    last.then_inc(QX.sem, 1)

            five_deep(pe, body)


def gru_and_routing(nc, c, adj, gnn_wT, w_ihT, w_hhT, b_ih, b_hh, gate_w, gate_b, weights):
    pairs, layers = NG // 2, 3
    with ExitStack() as ctx:
        def sb(name, shape, dt=F32):
            return ctx.enter_context(nc.sbuf_tensor("g_" + name, shape, dt))

        def pb(name, shape, dt=F32):
            return ctx.enter_context(nc.psum_tensor("g_" + name, shape, dt))

        def sem(name):
            return ctx.enter_context(nc.semaphore("g_" + name))

        two = range(2)
        wT_sb = sb("wT", [D, layers * D])
        wi_sb = sb("wi", [D, 3 * D])
        wh_sb = sb("wh", [D, 3 * D])
        wv_sb = sb("wv", [D, layers, 3 * D])
        bi_sb = sb("bi", [D, 3])
        bh_sb = sb("bh", [D, 3])
        bsum = sb("bsum", [D, 3])
        gw_sb = sb("gw", [D, E1])
        gb_sb = sb("gb", [P, E1])
        y = [sb(f"y{b}", [P, G, TOPK, D]) for b in two]
        adj_sb = [sb(f"adj{b}", [P, G, N], I32) for b in two]
        edges = [sb(f"edges{b}", [P, G, P]) for b in two]
        head_norm, tail_norm = norm_buffers(sb, "head"), norm_buffers(sb, "tail")
        xn = sb("xn", [P, G, D])
        state = [[sb(f"state{l}_{b}", [D, GN]) for b in two] for l in range(layers + 1)]
        tok = [sb(f"tok{b}", [P, G, D]) for b in two]
        agg = [sb(f"agg{b}", [D, GN]) for b in two]
        rg = [sb(f"rg{b}", [D, GN]) for b in two]
        zg = [sb(f"zg{b}", [D, GN]) for b in two]
        cand = [sb(f"cand{b}", [D, GN]) for b in two]
        new = [sb(f"new{b}", [D, GN]) for b in two]
        rT = sb("rT", [P, GN])
        r = route_buffers(sb, pb, sem, "q_", E1)

        ps_r, ps_z = pb("ps_r", [P, GN]), pb("ps_z", [P, GN])
        ps_n = [pb(f"ps_n{b}", [P, GN]) for b in two]
        ps_hn = [pb(f"ps_hn{b}", [P, GN]) for b in two]
        ps_m = pb("ps_m", [P, GN])
        ps_q = pb("ps_q", [P, GN])
        ps_rows = [ps_q, ps_m]
        r.ps_score = ps_q[:, 0:G * E1]
        r.ps_rank = ps_q[:, G * E1:G * E1 + (G + 1) * E1]

        loaded, ready = sem("weights_loaded"), sem("weights_ready")
        next_loaded = sem("next_weights_loaded")
        arrived = [sem(f"arrived{b}") for b in two]
        s_turned, s_agged, s_gates = sem("turned"), sem("agged"), sem("gates")
        s_tok, s_aggT, s_sig, s_new = sem("tok"), sem("aggT"), sem("sigmoids"), sem("new")
        VR = Steps(sem("v_run"), "reset cand diff scaled state")
        VH = Steps(sem("v_head"), "add0 x2")
        VN = Steps(sem("v_head_norm"), "stats agg vare")
        VE = Steps(sem("v_edges"), "edges")
        QH, AH, GH = Steps(sem("q_head"), "turned"), Steps(sem("a_head"), "state"), Steps(sem("g_head"), "rstd shift")
        AN = Steps(sem("a_head_norm"), "normed")
        VT = Steps(sem("v_tail"), "x3 stats agg vare ids")
        VS = Steps(sem("v_scores"), "scores top where wheref hot0 hot1 both")
        VK = Steps(sem("v_ranks"), "ranked carried slot0 slot1 slots gap")
        QT1, QT2, QT3, QT4 = (Steps(sem(f"q_tail{k}"), n) for k, n in enumerate(("back", "turned", "scored", "ranked")))
        AT0, AT1 = Steps(sem("a_tail_norm"), "normed"), Steps(sem("a_tail_rows"), "rT rows_copied")
        AT2 = Steps(sem("a_tail_probs"), "p0 p1")
        GT = Steps(sem("g_tail"), "rstd shift")

        block = ctx.enter_context(nc.Block())

        def run_steps(eng, body):
            body(-1, True, False, False)
            body(0, True, True, False)
            body(1, True, True, True)
            with eng.Fori(2, pairs - 1) as n:
                body(n, True, True, True)
            body(pairs - 1, False, True, True)
            body(pairs, False, False, True)

        def u_of(n, layer, b):
            return n * 6 + (2 * layer + b)

        def after(eng, s, u, back=0):
            if type(u) is int and u - back < 0:
                return
            eng.wait_ge(s, u + (1 - back))

        def after_step(eng, steps, name, u, back=0):
            if type(u) is int and u - back < 0:
                return
            eng.wait_ge(steps.sem, u * 5 + (steps.names.index(name) + 1 - 5 * back))

        def group(n, b):
            return At(n, b)

        @block.sync
        def _(sp):
            first = ((wT_sb[:], gnn_wT), (wi_sb[:], w_ihT), (wh_sb[:], w_hhT), (bi_sb[:], b_ih), (bh_sb[:], b_hh),
                     (gw_sb[:], gate_w), (gb_sb[:], gate_b.partition_broadcast(P)))
            for dst, src in first:
                sp.dma_start(dst, src).then_inc(loaded, 16)

            def load(at):
                if type(at.s) is not int or at.s >= 2:
                    sp.wait_ge(arrived[at.b], 32 * at.half)
                    alone(sp, c)
                    wait(sp, VH, "x2", at.back(2))
                    alone(sp, c)
                    wait(sp, VE, "edges", at.back(2))
                    alone(sp, c)
                sp.dma_start(y[at.b][:], results_of(c.result0, at.s)).then_inc(arrived[at.b], 16)
                sp.dma_start(adj_sb[at.b][:], adj[bass.ds(at.s * GN, GN), :]
                             .rearrange("(t p) d -> p t d", p=P)).then_inc(arrived[at.b], 16)
                if behind(at, 2):
                    load_share(sp, weights, at.back(2), next_loaded)

            load(At(0, 0))
            load(At(0, 1))
            with sp.Fori(1, pairs) as i:
                load(At(i, 0))
                load(At(i, 1))
            for s in (NG - 2, NG - 1):
                load_share(sp, weights, s, next_loaded)
            sp.wait_ge(next_loaded, 16 * NG * len(weights))
            for b in two:
                sp.wait_ge(r.queued[b], 16 * TOPK * G * pairs)

        @block.gpsimd
        def _(pool):
            def body(n, has_head, has_run, has_tail):
                if has_tail:
                    rstd_and_shift(pool, c, tail_norm, VT, GT, AT0, group(n - 1, 0))
                    rstd_and_shift(pool, c, tail_norm, VT, GT, AT0, group(n - 1, 1))
                if has_head:
                    rstd_and_shift(pool, c, head_norm, VN, GH, AN, group(n + 1, 0))
                if has_tail:
                    queue_rows(pool, c, r, VK, AT1, c.queue1, group(n - 1, 0), 0, G)
                if has_head:
                    rstd_and_shift(pool, c, head_norm, VN, GH, AN, group(n + 1, 1))
                if has_tail:
                    queue_rows(pool, c, r, VK, AT1, c.queue1, group(n - 1, 0), G)
                    queue_rows(pool, c, r, VK, AT1, c.queue1, group(n - 1, 1))

            run_steps(pool, body)

        @block.tensor
        def _(pe):
            pe.wait_ge(loaded, 16 * 7)
            for l in range(layers):
                last = pe.matmul((ps_r, ps_z, ps_m)[l][:, 0:3 * D], wT_sb[:, l * D:(l + 1) * D], wi_sb[:],
                                 start=True, stop=True)
            last.then_inc(ready, 1)
            pe.wait_ge(ready, 2)

            def run(n, l, b):
                u = u_of(n, l, b)
                h = state[l][b]
                at = group(n, b)
                if l == 0:
                    wait(pe, AH, "state", at.s)
                else:
                    after_step(pe, VR, "state", u, 2)
                after_step(pe, VR, "cand", u, 2)
                for t in range(G):
                    last = pe.transpose(ps_n[b][:, t * P:(t + 1) * P], h[:, t * P:(t + 1) * P], c.ident[:])
                last.then_inc(s_turned, 1)
                pe.matmul(ps_hn[b][:], wh_sb[:, 2 * D:3 * D], h[:], start=True, stop=True)
                after(pe, s_tok, u)
                if l == 0:
                    wait(pe, VE, "edges", at.s)
                for t in range(G):
                    last = pe.matmul(ps_n[b][:, t * P:(t + 1) * P], tok[b][:, t, :], edges[b][:, t, :],
                                     start=True, stop=True)
                last.then_inc(s_agged, 1)
                after(pe, s_sig, u, 1)
                pe.matmul(ps_r[:], wh_sb[:, 0:D], h[:], start=True, stop=False)
                pe.matmul(ps_z[:], wh_sb[:, D:2 * D], h[:], start=True, stop=False)
                after(pe, s_aggT, u)
                pe.matmul(ps_r[:], wv_sb[:, l, 0:D], agg[b][:], start=False, stop=True)
                pe.matmul(ps_z[:], wv_sb[:, l, D:2 * D], agg[b][:], start=False, stop=True)
                pe.matmul(ps_n[b][:], wv_sb[:, l, 2 * D:3 * D], agg[b][:], start=True,
                          stop=True).then_inc(s_gates, 1)

            def head(at):
                wait(pe, AN, "normed", at.s)
                for t in range(G):
                    last = pe.transpose(ps_m[:, t * P:(t + 1) * P], xn[:, t, :], c.ident[:])
                last.then_inc(QH.sem, 1)

            def tail_back(n, b):
                after_step(pe, VR, "state", u_of(n - 1, 2, b))
                for t in range(G):
                    last = pe.transpose(ps_m[:, t * P:(t + 1) * P], state[layers][b][:, t * P:(t + 1) * P],
                                        c.ident[:])
                last.then_inc(QT1.sem, 1)

            def tail_turn(at):
                wait(pe, AT0, "normed", at.s)
                for t in range(G):
                    last = pe.transpose(ps_rows[at.b][:, t * P:(t + 1) * P], r.rows[0][at.b][:, t, 0:D], c.ident[:])
                last.then_inc(QT2.sem, 1)

            def tail_score(at):
                wait(pe, AT1, "rT", at.s)
                for t in range(G):
                    last = pe.matmul(r.ps_score[:, t * E1:(t + 1) * E1], rT[:, t * P:(t + 1) * P], gw_sb[:],
                                     start=True, stop=True)
                last.then_inc(QT3.sem, 1)

            def body(n, has_head, has_run, has_tail):
                pa = [group(n - 1, b) for b in two] if has_tail else None
                nx = [group(n + 1, b) for b in two] if has_head else None
                if has_run:
                    run(n, 0, 0)
                if has_tail:
                    if has_run:
                        wait(pe, AH, "state", At(n, 1).s)
                    wait(pe, AT1, "rT", pa[0].s - 1)
                    tail_back(n, 0)
                if has_run:
                    run(n, 0, 1)
                if has_tail:
                    wait(pe, VT, "x3", pa[0].s)
                    tail_back(n, 1)
                    wait(pe, VK, "carried", pa[0].s - 1)
                    tail_turn(pa[0])
                if has_run:
                    run(n, 1, 0)
                if has_tail:
                    tail_score(pa[0])
                    wait(pe, VT, "x3", pa[1].s)
                    tail_turn(pa[1])
                if has_run:
                    run(n, 1, 1)
                if has_tail:
                    tail_rank(pa[0])
                    tail_score(pa[1])
                if has_run:
                    run(n, 2, 0)
                if has_tail:
                    tail_rank(pa[1])
                if has_head:
                    if has_tail:
                        wait(pe, AT1, "rT", pa[1].s)
                    head(nx[0])
                if has_run:
                    run(n, 2, 1)
                if has_head:
                    wait(pe, AH, "state", nx[0].s)
                    head(nx[1])

            def tail_rank(at):
                route_tensor(pe, c, r, VS, VK, QT4, at, E1)

            run_steps(pe, body)

        @block.scalar
        def _(act):
            def tok_out(n, l, b):
                u = u_of(n, l, b)
                after(act, s_turned, u)
                act.activation(tok[b][:].rearrange("p t d -> p (t d)"), ps_n[b][:], ACT.Copy).then_inc(s_tok, 1)

            def agg_out(n, l, b):
                u = u_of(n, l, b)
                after(act, s_agged, u)
                act.activation(agg[b][:], ps_n[b][:], ACT.Copy).then_inc(s_aggT, 1)

            def sigmoids(n, l, b):
                u = u_of(n, l, b)
                after(act, s_gates, u)
                after_step(act, VR, "scaled", u, 2)
                act.activation(rg[b][:], ps_r[:], ACT.Sigmoid, bias=bsum[:, 0:1])
                act.activation(zg[b][:], ps_z[:], ACT.Sigmoid, bias=bsum[:, 1:2]).then_inc(s_sig, 1)

            def new_out(n, l, b):
                u = u_of(n, l, b)
                after_step(act, VR, "cand", u)
                act.activation(new[b][:], cand[b][:], ACT.Tanh, bias=bi_sb[:, 2:3]).then_inc(s_new, 1)

            def tail_rows(at):
                wait(act, QT2, "turned", at.s)
                wait(act, QT3, "scored", at.back(1))
                act.activation(rT[:], ps_rows[at.b][:], ACT.Copy).then_inc(AT1.sem, 1)
                act.activation(r.rows[1][at.b][:, :, 0:D], r.rows[0][at.b][:, :, 0:D], ACT.Copy).then_inc(AT1.sem, 1)

            def tail_probs(at):
                wait(act, VK, "gap", at.s)
                act.activation(c.prob[:, 0, bass.ds(at.s * G, G)], r.gap[:], ACT.Sigmoid, scale=-1.0).then_inc(AT2.sem, 1)
                act.activation(c.prob[:, 1, bass.ds(at.s * G, G)], r.gap[:], ACT.Sigmoid).then_inc(AT2.sem, 1)

            def head(at):
                wait(act, QH, "turned", at.s)
                act.activation(state[0][at.b][:], ps_m[:], ACT.Copy).then_inc(AH.sem, 1)

            def norm_tail(at):
                if type(at.s) is not int or at.s >= 2:
                    act.wait_ge(r.queued[at.b], 16 * TOPK * G * at.half)
                normalise(act, c, tail_norm, GT, AT0, r.rows[0][at.b], at)

            def norm_head(at):
                wait(act, QH, "turned", at.back(1))
                normalise(act, c, head_norm, GH, AN, xn, at)

            def body(n, has_head, has_run, has_tail):
                pa = [group(n - 1, b) for b in two] if has_tail else None
                nx = [group(n + 1, b) for b in two] if has_head else None
                order = [(l, b) for l in range(layers) for b in two]
                before_gates = {1: has_tail and (lambda: norm_tail(pa[0])), 2: has_tail and (lambda: norm_tail(pa[1])),
                                4: has_head and (lambda: norm_head(nx[0])), 5: has_head and (lambda: norm_head(nx[1]))}
                behind_tok = {2: has_tail and (lambda: tail_rows(pa[0])), 3: has_tail and (lambda: tail_rows(pa[1])),
                              5: has_head and has_run and (lambda: head(nx[0]))}
                for k, (l, b) in enumerate(order):
                    if has_run:
                        tok_out(n, l, b)
                    if has_run and k:
                        new_out(n, *order[k - 1])
                    if k == 0 and has_tail:
                        new_out(n - 1, *order[-1])
                    if k == 0 and has_run:
                        head(group(n, 1))
                    if k == 1 and has_tail and (type(n) is not int or n >= 2):
                        tail_probs(group(n - 2, 1))
                    if behind_tok.get(k):
                        behind_tok[k]()
                    if has_run:
                        agg_out(n, l, b)
                    if before_gates.get(k):
                        before_gates[k]()
                    if has_run:
                        sigmoids(n, l, b)
                    if k == 5 and has_tail:
                        tail_probs(pa[0])
                if not has_run and not has_head:
                    tail_probs(pa[1])
                if not has_run and has_head:
                    head(nx[0])

            run_steps(act, body)

        @block.vector
        def _(v):
            for b in two:
                v.memset(edges[b][:], 0.0)
            v.tensor_copy(c.carry[:], c.region[:, 0:E1])
            v.wait_ge(ready, 1)
            for l in range(layers):
                v.tensor_copy(wv_sb[:, l, :], (ps_r, ps_z, ps_m)[l][:, 0:3 * D])
            v.tensor_tensor(bsum[:], bi_sb[:], bh_sb[:], ALU.add).then_inc(ready, 1)

            def gates_1(n, l, b):
                u = u_of(n, l, b)
                after(v, s_sig, u)
                v.scalar_tensor_tensor(out=cand[b][:], in0=ps_hn[b][:], scalar=bh_sb[:, 2:3], in1=rg[b][:],
                                       op0=ALU.add, op1=ALU.mult).then_inc(VR.sem, 1)
                after_step(v, VR, "reset", u)
                v.tensor_tensor(cand[b][:], ps_n[b][:], cand[b][:], ALU.add).then_inc(VR.sem, 1)

            def gates_2(n, l, b):
                u = u_of(n, l, b)
                after(v, s_new, u)
                v.tensor_tensor(rg[b][:], state[l][b][:], new[b][:], ALU.subtract).then_inc(VR.sem, 1)
                after_step(v, VR, "diff", u)
                v.tensor_tensor(rg[b][:], rg[b][:], zg[b][:], ALU.mult).then_inc(VR.sem, 1)
                after_step(v, VR, "scaled", u)
                if l == layers - 1:
                    if type(n) is not int or n >= 1:
                        wait(v, QT1, "back", group(n - 1, b).s)
                v.tensor_tensor(state[l + 1][b][:], rg[b][:], new[b][:], ALU.add).then_inc(VR.sem, 1)

            def add_result(at, k):
                v.wait_ge(arrived[at.b], 32 * at.half + 32)
                if k:
                    wait(v, VH, "add0", at.s)
                for t in range(G):
                    last = combine(v, c, y[at.b], t, k, at.s)
                last.then_inc(VH.sem, 1)

            def head_stats(at):
                wait(v, VH, "x2", at.s)
                statistics(v, c, head_norm, VN, GH, at)

            def make_edges(at):
                v.wait_ge(arrived[at.b], 32 * at.half + 32)
                for q in two:
                    rows = slice(q * N, (q + 1) * N)
                    last = v.tensor_scalar(edges[at.b][rows, :, q * N:(q + 1) * N], adj_sb[at.b][rows, :, :], 0.0,
                                           None, ALU.not_equal)
                last.then_inc(VE.sem, 1)

            def tail_1(at):
                wait(v, QT1, "back", at.s)
                xs = c.x[:, bass.ds(at.s * G, G), :]
                v.tensor_tensor(xs, ps_m[:].rearrange("p (t d) -> p t d", t=G), xs, ALU.add).then_inc(VT.sem, 1)
                wait(v, VT, "x3", at.s)
                statistics(v, c, tail_norm, VT, GT, at)

            def tail_ids(at):
                if type(at.s) is not int or at.s >= 2:
                    v.wait_ge(r.queued[at.b], 16 * TOPK * G * at.half)
                for k in range(TOPK):
                    last = v.tensor_copy(r.rows[k][at.b][:, :, D:ROW].bitcast(I32),
                                         c.ids[:, k, bass.ds(at.s * G, G)].unsqueeze(2))
                last.then_inc(VT.sem, 1)

            def body(n, has_head, has_run, has_tail):
                pa = [group(n - 1, b) for b in two] if has_tail else None
                nx = [group(n + 1, b) for b in two] if has_head else None
                if has_run:
                    gates_1(n, 0, 0)
                if has_tail:
                    tail_1(pa[0])
                    tail_ids(pa[0])
                if has_run:
                    gates_2(n, 0, 0)
                if has_head:
                    add_result(nx[0], 0)
                if has_run:
                    gates_1(n, 0, 1)
                if has_tail:
                    tail_1(pa[1])
                    tail_ids(pa[1])
                if has_run:
                    gates_2(n, 0, 1)
                if has_head:
                    add_result(nx[0], 1)
                if has_run:
                    gates_1(n, 1, 0)
                if has_tail:
                    route_vector(v, c, r, VS, QT3, pa[0], E1, gb_sb[:], QT4)
                if has_run:
                    gates_2(n, 1, 0)
                if has_head:
                    head_stats(nx[0])
                if has_run:
                    gates_1(n, 1, 1)
                if has_tail:
                    route_vector(v, c, r, VS, QT3, pa[1], E1, gb_sb[:], QT4)
                if has_run:
                    gates_2(n, 1, 1)
                if has_head:
                    add_result(nx[1], 0)
                if has_tail:
                    route_vector_2(v, c, r, VK, AT2, QT4, pa[0], E1)
                if has_run:
                    gates_1(n, 2, 0)
                if has_head:
                    add_result(nx[1], 1)
                if has_run:
                    gates_2(n, 2, 0)
                if has_head:
                    head_stats(nx[1])
                    make_edges(nx[0])
                if has_run:
                    gates_1(n, 2, 1)
                if has_tail:
                    route_vector_2(v, c, r, VK, AT2, QT4, pa[1], E1)
                if has_run:
                    gates_2(n, 2, 1)
                if has_head:
                    make_edges(nx[1])

            run_steps(v, body)


def tile_table(nc, c, experts_n):
    tiles = tiles_of(experts_n)
    with ExitStack() as ctx:
        def sb(name, shape, dt=F32):
            return ctx.enter_context(nc.sbuf_tensor(f"t{experts_n}_" + name, shape, dt))

        held = sb("held", [1, experts_n])
        held_i = sb("held_i", [1, experts_n], I32)
        count_i = sb("count_i", [1, experts_n], I32)
        count = sb("count", [1, experts_n])
        unit = sb("unit", [1, experts_n])
        upto = sb("upto", [1, experts_n + 1])
        base = sb("base", [1, experts_n + 1])
        passed = sb("passed", [1, tiles, experts_n])
        expert = sb("expert", [1, tiles])
        is_it = sb("is_it", [1, tiles, experts_n + 1])
        row = sb("row", [1, tiles])
        digits = sb("digits", [1, tiles // PACK, PACK])
        word = sb("word", [1, tiles // PACK])
        done = ctx.enter_context(nc.semaphore(f"t{experts_n}_table_step"))
        block = ctx.enter_context(nc.Block())

        @block.vector
        def _(v):
            count_of = [0]

            def link(instruction):
                count_of[0] += 1
                instruction.then_inc(done, 1)
                v.wait_ge(done, count_of[0])

            last = experts_n - 1
            region = c.region[0:1, 0:experts_n]
            v.tensor_copy(c.carry_i[0:1, 0:experts_n], c.carry[0:1, 0:experts_n])
            v.memset(unit[:], 1.0)
            v.memset(upto[0:1, 0:1], 0.0)
            link(v.scalar_tensor_tensor(out=held[:], in0=c.carry[0:1, 0:experts_n], scalar=float(P - 1),
                                        in1=region, op0=ALU.add, op1=ALU.subtract))
            link(v.tensor_copy(held_i[:], held[:]))
            link(v.tensor_scalar(count_i[:], held_i[:], P.bit_length() - 1, None, ALU.arith_shift_right))
            link(v.tensor_copy(count[:], count_i[:]))
            link(v.tensor_tensor_scan(upto[0:1, 1:experts_n + 1], unit[:], count[:], 0.0, ALU.mult, ALU.add))
            link(v.scalar_tensor_tensor(out=base[:], in0=upto[:], scalar=-float(P),
                                        in1=c.region[0:1, 0:experts_n + 1], op0=ALU.mult, op1=ALU.add))
            link(v.tensor_tensor(passed[:], upto[0:1, None, 1:experts_n + 1].to_broadcast([1, tiles, experts_n]),
                                 bc(c.iota_j[0:1, 0:tiles], experts_n), ALU.is_le))
            link(v.tensor_reduce(expert[:], passed[:], AX.X, ALU.add))
            link(v.tensor_tensor(is_it[:], c.iota_e[0:1, None, 0:experts_n + 1].to_broadcast([1, tiles, experts_n + 1]),
                                 bc(expert[:], experts_n + 1), ALU.is_equal))
            link(v.tensor_tensor(is_it[:], is_it[:], base[0:1, None, :].to_broadcast([1, tiles, experts_n + 1]),
                                 ALU.mult))
            link(v.tensor_reduce(row[:], is_it[:], AX.X, ALU.add))
            link(v.scalar_tensor_tensor(out=c.tile_row[0:1, 0:tiles], in0=c.iota_j[0:1, 0:tiles],
                                        scalar=float(P), in1=row[:], op0=ALU.mult, op1=ALU.add))
            link(v.tensor_scalar(expert[:], expert[:], float(last), None, ALU.min))
            link(v.tensor_tensor(digits[:], expert[:].rearrange("p (w q) -> p w q", q=PACK),
                                 c.digit[0:1, None, :].to_broadcast([1, tiles // PACK, PACK]), ALU.mult))
            link(v.tensor_reduce(word[:], digits[:], AX.X, ALU.add))
            link(v.tensor_copy(c.tile_experts[0:1, 0:tiles // PACK], word[:]))


class Tile:

    def __init__(self, i, k):
        self.i, self.k = i + k // UNROLL if k >= 0 or type(i) is int else i - (-(k // UNROLL)), k % UNROLL
        self.j = self.i * UNROLL + self.k

    def done(self, back=0):
        return self.j + (1 - back) if back <= 1 else self.j - (back - 1)

    def first(self, n):
        return type(self.i) is int and self.j < n


def experts(nc, c, layer, queue, result, experts_n, chunks, up, down, up_b, down_b):
    tiles = tiles_of(experts_n)
    wide = 512
    with ExitStack() as ctx:
        def sb(name, shape, dt=F32):
            return ctx.enter_context(nc.sbuf_tensor(f"e{layer}_" + name, shape, dt))

        def pb(name, shape, dt=F32):
            return ctx.enter_context(nc.psum_tensor(f"e{layer}_" + name, shape, dt))

        def sem(name):
            return ctx.enter_context(nc.semaphore(f"e{layer}_" + name))

        xq = [sb(f"xq{k}", [P, ROW]) for k in range(UNROLL)]
        xT = [sb(f"xT{b}", [P, P]) for b in range(2)]
        h = [sb(f"h{b}", [P, chunks * P]) for b in range(2)]
        th = sb("th", [P, H1])
        gated = [sb(f"gated{b}", [P, H1]) for b in range(2)]
        hT = [sb(f"hT{b}", [P, chunks * P]) for b in range(2)]
        y = [sb(f"y{k}", [P, D]) for k in range(4)]
        ps_x = [pb(f"ps_x{b}", [P, 512]) for b in range(2)]
        ps_h = [pb(f"ps_h{b}", [P, wide]) for b in range(2)]
        ps_hT = [pb(f"ps_hT{b}", [P, 512]) for b in range(2)]
        ps_y = [pb(f"ps_y{b}", [P, 512]) for b in range(2)]
        padded = sem("padded")
        arrived = [sem(f"arrived{k}") for k in range(UNROLL)]
        x_turned, xT_copied, h_made, h_ready = sem("x_turned"), sem("xT_copied"), sem("h_made"), sem("h_ready")
        h_tanh, h_gated = sem("h_tanh"), sem("h_gated")
        h_turned, hT_copied, y_made, y_copied = sem("h_turned"), sem("hT_copied"), sem("y_made"), sem("y_copied")
        sent = [sem(f"sent{k}") for k in range(4)]

        per = UNROLL // PACK

        def steps(eng, body, weights_used=False):
            held = {}

            def step(i, k):
                lagged = [Tile(i, k - lag) for lag in range(4)]
                for lag, t in enumerate(lagged):
                    t.held = held.get((k - lag) // PACK)
                if type(i) is int:
                    lagged = [t if 0 <= t.j < tiles else None for t in lagged]
                body(*lagged)

            def words(i):
                if not weights_used:
                    return
                for q in range(-1, per):
                    at = i * per + q if q >= 0 else i * per - 1
                    if type(i) is int and not 0 <= at < tiles // PACK:
                        continue
                    held[q] = eng.value_load(c.tile_experts[0:1, bass.ds(at, 1)], min_val=0,
                                             max_val=(1 << (BITS * PACK)) - 1)

            words(0)
            for k in range(UNROLL):
                step(0, k)
            with eng.Fori(1, tiles // UNROLL) as i:
                words(i)
                for k in range(UNROLL):
                    step(i, k)
            words(tiles // UNROLL)
            for k in range(3):
                step(tiles // UNROLL, k)

        def sent_of(t):
            return t.i * (UNROLL // 4) + (t.k // 4 + 1)

        block = ctx.enter_context(nc.Block())

        @block.sync
        def _(sp):
            sp.dma_start(queue[experts_n * REGION:experts_n * (REGION + P), :].rearrange("(u p) r -> p u r", p=P),
                         c.pad[:, experts_n:2 * experts_n, :]).then_inc(padded, 16)
            for e in range(experts_n):
                at = sp.value_load(c.carry_i[0:1, e:e + 1], min_val=e * REGION, max_val=e * REGION + TOKENS)
                sp.dma_start(queue[bass.ds(at, P), :], c.pad[:, e, :]).then_inc(padded, 16)
            sp.wait_ge(padded, 16 * (experts_n + 1))

            def load(t):
                at = sp.value_load(c.tile_row[0:1, bass.ds(t.j, 1)], min_val=0,
                                   max_val=experts_n * (REGION + P) - P)
                if not t.first(UNROLL):
                    sp.wait_ge(sent[t.k % 4], (sent_of(t) - 2) * 16)
                    alone(sp, c)
                    sp.wait_ge(x_turned, t.done(UNROLL))
                    alone(sp, c)
                sp.dma_start(xq[t.k][:], queue[bass.ds(at, P), :]).then_inc(arrived[t.k], 16)

            for k in range(UNROLL):
                load(Tile(0, k))
            with sp.Fori(1, tiles // UNROLL) as i:
                for k in range(UNROLL):
                    load(Tile(i, k))

        @block.gpsimd
        def _(pool):
            def send(t):
                if t is None:
                    return
                pool.wait_ge(y_copied, t.done())
                alone(pool, c)
                pool.indirect_dma_start(
                    out=result, out_offset=bass.IndirectOffsetOnAxis(ap=xq[t.k][:, D:ROW].bitcast(U32), axis=0),
                    in_=y[t.k % 4][:], in_offset=None).then_inc(sent[t.k % 4], 16)

            steps(pool, lambda t0, t1, t2, t3: send(t3))
            for k in range(4):
                pool.wait_ge(sent[k], 16 * tiles // 4)

        def expert_of(t):
            return (t.held >> (BITS * (t.k % PACK))) & (experts_n - 1)

        @block.tensor
        def _(pe):
            def body(t0, t1, t2, t3):
                e1 = expert_of(t1) if t1 else None
                e3 = expert_of(t3) if t3 else None
                if t0:
                    pe.wait_ge(arrived[t0.k], 16 * (t0.i + 1))
                    if not t0.first(2):
                        pe.wait_ge(xT_copied, t0.done(2))
                    pe.transpose(ps_x[t0.k % 2][:, 0:P], xq[t0.k][:, 0:D], c.ident[:]).then_inc(x_turned, 1)
                if t1:
                    pe.wait_ge(xT_copied, t1.done())
                    if not t1.first(2):
                        pe.wait_ge(h_ready, t1.done(2))
                    pe.matmul(ps_h[t1.k % 2][:], xT[t1.k % 2][:], up[:, bass.ds(e1 * wide, wide)],
                              start=True, stop=True).then_inc(h_made, 1)
                if t2:
                    pe.wait_ge(h_ready, t2.done())
                    if not t2.first(2):
                        pe.wait_ge(hT_copied, t2.done(2))
                    for q in range(chunks):
                        last = pe.transpose(ps_hT[t2.k % 2][:, q * P:(q + 1) * P],
                                            h[t2.k % 2][:, q * P:(q + 1) * P], c.ident[:])
                    last.then_inc(h_turned, 1)
                if t3:
                    pe.wait_ge(hT_copied, t3.done())
                    if not t3.first(2):
                        pe.wait_ge(y_copied, t3.done(2))
                    for q in range(chunks):
                        last = pe.matmul(ps_y[t3.k % 2][:, 0:D], hT[t3.k % 2][:, q * P:(q + 1) * P],
                                         down[:, bass.ds(e3 * (chunks * P) + q * P, P)],
                                         start=(q == 0), stop=(q == chunks - 1))
                    last.then_inc(y_made, 1)

            steps(pe, body, True)

        @block.scalar
        def _(act):
            def body(t0, t1, t2, t3):
                if t0:
                    act.wait_ge(x_turned, t0.done())
                    if not t0.first(2):
                        act.wait_ge(h_made, t0.done(2))
                    act.activation(xT[t0.k % 2][:], ps_x[t0.k % 2][:, 0:P], ACT.Copy).then_inc(xT_copied, 1)
                if t1 and layer == 1:
                    act.wait_ge(h_made, t1.done())
                    if not t1.first(1):
                        act.wait_ge(h_gated, t1.done(1))
                    act.activation(th[:], ps_h[t1.k % 2][:, 0:H1], ACT.Tanh, scale=0.5).then_inc(h_tanh, 1)
                if t2:
                    act.wait_ge(h_turned, t2.done())
                    if not t2.first(2):
                        act.wait_ge(y_made, t2.done(2))
                    act.activation(hT[t2.k % 2][:], ps_hT[t2.k % 2][:, 0:chunks * P],
                                   ACT.Relu if layer == 0 else ACT.Copy).then_inc(hT_copied, 1)

            steps(act, body)

        @block.vector
        def _(v):
            def body(t0, t1, t2, t3):
                if layer == 0:
                    e1 = expert_of(t1) if t1 else None
                    e3 = expert_of(t3) if t3 else None
                if t1 and layer == 0:
                    v.wait_ge(h_made, t1.done())
                    if not t1.first(2):
                        v.wait_ge(h_turned, t1.done(2))
                    v.tensor_tensor(h[t1.k % 2][:], ps_h[t1.k % 2][:], up_b[:, bass.ds(e1 * wide, wide)],
                                    ALU.add).then_inc(h_ready, 1)
                if t1 and layer == 1:
                    v.wait_ge(h_tanh, t1.done())
                    v.scalar_tensor_tensor(out=gated[t1.k % 2][:], in0=th[:], scalar=1.0, in1=ps_h[t1.k % 2][:, 0:H1],
                                           op0=ALU.add, op1=ALU.mult).then_inc(h_gated, 1)
                    v.wait_ge(h_gated, t1.done())
                    if not t1.first(2):
                        v.wait_ge(h_turned, t1.done(2))
                    v.scalar_tensor_tensor(out=h[t1.k % 2][:], in0=gated[t1.k % 2][:], scalar=0.5,
                                           in1=ps_h[t1.k % 2][:, H1:2 * H1], op0=ALU.mult,
                                           op1=ALU.mult).then_inc(h_ready, 1)
                if t3:
                    v.wait_ge(y_made, t3.done())
                    if not t3.first(4):
                        v.wait_ge(sent[t3.k % 4], (sent_of(t3) - 1) * 16)
                    if layer == 0:
                        v.tensor_tensor(y[t3.k % 4][:], ps_y[t3.k % 2][:, 0:D], down_b[:, bass.ds(e3 * D, D)],
                                        ALU.add).then_inc(y_copied, 1)
                    else:
                        v.tensor_copy(y[t3.k % 4][:], ps_y[t3.k % 2][:, 0:D]).then_inc(y_copied, 1)

            steps(v, body, layer == 0)


def combine(v, c, y, t, k, g):
    tile = g * G + t
    return v.scalar_tensor_tensor(out=c.x[:, tile, :], in0=y[:, t, k, :],
                                  scalar=c.prob[:, k, bass.ds(tile, 1)], in1=c.x[:, tile, :],
                                  op0=ALU.mult, op1=ALU.add)


def results_of(result, s):
    return result[bass.ds(s * (TOPK * GN), TOPK * GN), :].rearrange("(t p k) d -> p t k d", p=P, k=TOPK)


def combine_out(nc, c, out):
    with ExitStack() as ctx:
        def sem(name):
            return ctx.enter_context(nc.semaphore("o_" + name))

        y = [ctx.enter_context(nc.sbuf_tensor(f"o_y{b}", [P, G, TOPK, D], F32)) for b in range(4)]
        arrived = [sem(f"arrived{b}") for b in range(4)]
        first_added, added = sem("first_added"), sem("added")
        stored = sem("stored")
        block = ctx.enter_context(nc.Block())

        @block.sync
        def _(sp):
            for s in range(4):
                sp.dma_start(y[s][:], results_of(c.result1, s)).then_inc(arrived[s], 16)
            with sp.Fori(1, NG // 4) as i:
                for b in range(4):
                    sp.wait_ge(added, i * 4 + (b - 3))
                    alone(sp, c)
                    sp.dma_start(y[b][:], results_of(c.result1, i * 4 + b)).then_inc(arrived[b], 16)

        @block.vector
        def _(v):
            with v.Fori(0, NG // 4) as i:
                for b in range(4):
                    s = i * 4 + b
                    v.wait_ge(arrived[b], (i + 1) * 16)
                    for t in range(G):
                        last = combine(v, c, y[b], t, 0, s)
                    last.then_inc(first_added, 1)
                    v.wait_ge(first_added, s + 1)
                    for t in range(G):
                        last = combine(v, c, y[b], t, 1, s)
                    last.then_inc(added, 1)

        @block.scalar
        def _(act):
            with act.Fori(0, NG) as s:
                act.wait_ge(added, s + 1)
                act.dma_start(out[bass.ds(s * GN, GN), :].rearrange("(t p) d -> p t d", p=P),
                              c.x[:, bass.ds(s * G, G), :]).then_inc(stored, 16)
            act.wait_ge(stored, 16 * NG)


def lay_out(x, adj, L0_gnn_W, L0_gnn_a, L0_ffn_Wg, L0_ffn_bg, L0_ffn_W1, L0_ffn_b1, L0_ffn_W2, L0_ffn_b2,
            L1_gnn_weight, L1_gnn_w_ih, L1_gnn_w_hh, L1_gnn_b_ih, L1_gnn_b_hh, L1_ffn_gate_w, L1_ffn_gate_b,
            L1_ffn_w1, L1_ffn_w2, L1_ffn_w3):
    import numpy as np
    a = {
        "x": x.reshape(TOKENS, D),
        "adj": adj.reshape(TOKENS, N),
        "gat_w": L0_gnn_W,
        "gat_wT": L0_gnn_W.T,
        "gat_a2": L0_gnn_a.reshape(2, D).T,
        "gate0_w": L0_ffn_Wg.T,
        "gate0_b": L0_ffn_bg,
        "w1": L0_ffn_W1.transpose(2, 0, 1).reshape(D, E0 * H0),
        "b1": L0_ffn_b1.reshape(E0 * H0),
        "w2": L0_ffn_W2.reshape(E0, D, H0 // P, P).transpose(3, 0, 2, 1).reshape(P, E0 * H0),
        "b2": L0_ffn_b2.reshape(E0 * D),
        "gnn_wT": L1_gnn_weight.transpose(2, 0, 1).reshape(D, 3 * D),
        "w_ihT": L1_gnn_w_ih.T,
        "w_hhT": L1_gnn_w_hh.T,
        "b_ih": L1_gnn_b_ih.reshape(3, D).T,
        "b_hh": L1_gnn_b_hh.reshape(3, D).T,
        "gate1_w": L1_ffn_gate_w,
        "gate1_b": L1_ffn_gate_b,
        "w12": np.stack([L1_ffn_w1, L1_ffn_w2], axis=2).transpose(1, 0, 2, 3).reshape(D, E1 * 2 * H1),
        "w3": L1_ffn_w3.reshape(E1, H1 // P, P, D).transpose(2, 0, 1, 3).reshape(P, E1 * H1),
    }
    return {k: np.ascontiguousarray(v) for k, v in a.items()}


def kernel(**inputs):
    import numpy as np
    import concourse.bacc as bacc
    from concourse.bass_utils import run_bass_kernel_spmd

    arrays = lay_out(**{k: np.asarray(v) for k, v in inputs.items()})
    nc = bacc.Bacc("TRN2", target_bir_lowering=False, num_devices=1)
    args = [nc.dram_tensor(k, a.shape, mybir.dt.from_np(a.dtype), kind="ExternalInput").ap()
            for k, a in arrays.items()]
    args.append(nc.dram_tensor("out", (TOKENS, D), F32, kind="ExternalOutput").ap())
    program(nc, *args)
    r = run_bass_kernel_spmd(nc, [arrays], core_ids=[0])
    return r.results[0]["out"].reshape(GRAPHS, N, D)
```

```python
import concourse.bass as bass
from concourse import mybir
from contextlib import ExitStack

F32 = mybir.dt.float32
BF16 = mybir.dt.bfloat16
I32 = mybir.dt.int32
U32 = mybir.dt.uint32
ALU = mybir.AluOpType
ACT = mybir.ActivationFunctionType
AX = mybir.AxisListType

P = 128
GRAPHS, N, D = 128, 64, 128
TOKENS = GRAPHS * N
NT = TOKENS // P
G = 4
NG = NT // G
GN = G * P
UNROLL = 8
PACK, BITS = 4, 4
SPAN = PACK + UNROLL
WORDS = 4
NEG = -9.0e15
EPS = 1e-5
E0, H0 = 8, 512
E1, H1 = 16, 256
TOPK = 2
LAYERS = 3
REGION = TOKENS + P
ROW = D + 1


class Steps:

    def __init__(self, sem, names):
        self.sem, self.names = sem, names.split()

    def upto(self, name, s):
        return s * len(self.names) + (self.names.index(name) + 1)


def wait(eng, steps, name, s):
    if type(s) is int and s < 0:
        return
    eng.wait_ge(steps.sem, steps.upto(name, s))


def alone(eng, c):
    eng.nop(nofuse=True)


def behind(at, n):
    return type(at.s) is not int or at.s >= n


class At:

    def __init__(self, i, j):
        self.i, self.j = i, j
        self.s = 2 * i + j if type(i) is int else (i * 2 + j if j >= 0 else i * 2 - (-j))
        self.b = j % 2
        k = j // 2
        self.half = i + k if type(i) is int or k >= 0 else i - (-k)

    def back(self, n):
        return self.s - n


def tiles_of(experts):
    most = (TOKENS * TOPK - experts) // P + experts
    return -(-most // UNROLL) * UNROLL


def program(nc, x, adj, gat_w, gat_wT, gat_a2, gate0_w, gate0_b, w1, b1, w2, b2,
            gnn_wT, w_ihT, w_hhT, b_ih, b_hh, gate1_w, gate1_b, w12, w3, out):
    with ExitStack() as ctx:
        def sb(name, shape, dt=F32):
            return ctx.enter_context(nc.sbuf_tensor(name, shape, dt))

        c = Shared()
        c.queue0 = nc.dram_tensor("queue0", (E0 * (REGION + P), ROW), F32, kind="Internal").ap()
        c.queue1 = nc.dram_tensor("queue1", (E1 * (REGION + P), ROW), F32, kind="Internal").ap()
        c.result0 = nc.dram_tensor("result0", (TOPK * TOKENS + 2 * E0 * P, D), F32, kind="Internal").ap()
        c.result1 = nc.dram_tensor("result1", (TOPK * TOKENS + 2 * E1 * P, D), F32, kind="Internal").ap()
        c.x = sb("x_res", [P, NT, D])
        c.ident = sb("ident", [P, P])
        c.before = sb("before", [P, P], BF16)
        c.ones = sb("ones", [P, P], BF16)
        c.iota_e = sb("iota_e", [P, E1 + 1])
        c.region = sb("region", [P, E1 + 1])
        c.carry = sb("carry", [P, E1])
        c.ids = sb("ids", [P, TOPK, NT], I32)
        c.prob = sb("prob", [P, TOPK, NT])
        c.half_neg = sb("half_neg", [P, G])
        c.pad = sb("pad", [P, 2 * E1, ROW])
        c.iota_j = sb("iota_j", [P, SPAN])
        c.digit = sb("digit", [P, SPAN])
        c.tile_row = sb("tile_row", [1, tiles_of(E1)], I32)
        c.tile_experts = sb("tile_experts", [1, tiles_of(E1) // UNROLL + 1, WORDS], I32)
        c.carry_i = sb("carry_i", [1, E1], I32)
        c.gnn_w = sb("gnn_w", [D, LAYERS * D])
        c.w_ih = sb("w_ih_sb", [D, 3 * D])
        c.w_hh = sb("w_hh_sb", [D, 3 * D])
        c.w_agg = sb("w_agg", [D, LAYERS, 3 * D])
        c.b_ih = sb("b_ih_sb", [D, 3])
        c.b_hh = sb("b_hh_sb", [D, 3])
        c.gate1_w = sb("gate1_w_sb", [D, E1])
        c.gate1_b = sb("gate1_b_sb", [P, E1])
        c.filled = ctx.enter_context(nc.semaphore("filled"))
        c.half_made = ctx.enter_context(nc.semaphore("half_made"))
        c.constants_made = ctx.enter_context(nc.semaphore("constants_made"))
        with ExitStack() as stage:
            up = stage.enter_context(nc.sbuf_tensor("w1_sb", [D, E0 * H0], F32))
            down = stage.enter_context(nc.sbuf_tensor("w2_sb", [P, E0 * H0], F32))
            up_b = stage.enter_context(nc.sbuf_tensor("b1_sb", [P, E0 * H0 // P], F32))
            down_b = stage.enter_context(nc.sbuf_tensor("b2_sb", [P, E0 * D], F32))
            weights, small_weights = ((up, w1), (down, w2)), (
                (up_b[:], b1), (down_b[:], b2.partition_broadcast(P)), (c.gnn_w[:], gnn_wT), (c.w_ih[:], w_ihT),
                (c.w_hh[:], w_hhT), (c.b_ih[:], b_ih), (c.b_hh[:], b_hh), (c.gate1_w[:], gate1_w),
                (c.gate1_b[:], gate1_b.partition_broadcast(P)))
            gat_and_routing(nc, c, x, adj, gat_w, gat_wT, gat_a2, gate0_w, gate0_b, weights, small_weights)
            experts(nc, c, 0, c.queue0, c.result0, E0, H0 // P, up, down, up_b, down_b)
        with ExitStack() as stage:
            up = stage.enter_context(nc.sbuf_tensor("w12_sb", [D, E1 * 2 * H1], F32))
            down = stage.enter_context(nc.sbuf_tensor("w3_sb", [P, E1 * H1], F32))
            gru_and_routing(nc, c, adj, ((up, w12), (down, w3)))
            experts(nc, c, 1, c.queue1, c.result1, E1, H1 // P, up, down, None, None)
        combine_out(nc, c, out)


class Shared:
    pass


def make_constants(pool, c):
    pool.memset(c.half_neg[:], -0.5).then_inc(c.half_made, 1)
    pool.memset(c.ident[:], 0.0).then_inc(c.filled, 1)
    pool.memset(c.before[:], 1.0).then_inc(c.filled, 1)
    pool.memset(c.ones[:], 1.0)
    for q in range(SPAN):
        pool.memset(c.digit[:, q:q + 1], float(1 << (BITS * (q % PACK))))
    pool.iota(c.iota_e[:], pattern=[[1, E1 + 1]], base=0, channel_multiplier=0,
              allow_small_or_imprecise_dtypes=True)
    pool.iota(c.region[:], pattern=[[REGION, E1 + 1]], base=0, channel_multiplier=0,
              allow_small_or_imprecise_dtypes=True)
    pool.iota(c.iota_j[:], pattern=[[1, SPAN]], base=-PACK, channel_multiplier=UNROLL,
              allow_small_or_imprecise_dtypes=True)
    for k in range(TOPK):
        pool.iota(c.ids[:, k, :], pattern=[[TOPK * P, NT]], base=k, channel_multiplier=TOPK)
    pool.wait_ge(c.filled, 2)
    pool.affine_select(out=c.ident[:], in_=c.ident[:], compare_op=ALU.not_equal, fill=1.0,
                       base=0, pattern=[[-1, P]], channel_multiplier=1)
    pool.affine_select(out=c.before[:], in_=c.before[:], compare_op=ALU.is_gt, fill=0.0,
                       base=0, pattern=[[1, P]], channel_multiplier=-1).then_inc(c.constants_made, 1)
    pool.memset(c.pad[:, :, 0:D], 0.0)
    pool.iota(c.pad[:, :, D:ROW].bitcast(I32), pattern=[[P, 2 * E1], [1, 1]],
              base=TOPK * TOKENS, channel_multiplier=1)


def bc(ap, n):
    return ap.unsqueeze(len(ap.shape)).to_broadcast([*ap.shape, n])


def norm_buffers(sb, name):
    m = Shared()
    m.stats = sb(name + "_stats", [P, G, 6])
    m.mv = sb(name + "_mv", [P, G, 2])
    m.vare = sb(name + "_vare", [P, G])
    m.minus_mean = sb(name + "_minus_mean", [P, G])
    m.rstd = sb(name + "_rstd", [P, G])
    m.shift = sb(name + "_shift", [P, G])
    return m


def statistics(v, c, m, V, Gs, at):
    statistics_1(v, c, m, V, at)
    statistics_2(v, c, m, V, at)
    statistics_3(v, c, m, V, Gs, at)


def statistics_1(v, c, m, V, at):
    alone(v, c)
    for t in range(G):
        last = v.bn_stats(m.stats[:, t, :], c.x[:, at.s * G + t, :])
    last.then_inc(V.sem, 1)


def statistics_2(v, c, m, V, at):
    wait(v, V, "stats", at.s)
    alone(v, c)
    for t in range(G):
        last = v.bn_aggr(m.mv[:, t, :], m.stats[:, t, :])
    last.then_inc(V.sem, 1)


def statistics_3(v, c, m, V, Gs, at):
    wait(v, V, "agg", at.s)
    wait(v, Gs, "shift", at.back(1))
    v.tensor_scalar(m.minus_mean[:], m.mv[:, :, 0], -1.0, None, ALU.mult)
    v.tensor_scalar(m.vare[:], m.mv[:, :, 1], EPS, None, ALU.add).then_inc(V.sem, 1)


def rstd_and_shift(pool, c, m, V, Gs, A, at):
    wait(pool, V, "vare", at.s)
    wait(pool, A, "normed", at.back(1))
    pool.tensor_tensor(m.rstd[:], m.vare[:], c.half_neg[:], ALU.pow).then_inc(Gs.sem, 1)
    wait(pool, Gs, "rstd", at.s)
    pool.tensor_tensor(m.shift[:], m.minus_mean[:], m.rstd[:], ALU.mult).then_inc(Gs.sem, 1)


def normalise(act, c, m, Gs, A, dst, at):
    wait(act, Gs, "shift", at.s)
    for t in range(G):
        last = act.activation(dst[:, t, 0:D], c.x[:, at.s * G + t, :], ACT.Identity,
                              bias=m.shift[:, t:t + 1], scale=m.rstd[:, t:t + 1])
    last.then_inc(A.sem, 1)


def route_vector(v, c, r, V, Q, at, experts_n, gate_b, QR):
    route_scores(v, r, V, Q, at, experts_n, gate_b)
    route_best(v, c, r, V, at, experts_n)
    route_hot(v, c, r, V, QR, at, experts_n)


def route_scores(v, r, V, Q, at, experts_n, gate_b):
    s = at.s
    wait(v, Q, "scored", s)
    v.tensor_tensor(r.score[:, :, 0:experts_n], r.ps_score[:, 0:G * experts_n].rearrange("p (t e) -> p t e", t=G),
                    gate_b[:, None, :].to_broadcast([P, G, experts_n]), ALU.add).then_inc(V.sem, 1)


def route_best(v, c, r, V, at, experts_n):
    s, b = at.s, at.b
    wait(v, V, "scores", s)
    alone(v, c)
    for t in range(G):
        last = v.max(r.top[b][:, t, :], r.score[:, t, 0:experts_n])
    last.then_inc(V.sem, 1)
    wait(v, V, "top", s)
    alone(v, c)
    for t in range(G):
        last = v.max_index(r.where[:, t, :], r.top[b][:, t, :], r.score[:, t, 0:experts_n])
    last.then_inc(V.sem, 1)


def route_hot(v, c, r, V, QR, at, experts_n):
    s, b = at.s, at.b
    wait(v, V, "where", s)
    v.tensor_copy(r.wheref[:], r.where[:, :, 0:TOPK]).then_inc(V.sem, 1)
    wait(v, V, "wheref", s)
    iota = c.iota_e[:, None, 0:experts_n].to_broadcast([P, G, experts_n])
    for k in range(TOPK):
        v.tensor_tensor(r.hot[k][b][:], iota, bc(r.wheref[:, :, k], experts_n), ALU.is_equal).then_inc(V.sem, 1)
    wait(v, V, "hot1", s)
    wait(v, QR, "ranked", at.back(2))
    v.tensor_tensor(r.both[b][:], r.hot[0][b][:], r.hot[1][b][:], ALU.add).then_inc(V.sem, 1)


def route_vector_2(v, c, r, V, A, Q, at, experts_n):
    route_ranks(v, c, r, V, Q, at, experts_n)
    route_slots(v, r, V, A, at)


def route_ranks(v, c, r, V, Q, at, experts_n):
    s, b = at.s, at.b
    carry = c.carry[:, 0:experts_n]
    wait(v, Q, "ranked", s)
    wait(v, V, "carried", at.back(1))
    v.tensor_tensor(r.rank[:], r.ps_rank[:, 0:G * experts_n].rearrange("p (t e) -> p t e", t=G),
                    carry[:, None, :].to_broadcast([P, G, experts_n]), ALU.add).then_inc(V.sem, 1)
    wait(v, V, "ranked", s)
    v.tensor_tensor(carry, r.ps_rank[:, G * experts_n:(G + 1) * experts_n], carry, ALU.add).then_inc(V.sem, 1)
    for k in range(TOPK):
        v.tensor_tensor(r.pick[k][:], r.hot[k][b][:], r.rank[:], ALU.mult).then_inc(r.picked, 1)


def route_slots(v, r, V, A, at):
    s, b = at.s, at.b
    for k in range(TOPK):
        v.wait_ge(r.picked, s * TOPK + (k + 1))
        v.tensor_reduce(r.slotf[:, k, :], r.pick[k][:], AX.X, ALU.add).then_inc(V.sem, 1)
    wait(v, V, "slot1", s)
    v.tensor_copy(r.slots[b][:], r.slotf[:]).then_inc(V.sem, 1)
    if A:
        wait(v, A, "p1", at.back(1))
    v.tensor_tensor(r.gap[:], r.top[b][:, :, 1], r.top[b][:, :, 0], ALU.subtract).then_inc(V.sem, 1)


def route_vector_3(v, c, r, V, A, at):
    s = at.s
    wait(v, A, "gap_exp", s)
    v.tensor_scalar(r.den[:], r.egap[:], 1.0, None, ALU.add).then_inc(V.sem, 1)
    wait(v, V, "den", s)
    v.reciprocal(c.prob[:, 0, bass.ds(s * G, G)], r.den[:]).then_inc(V.sem, 1)
    wait(v, V, "p0", s)
    v.tensor_tensor(c.prob[:, 1, bass.ds(s * G, G)], r.egap[:], c.prob[:, 0, bass.ds(s * G, G)],
                    ALU.mult).then_inc(V.sem, 1)


def route_tensor(pe, c, r, V, VR, Q, at, experts_n):
    wait(pe, V, "both", at.s)
    wait(pe, VR, "carried", at.back(1))
    for t in range(G + 1):
        cols = r.ps_rank[:, t * experts_n:(t + 1) * experts_n]
        for u in range(min(t, G - 1) + 1):
            last = pe.matmul(cols, c.before[:] if u == t else c.ones[:], r.both[at.b][:, u, :],
                             start=(u == 0), stop=(u == min(t, G - 1)))
    last.then_inc(Q.sem, 1)


def route_buffers(sb, pb, sem, prefix, experts_n):
    r = Shared()
    r.score = sb(prefix + "score", [P, G, experts_n])
    r.top = [sb(prefix + f"top{b}", [P, G, 8]) for b in range(2)]
    r.where = sb(prefix + "where", [P, G, 8], U32)
    r.wheref = sb(prefix + "wheref", [P, G, TOPK])
    r.hot = [[sb(prefix + f"hot{k}_{b}", [P, G, experts_n]) for b in range(2)] for k in range(TOPK)]
    r.both = [sb(prefix + f"both{b}", [P, G, experts_n], BF16) for b in range(2)]
    r.rank = sb(prefix + "rank", [P, G, experts_n])
    r.pick = [sb(prefix + f"pick{k}", [P, G, experts_n]) for k in range(TOPK)]
    r.slotf = sb(prefix + "slotf", [P, TOPK, G])
    r.slots = [sb(prefix + f"slots{b}", [P, TOPK, G], U32) for b in range(2)]
    r.gap = sb(prefix + "gap", [P, G])
    r.egap = sb(prefix + "egap", [P, G])
    r.den = sb(prefix + "den", [P, G])
    r.rows = [[sb(prefix + f"rows{k}_{b}", [P, G, ROW]) for b in range(2)] for k in range(TOPK)]
    r.picked = sem(prefix + "picked")
    r.queued = [sem(prefix + f"queued{b}") for b in range(2)]
    return r


def queue_rows(pool, c, r, V, A, queue, at, first=0, last=TOPK * G):
    wait(pool, V, "slots", at.s)
    wait(pool, A, "rows_copied", at.s)
    alone(pool, c)
    for k, t in [divmod(m, G) for m in range(first, last)]:
        pool.indirect_dma_start(
            out=queue, out_offset=bass.IndirectOffsetOnAxis(ap=r.slots[at.b][:, k, t:t + 1], axis=0),
            in_=r.rows[k][at.b][:, t, :], in_offset=None).then_inc(r.queued[at.b], 16)


def five_deep(eng, body):

    def step(i, j):
        groups = [At(i, j - lag) for lag in range(5)]
        if type(i) is int:
            groups = [g if 0 <= g.s < NG else None for g in groups]
        body(*groups)

    for n in range(6):
        step(n // 2, n % 2)
    with eng.Fori(3, NG // 2) as i:
        step(i, 0)
        step(i, 1)
    for n in range(4):
        step(NG // 2, n)


def table_buffers(sb, sem, experts_n):
    b = Shared()
    b.held = sb("t_held", [P, experts_n])
    b.held_i = sb("t_held_i", [P, experts_n], I32)
    b.count_i = sb("t_count_i", [P, experts_n], I32)
    b.count = sb("t_count", [P, experts_n])
    b.unit = sb("t_unit", [P, experts_n])
    b.upto = sb("t_upto", [P, experts_n + 1])
    b.base = sb("t_base", [P, experts_n + 1])
    b.passed = sb("t_passed", [P, SPAN, experts_n])
    b.is_it = sb("t_is_it", [P, SPAN, experts_n + 1])
    b.expert = sb("t_expert", [P, SPAN])
    b.row = sb("t_row", [P, SPAN])
    b.row_i = sb("t_row_i", [P, SPAN], I32)
    b.word = sb("t_word", [P, SPAN // PACK])
    b.word_i = sb("t_word_i", [P, WORDS], I32)
    b.carry_made = sem("t_carry_made")
    b.made = sem("t_made")
    b.step = sem("t_step")
    b.written = sem("t_written")
    b.padded = [sem(f"t_padded{k}") for k in range(2)]
    return b


def tile_table(v, c, b, experts_n):
    count_of = [0]

    def link(instruction):
        count_of[0] += 1
        instruction.then_inc(b.step, 1)
        v.wait_ge(b.step, count_of[0])

    def each(ap, n):
        return ap[:, None, :].to_broadcast([P, SPAN, n])

    v.tensor_copy(c.carry_i[0:1, 0:experts_n], c.carry[0:1, 0:experts_n]).then_inc(b.carry_made, 1)
    v.memset(b.unit[:], 1.0)
    v.memset(b.word_i[:], 0)
    v.memset(b.upto[:, 0:1], 0.0)
    link(v.scalar_tensor_tensor(out=b.held[:], in0=c.carry[:, 0:experts_n], scalar=float(P - 1),
                                in1=c.region[:, 0:experts_n], op0=ALU.add, op1=ALU.subtract))
    link(v.tensor_copy(b.held_i[:], b.held[:]))
    link(v.tensor_scalar(b.count_i[:], b.held_i[:], P.bit_length() - 1, None, ALU.arith_shift_right))
    link(v.tensor_copy(b.count[:], b.count_i[:]))
    link(v.tensor_tensor_scan(b.upto[:, 1:experts_n + 1], b.unit[:], b.count[:], 0.0, ALU.mult, ALU.add))
    link(v.scalar_tensor_tensor(out=b.base[:], in0=b.upto[:], scalar=-float(P),
                                in1=c.region[:, 0:experts_n + 1], op0=ALU.mult, op1=ALU.add))
    link(v.tensor_tensor(b.passed[:], each(b.upto[:, 1:experts_n + 1], experts_n), bc(c.iota_j[:], experts_n),
                         ALU.is_le))
    link(v.tensor_reduce(b.expert[:], b.passed[:], AX.X, ALU.add))
    link(v.tensor_tensor(b.is_it[:], each(c.iota_e[:, 0:experts_n + 1], experts_n + 1),
                         bc(b.expert[:], experts_n + 1), ALU.is_equal))
    link(v.tensor_tensor(b.is_it[:], b.is_it[:], each(b.base[:], experts_n + 1), ALU.mult))
    link(v.tensor_reduce(b.row[:], b.is_it[:], AX.X, ALU.add))
    link(v.scalar_tensor_tensor(out=b.row_i[:], in0=c.iota_j[:], scalar=float(P), in1=b.row[:],
                                op0=ALU.mult, op1=ALU.add))
    link(v.tensor_scalar(b.expert[:], b.expert[:], float(experts_n - 1), None, ALU.min))
    link(v.tensor_tensor(b.expert[:], b.expert[:], c.digit[:], ALU.mult))
    link(v.tensor_reduce(b.word[:], b.expert[:].rearrange("p (w q) -> p w q", q=PACK), AX.X, ALU.add))
    v.tensor_copy(b.word_i[:, 0:SPAN // PACK], b.word[:]).then_inc(b.made, 1)


def write_table(eng, c, b, experts_n):
    rounds = tiles_of(experts_n) // UNROLL
    eng.wait_ge(b.made, 1)
    eng.dma_start(c.tile_row[0:1, 0:rounds * UNROLL].rearrange("o (i k) -> o i k", k=UNROLL),
                  b.row_i[0:rounds, PACK:SPAN]).then_inc(b.written, 16)
    eng.dma_start(c.tile_experts[0:1, 0:rounds + 1, :], b.word_i[0:rounds + 1, :]).then_inc(b.written, 16)

def pad_queues(eng, c, b, queue, experts_n, half):
    per = experts_n // 2
    first = experts_n * REGION + half * per * P
    eng.dma_start(queue[first:first + per * P, :].rearrange("(u p) r -> p u r", p=P),
                  c.pad[:, experts_n + half * per:experts_n + (half + 1) * per, :]).then_inc(b.padded[half], 16)
    eng.wait_ge(b.carry_made, 1)
    for e in range(half, experts_n, 2):
        at = eng.value_load(c.carry_i[0:1, e:e + 1], min_val=e * REGION, max_val=e * REGION + TOKENS)
        eng.dma_start(queue[bass.ds(at, P), :], c.pad[:, e, :]).then_inc(b.padded[half], 16)

def wait_table(sp, b, experts_n):
    for half in range(2):
        sp.wait_ge(b.padded[half], 16 * (experts_n // 2 + 1))
    sp.wait_ge(b.written, 16 * 2)


def load_share(sp, weights, s, loaded):
    for dst, src in weights:
        share = dst.shape[1] // NG
        sp.dma_start(dst[:, bass.ds(s * share, share)], src[:, bass.ds(s * share, share)]).then_inc(loaded, 16)


def gat_and_routing(nc, c, x, adj, gat_w, gat_wT, gat_a2, gate_w, gate_b, weights, small_weights):
    with ExitStack() as ctx:
        def sb(name, shape, dt=F32):
            return ctx.enter_context(nc.sbuf_tensor("a_" + name, shape, dt))

        def pb(name, shape, dt=F32):
            return ctx.enter_context(nc.psum_tensor("a_" + name, shape, dt))

        def sem(name):
            return ctx.enter_context(nc.semaphore("a_" + name))

        w_sb = sb("w", [D, D + 1])
        wT_sb = sb("wT", [D, D])
        a2_sb = sb("a2", [D, 2])
        wa2_wide = sb("wa2_wide", [D, N])
        gw_sb = sb("gw", [D, E0])
        gb_sb = sb("gb", [P, E0])
        adj_sb = [sb(f"adj{b}", [P, G, N], I32) for b in range(2)]
        neg = sb("neg", [P, G, N])
        norm1, norm2 = norm_buffers(sb, "norm1"), norm_buffers(sb, "norm2")
        xn, xn2 = sb("xn", [P, G, D]), sb("xn2", [P, G, D])
        xnT = sb("xnT", [P, GN])
        h = [sb(f"h{b}", [P, G, D + 1]) for b in range(2)]
        e = sb("e", [P, G, N])
        rowmax = sb("rowmax", [P, G])
        pbd = sb("pbd", [P, G, P])
        rowsum = sb("rowsum", [P, G])
        rinv = sb("rinv", [P, G])
        pT = sb("pT", [P, GN])
        z = sb("z", [P, G, D])
        zmin = sb("zmin", [P, G, D])
        zexp = sb("zexp", [P, G, D])
        act_warm = sb("act_warm", [P, 1])
        xz = sb("xz", [P, G, D])
        rT = sb("rT", [P, GN])
        r = route_buffers(sb, pb, sem, "r_", E0)
        table = table_buffers(sb, sem, E0)

        ps_t = pb("ps_t", [P, GN])
        ps_h = pb("ps_h", [P, 2, GN])
        ps_s = pb("ps_s", [P, G * N])
        ps_p = pb("ps_p", [P, GN])
        ps_o = pb("ps_o", [P, GN])
        ps_r = pb("ps_r", [P, GN])
        ps_q = pb("ps_q", [P, GN])
        r.ps_score = ps_q[:, 0:G * E0]
        r.ps_rank = ps_q[:, G * E0:G * E0 + (G + 1) * E0]

        loaded, next_loaded = sem("weights_loaded"), sem("next_weights_loaded")
        small_loaded, product_made = sem("small_weights_loaded"), sem("product_made")
        arrived = [sem(f"arrived{b}") for b in range(2)]
        ready = sem("weights_ready")
        VN1, VN2 = (Steps(sem(f"v_norm{k}"), "stats agg vare") for k in (1, 2))
        GN1, GN2 = (Steps(sem(f"g_norm{k}"), "rstd shift") for k in (1, 2))
        AN1, AN2 = (Steps(sem(f"a_norm{k}"), "normed") for k in (1, 2))
        VM = Steps(sem("v_mask"), "neg")
        VA = Steps(sem("v_attend"), "e lrelu masked max centred sum rinv")
        VU = Steps(sem("v_update"), "z zmin xz x1")
        VS = Steps(sem("v_scores"), "ids scores top where wheref hot0 hot1 both")
        VK = Steps(sem("v_ranks"), "ranked carried slot0 slot1 slots gap")
        VP = Steps(sem("v_weights"), "den p0 p1")
        AX1, AH1 = Steps(sem("a_turned"), "xnT"), Steps(sem("a_h"), "h")
        AA, AZ = Steps(sem("a_attend"), "exp pT"), Steps(sem("a_update"), "zexp")
        AR1, AR2 = Steps(sem("a_rows"), "rT rows_copied"), Steps(sem("a_weights"), "gap_exp")
        QX, QA = Steps(sem("q_project"), "turned h s"), Steps(sem("q_attend"), "probs_turned mixed")
        QR1, QR2 = Steps(sem("q_route"), "turned scored"), Steps(sem("q_ranks"), "ranked")

        block = ctx.enter_context(nc.Block())

        @block.sync
        def _(sp):
            def load(at, first):
                if not first:
                    sp.wait_ge(arrived[at.b], 32 * at.half)
                    alone(sp, c)
                    wait(sp, VM, "neg", at.back(2))
                    alone(sp, c)
                rows = x[bass.ds(at.s * GN, GN), :]
                sp.dma_start(c.x[:, bass.ds(at.s * G, G), :],
                             rows.rearrange("(t p) d -> p t d", p=P)).then_inc(arrived[at.b], 16)
                sp.dma_start(adj_sb[at.b][:], adj[bass.ds(at.s * GN, GN), :]
                             .rearrange("(t p) d -> p t d", p=P)).then_inc(arrived[at.b], 16)
                if behind(at, 2):
                    load_share(sp, weights, at.back(2), next_loaded)

            load(At(0, 0), True)
            for dst, src in ((w_sb[:, 0:D], gat_w), (wT_sb[:], gat_wT), (a2_sb[:], gat_a2), (gw_sb[:], gate_w),
                             (gb_sb[:], gate_b.partition_broadcast(P))):
                sp.dma_start(dst, src).then_inc(loaded, 16)
            load(At(0, 1), True)
            for dst, src in small_weights:
                sp.dma_start(dst, src).then_inc(small_loaded, 16)
            with sp.Fori(1, NG // 2) as i:
                load(At(i, 0), False)
                load(At(i, 1), False)
            for s in (NG - 2, NG - 1):
                load_share(sp, weights, s, next_loaded)
            sp.wait_ge(loaded, 16 * 5)
            sp.wait_ge(next_loaded, 16 * NG * len(weights))
            pad_queues(sp, c, table, c.queue0, E0, 0)
            wait_table(sp, table, E0)
            for b in range(2):
                sp.wait_ge(r.queued[b], 16 * TOPK * G * (NG // 2))

        @block.gpsimd
        def _(pool):
            make_constants(pool, c)

            def body(g0, g1, g2, g3, g4):
                if g4:
                    queue_rows(pool, c, r, VK, AR1, c.queue0, g4, 0, 3)
                if g0:
                    rstd_and_shift(pool, c, norm1, VN1, GN1, AN1, g0)
                if g4:
                    queue_rows(pool, c, r, VK, AR1, c.queue0, g4, 3, 5)
                if g2:
                    rstd_and_shift(pool, c, norm2, VN2, GN2, AN2, g2)
                if g4:
                    queue_rows(pool, c, r, VK, AR1, c.queue0, g4, 5, 8)

            five_deep(pool, body)

        @block.vector
        def _(v):
            v.wait_ge(c.constants_made, 1)
            v.tensor_copy(c.carry[:], c.region[:, 0:E1])
            v.memset(pbd[:], 0.0)

            def finish_weights():
                v.wait_ge(ready, 1)
                v.tensor_copy(w_sb[:, D:D + 1], ps_t[:, 0:1])
                v.tensor_copy(wa2_wide[:], ps_t[:, 1:2].to_broadcast([D, N])).then_inc(ready, 1)

            def body(g0, g1, g2, g3, g4):
                if g2:
                    xs = c.x[:, bass.ds(g2.s * G, G), :]
                    wait(v, QA, "mixed", g2.s)
                    wait(v, VA, "rinv", g2.s)
                    v.tensor_tensor(z[:], ps_o[:].rearrange("p (t d) -> p t d", t=G), bc(rinv[:], D),
                                    ALU.mult).then_inc(VU.sem, 1)
                if g0:
                    v.wait_ge(arrived[g0.b], 32 * g0.half + 32)
                    statistics_1(v, c, norm1, VN1, g0)
                if g2:
                    wait(v, VU, "z", g2.s)
                    v.tensor_scalar(zmin[:], z[:], 0.0, None, ALU.min).then_inc(VU.sem, 1)
                if g0:
                    statistics_2(v, c, norm1, VN1, g0)
                if g2:
                    v.scalar_tensor_tensor(out=xz[:], in0=z[:], scalar=0.0, in1=xs,
                                           op0=ALU.max, op1=ALU.add).then_inc(VU.sem, 1)
                if g0:
                    statistics_3(v, c, norm1, VN1, GN1, g0)
                    if type(g0.s) is int and g0.s == 0:
                        finish_weights()
                if g2:
                    wait(v, VU, "xz", g2.s)
                    wait(v, AZ, "zexp", g2.s)
                    v.scalar_tensor_tensor(out=xs, in0=zexp[:], scalar=-1.0, in1=xz[:],
                                           op0=ALU.add, op1=ALU.add).then_inc(VU.sem, 1)
                if g1:
                    wait(v, AH1, "h", g1.s)
                    wait(v, QX, "s", g1.s)
                    wait(v, AA, "exp", g1.back(1))
                    v.tensor_tensor(e[:], ps_s[:].rearrange("p (t n) -> p t n", t=G), bc(h[g1.b][:, :, D], N),
                                    ALU.add).then_inc(VA.sem, 1)
                if g2:
                    wait(v, VU, "x1", g2.s)
                    statistics_1(v, c, norm2, VN2, g2)
                if g1:
                    wait(v, VA, "e", g1.s)
                    v.scalar_tensor_tensor(out=e[:], in0=e[:], scalar=0.2, in1=e[:], op0=ALU.mult,
                                           op1=ALU.max).then_inc(VA.sem, 1)
                if g2:
                    statistics_2(v, c, norm2, VN2, g2)
                if g1:
                    wait(v, VA, "lrelu", g1.s)
                    wait(v, VM, "neg", g1.s)
                    v.tensor_tensor(e[:], e[:], neg[:], ALU.add).then_inc(VA.sem, 1)
                if g2:
                    statistics_3(v, c, norm2, VN2, GN2, g2)
                if g1:
                    wait(v, VA, "masked", g1.s)
                    v.tensor_reduce(rowmax[:], e[:], AX.X, ALU.max).then_inc(VA.sem, 1)
                if g0:
                    v.tensor_scalar(neg[:], adj_sb[g0.b][:], 0.0, NEG, ALU.is_le, ALU.mult).then_inc(VM.sem, 1)
                if g1:
                    wait(v, VA, "max", g1.s)
                    v.tensor_tensor(e[:], e[:], bc(rowmax[:], N), ALU.subtract).then_inc(VA.sem, 1)
                if g3:
                    if behind(g3, 2):
                        v.wait_ge(r.queued[g3.b], 16 * TOPK * G * g3.half)
                    for k in range(TOPK):
                        last = v.tensor_copy(r.rows[k][g3.b][:, :, D:ROW].bitcast(I32),
                                             c.ids[:, k, bass.ds(g3.s * G, G)].unsqueeze(2))
                    last.then_inc(VS.sem, 1)
                    route_scores(v, r, VS, QR1, g3, E0, gb_sb[:])
                    route_best(v, c, r, VS, g3, E0)
                    route_hot(v, c, r, VS, QR2, g3, E0)
                if g1:
                    wait(v, AA, "exp", g1.s)
                    v.tensor_reduce(rowsum[:], pbd[:], AX.X, ALU.add).then_inc(VA.sem, 1)
                    wait(v, VA, "sum", g1.s)
                    v.reciprocal(rinv[:], rowsum[:]).then_inc(VA.sem, 1)
                if g4:
                    route_vector_3(v, c, r, VP, AR2, g4)
                if g3:
                    route_ranks(v, c, r, VK, QR2, g3, E0)
                    route_slots(v, r, VK, None, g3)

            five_deep(v, body)
            tile_table(v, c, table, E0)

        @block.scalar
        def _(act):
            act.wait_ge(c.half_made, 1)
            act.activation(act_warm[:], c.half_neg[:, 0:1], ACT.Exp)
            act.wait_ge(ready, 2)

            def body(g0, g1, g2, g3, g4):
                if g2:
                    wait(act, VU, "zmin", g2.s)
                    act.activation(zexp[:], zmin[:], ACT.Exp).then_inc(AZ.sem, 1)
                if g3:
                    wait(act, QR1, "turned", g3.s)
                    act.activation(rT[:], ps_r[:], ACT.Copy).then_inc(AR1.sem, 1)
                    if behind(g3, 2):
                        act.wait_ge(r.queued[g3.b], 16 * TOPK * G * g3.half)
                    wait(act, AN2, "normed", g3.s)
                    for k in range(TOPK):
                        last = act.activation(r.rows[k][g3.b][:, :, 0:D], xn2[:], ACT.Copy)
                    last.then_inc(AR1.sem, 1)
                if g1:
                    wait(act, VA, "centred", g1.s)
                    for q in range(2):
                        rows = slice(q * N, (q + 1) * N)
                        last = act.activation(pbd[rows, :, q * N:(q + 1) * N], e[rows, :, :], ACT.Exp)
                    last.then_inc(AA.sem, 1)
                if g0:
                    wait(act, QX, "turned", g0.back(1))
                    normalise(act, c, norm1, GN1, AN1, xn, g0)
                if g1:
                    wait(act, QA, "probs_turned", g1.s)
                    act.activation(pT[:], ps_p[:], ACT.Copy).then_inc(AA.sem, 1)
                if g0:
                    wait(act, QX, "turned", g0.s)
                    act.activation(xnT[:], ps_t[:], ACT.Copy).then_inc(AX1.sem, 1)
                if g2:
                    wait(act, AR1, "rows_copied", g2.back(1))
                    normalise(act, c, norm2, GN2, AN2, xn2, g2)
                if g0:
                    wait(act, QX, "h", g0.s)
                    act.activation(h[g0.b][:].rearrange("p (b j) d -> p b (j d)", b=2), ps_h[:, :, 0:2 * (D + 1)],
                                   ACT.Copy).then_inc(AH1.sem, 1)
                if g3:
                    wait(act, VK, "gap", g3.s)
                    act.activation(r.egap[:], r.gap[:], ACT.Exp).then_inc(AR2.sem, 1)

            five_deep(act, body)
            pad_queues(act, c, table, c.queue0, E0, 1)
            write_table(act, c, table, E0)
            act.wait_ge(product_made, 1)
            for l in range(LAYERS):
                act.activation(c.w_agg[:, l, :], (ps_t, ps_p, ps_o)[l][:, 0:3 * D], ACT.Copy)

        @block.tensor
        def _(pe):
            pe.wait_ge(c.constants_made, 1)
            pe.wait_ge(loaded, 16 * 5)
            pe.matmul(ps_t[:, 0:2], wT_sb[:], a2_sb[:], start=True, stop=True).then_inc(ready, 1)
            pe.wait_ge(ready, 2)

            def body(g0, g1, g2, g3, g4):
                if g3:
                    wait(pe, AN2, "normed", g3.s)
                    wait(pe, AR1, "rT", g3.back(1))
                    for t in range(G):
                        last = pe.transpose(ps_r[:, t * P:(t + 1) * P], xn2[:, t, :], c.ident[:])
                    last.then_inc(QR1.sem, 1)
                    wait(pe, AR1, "rT", g3.s)
                    wait(pe, VK, "carried", g3.back(1))
                    for t in range(G):
                        last = pe.matmul(r.ps_score[:, t * E0:(t + 1) * E0], rT[:, t * P:(t + 1) * P], gw_sb[:],
                                         start=True, stop=True)
                    last.then_inc(QR1.sem, 1)
                if g1:
                    wait(pe, AA, "exp", g1.s)
                    wait(pe, AA, "pT", g1.back(1))
                    for t in range(G):
                        last = pe.transpose(ps_p[:, t * P:(t + 1) * P], pbd[:, t, :], c.ident[:])
                    last.then_inc(QA.sem, 1)
                if g0:
                    wait(pe, AN1, "normed", g0.s)
                    wait(pe, AX1, "xnT", g0.back(1))
                    for t in range(G):
                        last = pe.transpose(ps_t[:, t * P:(t + 1) * P], xn[:, t, :], c.ident[:])
                    last.then_inc(QX.sem, 1)
                if g3:
                    route_tensor(pe, c, r, VS, VK, QR2, g3, E0)
                if g1:
                    wait(pe, AA, "pT", g1.s)
                    wait(pe, VU, "z", g1.back(1))
                    for t in range(G):
                        last = pe.matmul(ps_o[:, t * P:(t + 1) * P], pT[:, t * P:(t + 1) * P],
                                         h[g1.b][:, t, 0:D], start=True, stop=True)
                    last.then_inc(QA.sem, 1)
                if g0:
                    wait(pe, AX1, "xnT", g0.s)
                    wait(pe, AH1, "h", g0.back(1))
                    for t in range(G):
                        last = pe.matmul(ps_h[:, t // 2, (t % 2) * (D + 1):(t % 2 + 1) * (D + 1)],
                                         xnT[:, t * P:(t + 1) * P], w_sb[:], start=True, stop=True)
                    last.then_inc(QX.sem, 1)
                if g0:
                    wait(pe, VA, "e", g0.back(1))
                    for q in range(2):
                        last = pe.matmul(ps_s[q * N:(q + 1) * N, :], wa2_wide[:],
                                         xnT[:].rearrange("p (t q n) -> p t q n", t=G, q=2)[:, :, q, :],
                                         start=True, stop=True)
                    last.then_inc(QX.sem, 1)

            five_deep(pe, body)
            pe.wait_ge(small_loaded, 16 * len(small_weights))
            wait(pe, AX1, "xnT", NG - 1)
            wait(pe, AA, "pT", NG - 1)
            wait(pe, VU, "z", NG - 1)
            for l in range(LAYERS):
                last = pe.matmul((ps_t, ps_p, ps_o)[l][:, 0:3 * D], c.gnn_w[:, l * D:(l + 1) * D], c.w_ih[:],
                                 start=True, stop=True)
            last.then_inc(product_made, 1)


def gru_and_routing(nc, c, adj, weights):
    pairs, layers = NG // 2, LAYERS
    with ExitStack() as ctx:
        def sb(name, shape, dt=F32):
            return ctx.enter_context(nc.sbuf_tensor("g_" + name, shape, dt))

        def pb(name, shape, dt=F32):
            return ctx.enter_context(nc.psum_tensor("g_" + name, shape, dt))

        def sem(name):
            return ctx.enter_context(nc.semaphore("g_" + name))

        two = range(2)
        bsum = sb("bsum", [D, 3])
        y = [sb(f"y{b}", [P, G, TOPK, D]) for b in two]
        adj_sb = [sb(f"adj{b}", [P, G, N], I32) for b in two]
        edges = [sb(f"edges{b}", [P, G, P]) for b in two]
        head_norm, tail_norm = norm_buffers(sb, "head"), norm_buffers(sb, "tail")
        xn = sb("xn", [P, G, D])
        state = [[sb(f"state{l}_{b}", [D, GN]) for b in two] for l in range(layers + 1)]
        tok = [sb(f"tok{b}", [P, G, D]) for b in two]
        agg = [sb(f"agg{b}", [D, GN]) for b in two]
        rg = [sb(f"rg{b}", [D, GN]) for b in two]
        zg = [sb(f"zg{b}", [D, GN]) for b in two]
        cand = [sb(f"cand{b}", [D, GN]) for b in two]
        new = [sb(f"new{b}", [D, GN]) for b in two]
        rT = sb("rT", [P, GN])
        r = route_buffers(sb, pb, sem, "q_", E1)
        table = table_buffers(sb, sem, E1)

        ps_r, ps_z = pb("ps_r", [P, GN]), pb("ps_z", [P, GN])
        ps_n = [pb(f"ps_n{b}", [P, GN]) for b in two]
        ps_hn = [pb(f"ps_hn{b}", [P, GN]) for b in two]
        ps_m = pb("ps_m", [P, GN])
        ps_q = pb("ps_q", [P, GN])
        ps_rows = [ps_q, ps_m]
        r.ps_score = ps_q[:, 0:G * E1]
        r.ps_rank = ps_q[:, G * E1:G * E1 + (G + 1) * E1]

        bias_made = sem("bias_made")
        next_loaded = sem("next_weights_loaded")
        arrived = [sem(f"arrived{b}") for b in two]
        s_turned, s_agged, s_gates = sem("turned"), sem("agged"), sem("gates")
        s_tok, s_aggT, s_r, s_z, s_new = sem("tok"), sem("aggT"), sem("r"), sem("z"), sem("new")
        VR = Steps(sem("v_run"), "reset cand diff scaled state")
        VH = Steps(sem("v_head"), "add0 x2")
        VN = Steps(sem("v_head_norm"), "stats agg vare")
        VE = Steps(sem("v_edges"), "edges")
        QH, AH, GH = Steps(sem("q_head"), "turned"), Steps(sem("a_head"), "state"), Steps(sem("g_head"), "rstd shift")
        AN = Steps(sem("a_head_norm"), "normed")
        VT = Steps(sem("v_tail"), "x3 stats agg vare ids")
        VS = Steps(sem("v_scores"), "scores top where wheref hot0 hot1 both")
        VK = Steps(sem("v_ranks"), "ranked carried slot0 slot1 slots gap")
        QT1, QT2, QT3, QT4 = (Steps(sem(f"q_tail{k}"), n) for k, n in enumerate(("back", "turned", "scored", "ranked")))
        AT0, AT1 = Steps(sem("a_tail_norm"), "normed"), Steps(sem("a_tail_rows"), "rT rows_copied")
        AT2 = Steps(sem("a_tail_probs"), "p0 p1")
        GT = Steps(sem("g_tail"), "rstd shift")

        block = ctx.enter_context(nc.Block())

        def run_steps(eng, body):
            body(-1, True, False, False)
            body(0, True, True, False)
            body(1, True, True, True)
            with eng.Fori(2, pairs - 1) as n:
                body(n, True, True, True)
            body(pairs - 1, False, True, True)
            body(pairs, False, False, True)

        def u_of(n, layer, b):
            return n * 6 + (2 * layer + b)

        def after(eng, s, u, back=0):
            if type(u) is int and u - back < 0:
                return
            eng.wait_ge(s, u + (1 - back))

        def after_step(eng, steps, name, u, back=0):
            if type(u) is int and u - back < 0:
                return
            eng.wait_ge(steps.sem, u * 5 + (steps.names.index(name) + 1 - 5 * back))

        def group(n, b):
            return At(n, b)

        @block.sync
        def _(sp):
            def load(at):
                if type(at.s) is not int or at.s >= 2:
                    sp.wait_ge(arrived[at.b], 32 * at.half)
                    alone(sp, c)
                    wait(sp, VH, "x2", at.back(2))
                    alone(sp, c)
                    wait(sp, VE, "edges", at.back(2))
                    alone(sp, c)
                sp.dma_start(y[at.b][:], results_of(c.result0, at.s)).then_inc(arrived[at.b], 16)
                sp.dma_start(adj_sb[at.b][:], adj[bass.ds(at.s * GN, GN), :]
                             .rearrange("(t p) d -> p t d", p=P)).then_inc(arrived[at.b], 16)
                if behind(at, 2):
                    load_share(sp, weights, at.back(2), next_loaded)

            load(At(0, 0))
            load(At(0, 1))
            with sp.Fori(1, pairs) as i:
                load(At(i, 0))
                load(At(i, 1))
            for s in (NG - 2, NG - 1):
                load_share(sp, weights, s, next_loaded)
            sp.wait_ge(next_loaded, 16 * NG * len(weights))
            pad_queues(sp, c, table, c.queue1, E1, 0)
            wait_table(sp, table, E1)
            for b in two:
                sp.wait_ge(r.queued[b], 16 * TOPK * G * pairs)

        @block.gpsimd
        def _(pool):
            def body(n, has_head, has_run, has_tail):
                late = group(n - 2, 1) if has_tail and (type(n) is not int or n >= 2) else None
                if late:
                    queue_rows(pool, c, r, VK, AT1, c.queue1, late, 0, 4)
                if has_tail:
                    rstd_and_shift(pool, c, tail_norm, VT, GT, AT0, group(n - 1, 0))
                if late:
                    queue_rows(pool, c, r, VK, AT1, c.queue1, late, 4)
                if has_tail:
                    rstd_and_shift(pool, c, tail_norm, VT, GT, AT0, group(n - 1, 1))
                if has_head:
                    rstd_and_shift(pool, c, head_norm, VN, GH, AN, group(n + 1, 0))
                if has_head:
                    rstd_and_shift(pool, c, head_norm, VN, GH, AN, group(n + 1, 1))
                if has_tail:
                    queue_rows(pool, c, r, VK, AT1, c.queue1, group(n - 1, 0))
                if has_tail and not has_run:
                    queue_rows(pool, c, r, VK, AT1, c.queue1, group(n - 1, 1))

            run_steps(pool, body)

        @block.tensor
        def _(pe):
            def run(n, l, b, inside=None):
                u = u_of(n, l, b)
                h = state[l][b]
                at = group(n, b)
                if l == 0:
                    wait(pe, AH, "state", at.s)
                else:
                    after_step(pe, VR, "state", u, 2)
                after_step(pe, VR, "cand", u, 2)
                for t in range(G):
                    last = pe.transpose(ps_n[b][:, t * P:(t + 1) * P], h[:, t * P:(t + 1) * P], c.ident[:])
                last.then_inc(s_turned, 1)
                pe.matmul(ps_hn[b][:], c.w_hh[:, 2 * D:3 * D], h[:], start=True, stop=True)
                after(pe, s_tok, u)
                if l == 0:
                    wait(pe, VE, "edges", at.s)
                for t in range(G):
                    last = pe.matmul(ps_n[b][:, t * P:(t + 1) * P], tok[b][:, t, :], edges[b][:, t, :],
                                     start=True, stop=True)
                last.then_inc(s_agged, 1)
                if inside:
                    inside()
                after(pe, s_z, u, 1)
                pe.matmul(ps_r[:], c.w_hh[:, 0:D], h[:], start=True, stop=False)
                pe.matmul(ps_z[:], c.w_hh[:, D:2 * D], h[:], start=True, stop=False)
                after(pe, s_aggT, u)
                pe.matmul(ps_r[:], c.w_agg[:, l, 0:D], agg[b][:], start=False, stop=True)
                pe.matmul(ps_z[:], c.w_agg[:, l, D:2 * D], agg[b][:], start=False, stop=True)
                pe.matmul(ps_n[b][:], c.w_agg[:, l, 2 * D:3 * D], agg[b][:], start=True,
                          stop=True).then_inc(s_gates, 1)

            def head(at):
                wait(pe, AN, "normed", at.s)
                wait(pe, AH, "state", at.s - 1)
                for t in range(G):
                    last = pe.transpose(ps_m[:, t * P:(t + 1) * P], xn[:, t, :], c.ident[:])
                last.then_inc(QH.sem, 1)

            def tail_back(n, b):
                after_step(pe, VR, "state", u_of(n - 1, 2, b))
                for t in range(G):
                    last = pe.transpose(ps_m[:, t * P:(t + 1) * P], state[layers][b][:, t * P:(t + 1) * P],
                                        c.ident[:])
                last.then_inc(QT1.sem, 1)

            def tail_turn(at):
                wait(pe, AT0, "normed", at.s)
                for t in range(G):
                    last = pe.transpose(ps_rows[at.b][:, t * P:(t + 1) * P], r.rows[0][at.b][:, t, 0:D], c.ident[:])
                last.then_inc(QT2.sem, 1)

            def tail_score(at):
                wait(pe, AT1, "rT", at.s)
                for t in range(G):
                    last = pe.matmul(r.ps_score[:, t * E1:(t + 1) * E1], rT[:, t * P:(t + 1) * P], c.gate1_w[:],
                                     start=True, stop=True)
                last.then_inc(QT3.sem, 1)

            def body(n, has_head, has_run, has_tail):
                pa = [group(n - 1, b) for b in two] if has_tail else None
                nx = [group(n + 1, b) for b in two] if has_head else None
                if has_run:
                    run(n, 0, 0, lambda: head(group(n, 1)))
                if has_tail:
                    if has_run:
                        wait(pe, AH, "state", At(n, 1).s)
                    wait(pe, AT1, "rT", pa[0].s - 1)
                    tail_back(n, 0)
                if has_run:
                    run(n, 0, 1)
                if has_tail:
                    wait(pe, VT, "x3", pa[0].s)
                    tail_back(n, 1)

                def first_turn():
                    wait(pe, VK, "carried", pa[0].s - 1)
                    tail_turn(pa[0])

                if has_run:
                    run(n, 1, 0, first_turn if has_tail else None)
                elif has_tail:
                    first_turn()
                if has_tail:
                    tail_score(pa[0])
                    wait(pe, VT, "x3", pa[1].s)
                    tail_turn(pa[1])
                if has_run:
                    run(n, 1, 1)
                if has_tail:
                    tail_rank(pa[0])
                    if not has_run:
                        wait(pe, VK, "carried", pa[0].s)
                    tail_score(pa[1])
                if has_run:
                    run(n, 2, 0)
                if has_head:
                    if has_tail:
                        wait(pe, AT1, "rT", pa[1].s)
                    head(nx[0])
                if has_tail and not has_head:
                    tail_rank(pa[1])
                if has_run:
                    run(n, 2, 1)
                if has_tail and has_head:
                    tail_rank(pa[1])

            def tail_rank(at):
                route_tensor(pe, c, r, VS, VK, QT4, at, E1)

            run_steps(pe, body)

        @block.scalar
        def _(act):
            act.wait_ge(bias_made, 1)

            def tok_out(n, l, b):
                u = u_of(n, l, b)
                after(act, s_turned, u)
                act.activation(tok[b][:].rearrange("p t d -> p (t d)"), ps_n[b][:], ACT.Copy).then_inc(s_tok, 1)

            def agg_out(n, l, b):
                u = u_of(n, l, b)
                after(act, s_agged, u)
                act.activation(agg[b][:], ps_n[b][:], ACT.Copy).then_inc(s_aggT, 1)

            def gate_r(n, l, b):
                u = u_of(n, l, b)
                after(act, s_gates, u)
                after_step(act, VR, "scaled", u, 2)
                act.activation(rg[b][:], ps_r[:], ACT.Sigmoid, bias=bsum[:, 0:1]).then_inc(s_r, 1)

            def gate_z(n, l, b):
                act.activation(zg[b][:], ps_z[:], ACT.Sigmoid, bias=bsum[:, 1:2]).then_inc(s_z, 1)

            def new_out(n, l, b):
                u = u_of(n, l, b)
                after_step(act, VR, "cand", u)
                act.activation(new[b][:], cand[b][:], ACT.Tanh, bias=c.b_ih[:, 2:3]).then_inc(s_new, 1)

            def tail_rows(at):
                wait(act, QT2, "turned", at.s)
                wait(act, QT3, "scored", at.back(1))
                act.activation(rT[:], ps_rows[at.b][:], ACT.Copy).then_inc(AT1.sem, 1)
                act.activation(r.rows[1][at.b][:, :, 0:D], r.rows[0][at.b][:, :, 0:D], ACT.Copy).then_inc(AT1.sem, 1)

            def tail_probs(at):
                wait(act, VK, "gap", at.s)
                act.activation(c.prob[:, 0, bass.ds(at.s * G, G)], r.gap[:], ACT.Sigmoid, scale=-1.0).then_inc(AT2.sem, 1)
                act.activation(c.prob[:, 1, bass.ds(at.s * G, G)], r.gap[:], ACT.Sigmoid).then_inc(AT2.sem, 1)

            def head(at):
                wait(act, QH, "turned", at.s)
                act.activation(state[0][at.b][:], ps_m[:], ACT.Copy).then_inc(AH.sem, 1)

            def norm_tail(at):
                if type(at.s) is not int or at.s >= 2:
                    act.wait_ge(r.queued[at.b], 16 * TOPK * G * at.half)
                normalise(act, c, tail_norm, GT, AT0, r.rows[0][at.b], at)

            def norm_head(at):
                wait(act, QH, "turned", at.back(1))
                normalise(act, c, head_norm, GH, AN, xn, at)

            def body(n, has_head, has_run, has_tail):
                pa = [group(n - 1, b) for b in two] if has_tail else None
                nx = [group(n + 1, b) for b in two] if has_head else None
                order = [(l, b) for l in range(layers) for b in two]
                for k, (l, b) in enumerate(order):
                    if has_run:
                        tok_out(n, l, b)
                    before = (n, *order[k - 1]) if k else (n - 1, *order[-1])
                    if has_run if k else has_tail:
                        gate_z(*before)
                    if k == 5 and has_head and has_run:
                        head(nx[0])
                    if has_run:
                        agg_out(n, l, b)
                    if k == 0 and has_run:
                        head(group(n, 1))
                    if has_run if k else has_tail:
                        new_out(*before)
                    if k == 1 and has_tail and (type(n) is not int or n >= 2):
                        tail_probs(group(n - 2, 1))
                    if k in (2, 3) and has_tail:
                        tail_rows(pa[k - 2])
                    if k in (1, 2) and has_tail:
                        norm_tail(pa[k - 1])
                    if k in (4, 5) and has_head:
                        norm_head(nx[k - 4])
                    if k == 5 and has_tail and not has_head:
                        tail_probs(pa[0])
                    if has_run:
                        gate_r(n, l, b)
                    if k == 5 and has_tail and has_head:
                        tail_probs(pa[0])
                if not has_run and not has_head:
                    tail_probs(pa[1])
                if not has_run and has_head:
                    head(nx[0])

            run_steps(act, body)
            pad_queues(act, c, table, c.queue1, E1, 1)
            write_table(act, c, table, E1)

        @block.vector
        def _(v):
            for b in two:
                v.memset(edges[b][:], 0.0)
            v.tensor_copy(c.carry[:], c.region[:, 0:E1])
            v.tensor_tensor(bsum[:], c.b_ih[:], c.b_hh[:], ALU.add).then_inc(bias_made, 1)

            def gates_1(n, l, b):
                u = u_of(n, l, b)
                after(v, s_r, u)
                v.scalar_tensor_tensor(out=cand[b][:], in0=ps_hn[b][:], scalar=c.b_hh[:, 2:3], in1=rg[b][:],
                                       op0=ALU.add, op1=ALU.mult).then_inc(VR.sem, 1)
                after_step(v, VR, "reset", u)
                v.tensor_tensor(cand[b][:], ps_n[b][:], cand[b][:], ALU.add).then_inc(VR.sem, 1)

            def gates_2(n, l, b):
                u = u_of(n, l, b)
                after(v, s_new, u)
                v.tensor_tensor(rg[b][:], state[l][b][:], new[b][:], ALU.subtract).then_inc(VR.sem, 1)
                after_step(v, VR, "diff", u)
                v.tensor_tensor(rg[b][:], rg[b][:], zg[b][:], ALU.mult).then_inc(VR.sem, 1)
                after_step(v, VR, "scaled", u)
                if l == layers - 1:
                    if type(n) is not int or n >= 1:
                        wait(v, QT1, "back", group(n - 1, b).s)
                v.tensor_tensor(state[l + 1][b][:], rg[b][:], new[b][:], ALU.add).then_inc(VR.sem, 1)

            def add_result(at, k):
                v.wait_ge(arrived[at.b], 32 * at.half + 32)
                if k:
                    wait(v, VH, "add0", at.s)
                for t in range(G):
                    last = combine(v, c, y[at.b], t, k, at.s)
                last.then_inc(VH.sem, 1)

            def head_stats(at):
                wait(v, VH, "x2", at.s)
                statistics(v, c, head_norm, VN, GH, at)

            def make_edges(at):
                v.wait_ge(arrived[at.b], 32 * at.half + 32)
                for q in two:
                    rows = slice(q * N, (q + 1) * N)
                    last = v.tensor_scalar(edges[at.b][rows, :, q * N:(q + 1) * N], adj_sb[at.b][rows, :, :], 0.0,
                                           None, ALU.not_equal)
                last.then_inc(VE.sem, 1)

            def tail_1(at):
                wait(v, QT1, "back", at.s)
                xs = c.x[:, bass.ds(at.s * G, G), :]
                v.tensor_tensor(xs, ps_m[:].rearrange("p (t d) -> p t d", t=G), xs, ALU.add).then_inc(VT.sem, 1)

            def tail_2(at):
                wait(v, VT, "x3", at.s)
                statistics(v, c, tail_norm, VT, GT, at)

            def tail_ids(at):
                if type(at.s) is not int or at.s >= 2:
                    v.wait_ge(r.queued[at.b], 16 * TOPK * G * at.half)
                for k in range(TOPK):
                    last = v.tensor_copy(r.rows[k][at.b][:, :, D:ROW].bitcast(I32),
                                         c.ids[:, k, bass.ds(at.s * G, G)].unsqueeze(2))
                last.then_inc(VT.sem, 1)

            def body(n, has_head, has_run, has_tail):
                pa = [group(n - 1, b) for b in two] if has_tail else None
                nx = [group(n + 1, b) for b in two] if has_head else None
                for k, (l, b) in enumerate([(l, b) for l in range(layers) for b in two]):
                    if k in (0, 1) and has_tail:
                        tail_1(pa[k])
                    if k == 5 and has_tail and not has_head:
                        route_vector_2(v, c, r, VK, AT2, QT4, pa[1], E1)
                    if has_run:
                        gates_1(n, l, b)
                    if k in (0, 1) and has_tail:
                        tail_2(pa[k])
                        tail_ids(pa[k])
                    if k == 3 and has_tail and not has_run:
                        route_vector_2(v, c, r, VK, AT2, QT4, pa[0], E1)
                    if k in (2, 3) and has_tail:
                        route_vector(v, c, r, VS, QT3, pa[k - 2], E1, c.gate1_b[:], QT4)
                    if k == 4 and has_tail and has_run:
                        route_vector_2(v, c, r, VK, AT2, QT4, pa[0], E1)
                    if k in (4, 5) and has_head:
                        make_edges(nx[k - 4])
                    if k == 5 and has_tail and has_head:
                        route_vector_2(v, c, r, VK, AT2, QT4, pa[1], E1)
                    if has_run:
                        gates_2(n, l, b)
                    if k in (0, 1) and has_head:
                        add_result(nx[0], k)
                    if k == 2 and has_head:
                        head_stats(nx[0])
                        add_result(nx[1], 0)
                    if k == 3 and has_head:
                        add_result(nx[1], 1)
                        head_stats(nx[1])

            run_steps(v, body)
            tile_table(v, c, table, E1)


class Tile:

    def __init__(self, i, k):
        self.i, self.k = i + k // UNROLL if k >= 0 or type(i) is int else i - (-(k // UNROLL)), k % UNROLL
        self.j = self.i * UNROLL + self.k

    def done(self, back=0):
        return self.j + (1 - back) if back <= 1 else self.j - (back - 1)

    def first(self, n):
        return type(self.i) is int and self.j < n


def experts(nc, c, layer, queue, result, experts_n, chunks, up, down, up_b, down_b):
    tiles = tiles_of(experts_n)
    wide = 512
    with ExitStack() as ctx:
        def sb(name, shape, dt=F32):
            return ctx.enter_context(nc.sbuf_tensor(f"e{layer}_" + name, shape, dt))

        def pb(name, shape, dt=F32):
            return ctx.enter_context(nc.psum_tensor(f"e{layer}_" + name, shape, dt))

        def sem(name):
            return ctx.enter_context(nc.semaphore(f"e{layer}_" + name))

        xq = [sb(f"xq{k}", [P, ROW]) for k in range(UNROLL)]
        xT = [sb(f"xT{b}", [P, P]) for b in range(2)]
        up_of = [sb(f"up_of{b}", [P, wide]) for b in range(2)]
        th = sb("th", [P, H1])
        gated = [sb(f"gated{b}", [P, H1]) for b in range(2)]
        hT = [sb(f"hT{b}", [P, chunks * P]) for b in range(4)]
        ids = [sb(f"ids{k}", [P, 1]) for k in range(UNROLL)]
        y = [sb(f"y{k}", [P, D]) for k in range(UNROLL)]
        ps_x = [pb(f"ps_x{b}", [P, 512]) for b in range(2)]
        ps_h = [pb(f"ps_h{b}", [P, wide]) for b in range(2)]
        ps_y = [pb(f"ps_y{b}", [P, 512]) for b in range(2)]
        arrived = [sem(f"arrived{k}") for k in range(UNROLL)]
        x_turned, xT_copied, h_made, hT_ready = sem("x_turned"), sem("xT_copied"), sem("h_made"), sem("hT_ready")
        up_copied, ids_copied = sem("up_copied"), sem("ids_copied")
        h_tanh, h_gated, y_made, y_copied = sem("h_tanh"), sem("h_gated"), sem("y_made"), sem("y_copied")
        sent = [sem(f"sent{k}") for k in range(UNROLL)]

        def steps(eng, body, weights_used=False):
            held = []

            def step(i, k):
                lagged = [Tile(i, k - lag) for lag in (0, 1, 3)]
                if weights_used:
                    for lag, t in zip((0, 1, 3), lagged):
                        t.held, t.word = held, (k - lag) // PACK + 1
                if type(i) is int:
                    lagged = [t if 0 <= t.j < tiles else None for t in lagged]
                body(*lagged, lambda: load_words(i, k))

            def load_words(i, k):
                if weights_used and k == 0:
                    row = c.tile_experts[0:1, bass.ds(i, 1), :].rearrange("p i w -> p (i w)")
                    held[:] = [nc.values_load_multi_w_load_instructions(
                        row, engines=[eng.engine], min_val=0, max_val=(1 << (BITS * PACK)) - 1,
                        skip_runtime_bounds_check_because="expert_of masks what it takes from a word")[1]]

            for k in range(UNROLL):
                step(0, k)
            with eng.Fori(1, tiles // UNROLL) as i:
                for k in range(UNROLL):
                    step(i, k)
            for k in range(3):
                step(tiles // UNROLL, k)

        block = ctx.enter_context(nc.Block())

        @block.sync
        def _(sp):
            def load(t):
                at = sp.value_load(c.tile_row[0:1, bass.ds(t.j, 1)], min_val=0,
                                   max_val=experts_n * (REGION + P) - P)
                if not t.first(UNROLL):
                    sp.wait_ge(ids_copied, t.done(UNROLL))
                    alone(sp, c)
                    sp.wait_ge(x_turned, t.done(UNROLL))
                    alone(sp, c)
                sp.dma_start(xq[t.k][:], queue[bass.ds(at, P), :]).then_inc(arrived[t.k], 16)

            for k in range(UNROLL):
                load(Tile(0, k))
            with sp.Fori(1, tiles // UNROLL) as i:
                for k in range(UNROLL):
                    load(Tile(i, k))

        @block.gpsimd
        def _(pool):
            def send(t0, t1, t3, words):
                if t3 is None:
                    return
                pool.wait_ge(y_copied, t3.done())
                alone(pool, c)
                pool.indirect_dma_start(
                    out=result, out_offset=bass.IndirectOffsetOnAxis(ap=ids[t3.k][:].bitcast(U32), axis=0),
                    in_=y[t3.k][:], in_offset=None).then_inc(sent[t3.k], 16)

            steps(pool, send)
            for k in range(UNROLL):
                pool.wait_ge(sent[k], 16 * tiles // UNROLL)

        def expert_of(t):
            return (t.held[0][t.word] >> (BITS * (t.k % PACK))) & (experts_n - 1)

        @block.tensor
        def _(pe):
            def body(t0, t1, t3, words):
                if t0:
                    pe.wait_ge(arrived[t0.k], 16 * (t0.i + 1))
                    if not t0.first(2):
                        pe.wait_ge(xT_copied, t0.done(2))
                    pe.transpose(ps_x[t0.k % 2][:, 0:P], xq[t0.k][:, 0:D], c.ident[:]).then_inc(x_turned, 1)
                if t1:
                    pe.wait_ge(xT_copied, t1.done())
                    pe.wait_ge(up_copied, t1.done())
                    if not t1.first(2):
                        pe.wait_ge(hT_ready, t1.done(2))
                    for q in range(wide // P):
                        last = pe.matmul(ps_h[t1.k % 2][:, q * P:(q + 1) * P],
                                         up_of[t1.k % 2][:, q * P:(q + 1) * P], xT[t1.k % 2][:],
                                         start=True, stop=True)
                    last.then_inc(h_made, 1)
                words()
                if t3:
                    e3 = expert_of(t3)
                    pe.wait_ge(hT_ready, t3.done())
                    if not t3.first(2):
                        pe.wait_ge(y_copied, t3.done(2))
                    for q in range(chunks):
                        last = pe.matmul(ps_y[t3.k % 2][:, 0:D], hT[t3.k % 4][:, q * P:(q + 1) * P],
                                         down[:, bass.ds(e3 * (chunks * P) + q * P, P)],
                                         start=(q == 0), stop=(q == chunks - 1))
                    last.then_inc(y_made, 1)

            steps(pe, body, True)

        @block.scalar
        def _(act):
            def body(t0, t1, t3, words):
                if t0:
                    act.wait_ge(x_turned, t0.done())
                    if not t0.first(2):
                        act.wait_ge(h_made, t0.done(2))
                    act.activation(xT[t0.k % 2][:], ps_x[t0.k % 2][:, 0:P], ACT.Copy).then_inc(xT_copied, 1)
                words()
                if t0 and layer == 1:
                    act.activation(up_of[t0.k % 2][:], up[:, bass.ds(expert_of(t0) * wide, wide)],
                                   ACT.Copy).then_inc(up_copied, 1)
                if t1 and layer == 0:
                    e1 = expert_of(t1)
                    act.wait_ge(h_made, t1.done())
                    if not t1.first(4):
                        act.wait_ge(y_made, t1.done(4))
                    for q in range(chunks):
                        cols = slice(q * P, (q + 1) * P)
                        last = act.activation(hT[t1.k % 4][:, cols], ps_h[t1.k % 2][:, cols], ACT.Relu,
                                              bias=up_b[:, bass.ds(e1 * chunks + q, 1)])
                    last.then_inc(hT_ready, 1)
                if t1 and layer == 1:
                    act.wait_ge(h_made, t1.done())
                    if not t1.first(1):
                        act.wait_ge(h_gated, t1.done(1))
                    act.activation(th[:], ps_h[t1.k % 2][:, 0:H1], ACT.Tanh, scale=0.5).then_inc(h_tanh, 1)

            steps(act, body, True)

        @block.vector
        def _(v):
            def body(t0, t1, t3, words):
                if t0:
                    v.wait_ge(arrived[t0.k], 16 * (t0.i + 1))
                    if not t0.first(UNROLL):
                        v.wait_ge(sent[t0.k], t0.i * 16)
                    v.tensor_copy(ids[t0.k][:], xq[t0.k][:, D:ROW]).then_inc(ids_copied, 1)
                words()
                if t0 and layer == 0:
                    if not t0.first(2):
                        v.wait_ge(h_made, t0.done(2))
                    v.tensor_copy(up_of[t0.k % 2][:], up[:, bass.ds(expert_of(t0) * wide, wide)]
                                  ).then_inc(up_copied, 1)
                if t1 and layer == 1:
                    v.wait_ge(h_tanh, t1.done())
                    v.scalar_tensor_tensor(out=gated[t1.k % 2][:], in0=th[:], scalar=1.0, in1=ps_h[t1.k % 2][:, 0:H1],
                                           op0=ALU.add, op1=ALU.mult).then_inc(h_gated, 1)
                    v.wait_ge(h_gated, t1.done())
                    if not t1.first(4):
                        v.wait_ge(y_made, t1.done(4))
                    v.scalar_tensor_tensor(out=hT[t1.k % 4][:], in0=gated[t1.k % 2][:], scalar=0.5,
                                           in1=ps_h[t1.k % 2][:, H1:2 * H1], op0=ALU.mult,
                                           op1=ALU.mult).then_inc(hT_ready, 1)
                if t3:
                    v.wait_ge(y_made, t3.done())
                    if layer == 0:
                        e3 = expert_of(t3)
                        v.tensor_tensor(y[t3.k][:], ps_y[t3.k % 2][:, 0:D], down_b[:, bass.ds(e3 * D, D)],
                                        ALU.add).then_inc(y_copied, 1)
                    else:
                        v.tensor_copy(y[t3.k][:], ps_y[t3.k % 2][:, 0:D]).then_inc(y_copied, 1)

            steps(v, body, layer == 0)


def combine(v, c, y, t, k, g):
    tile = g * G + t
    return v.scalar_tensor_tensor(out=c.x[:, tile, :], in0=y[:, t, k, :],
                                  scalar=c.prob[:, k, bass.ds(tile, 1)], in1=c.x[:, tile, :],
                                  op0=ALU.mult, op1=ALU.add)


def results_of(result, s):
    return result[bass.ds(s * (TOPK * GN), TOPK * GN), :].rearrange("(t p k) d -> p t k d", p=P, k=TOPK)


def combine_out(nc, c, out):
    buffers = 4
    with ExitStack() as ctx:
        def sem(name):
            return ctx.enter_context(nc.semaphore("o_" + name))

        y = [ctx.enter_context(nc.sbuf_tensor(f"o_y{b}", [P, G, TOPK, D], F32)) for b in range(buffers)]
        arrived = [sem(f"arrived{b}") for b in range(buffers)]
        scaled, first_added, added, stored = sem("scaled"), sem("first_added"), sem("added"), sem("stored")
        block = ctx.enter_context(nc.Block())

        @block.sync
        def _(sp):
            def load(s, b):
                sp.dma_start(y[b][:], results_of(c.result1, s)).then_inc(arrived[b], 16)

            def store(s):
                sp.wait_ge(added, s + 1)
                alone(sp, c)
                sp.dma_start(out[bass.ds(s * GN, GN), :].rearrange("(t p) d -> p t d", p=P),
                             c.x[:, bass.ds(s * G, G), :]).then_inc(stored, 16)

            for s in range(buffers):
                load(s, s)
            with sp.Fori(0, NG // buffers - 1) as i:
                for b in range(buffers):
                    store(i * buffers + b)
                    load(i * buffers + (b + buffers), b)
            for s in range(NG - buffers, NG):
                store(s)
            sp.wait_ge(stored, 16 * NG)

        @block.scalar
        def _(act):
            with act.Fori(0, NG // buffers) as i:
                for b in range(buffers):
                    act.wait_ge(arrived[b], (i + 1) * 16)
                    for t in range(G):
                        last = act.activation(y[b][:, t, 1, :], y[b][:, t, 1, :], ACT.Copy,
                                              scale=c.prob[:, 1, bass.ds((i * buffers + b) * G + t, 1)])
                    last.then_inc(scaled, 1)

        @block.vector
        def _(v):
            with v.Fori(0, NG // buffers) as i:
                for b in range(buffers):
                    s = i * buffers + b
                    v.wait_ge(arrived[b], (i + 1) * 16)
                    for t in range(G):
                        last = combine(v, c, y[b], t, 0, s)
                    last.then_inc(first_added, 1)
                    v.wait_ge(first_added, s + 1)
                    v.wait_ge(scaled, s + 1)
                    xs = c.x[:, bass.ds(s * G, G), :]
                    v.tensor_tensor(xs, y[b][:, :, 1, :], xs, ALU.add).then_inc(added, 1)


def lay_out(x, adj, L0_gnn_W, L0_gnn_a, L0_ffn_Wg, L0_ffn_bg, L0_ffn_W1, L0_ffn_b1, L0_ffn_W2, L0_ffn_b2,
            L1_gnn_weight, L1_gnn_w_ih, L1_gnn_w_hh, L1_gnn_b_ih, L1_gnn_b_hh, L1_ffn_gate_w, L1_ffn_gate_b,
            L1_ffn_w1, L1_ffn_w2, L1_ffn_w3):
    import numpy as np
    a = {
        "x": x.reshape(TOKENS, D),
        "adj": adj.reshape(TOKENS, N),
        "gat_w": L0_gnn_W,
        "gat_wT": L0_gnn_W.T,
        "gat_a2": L0_gnn_a.reshape(2, D).T,
        "gate0_w": L0_ffn_Wg.T,
        "gate0_b": L0_ffn_bg,
        "w1": L0_ffn_W1.transpose(2, 0, 1).reshape(D, E0 * H0),
        "b1": L0_ffn_b1.reshape(E0 * H0 // P, P).T,
        "w2": L0_ffn_W2.reshape(E0, D, H0 // P, P).transpose(3, 0, 2, 1).reshape(P, E0 * H0),
        "b2": L0_ffn_b2.reshape(E0 * D),
        "gnn_wT": L1_gnn_weight.transpose(2, 0, 1).reshape(D, 3 * D),
        "w_ihT": L1_gnn_w_ih.T,
        "w_hhT": L1_gnn_w_hh.T,
        "b_ih": L1_gnn_b_ih.reshape(3, D).T,
        "b_hh": L1_gnn_b_hh.reshape(3, D).T,
        "gate1_w": L1_ffn_gate_w,
        "gate1_b": L1_ffn_gate_b,
        "w12": np.stack([L1_ffn_w1, L1_ffn_w2], axis=2).transpose(1, 0, 2, 3).reshape(D, E1 * 2 * H1),
        "w3": L1_ffn_w3.reshape(E1, H1 // P, P, D).transpose(2, 0, 1, 3).reshape(P, E1 * H1),
    }
    return {k: np.ascontiguousarray(v) for k, v in a.items()}


def kernel(**inputs):
    import numpy as np
    import concourse.bacc as bacc
    from concourse.bass_utils import run_bass_kernel_spmd

    arrays = lay_out(**{k: np.asarray(v) for k, v in inputs.items()})
    nc = bacc.Bacc("TRN2", target_bir_lowering=False, num_devices=1)
    args = [nc.dram_tensor(k, a.shape, mybir.dt.from_np(a.dtype), kind="ExternalInput").ap()
            for k, a in arrays.items()]
    args.append(nc.dram_tensor("out", (TOKENS, D), F32, kind="ExternalOutput").ap())
    program(nc, *args)
    r = run_bass_kernel_spmd(nc, [arrays], core_ids=[0])
    return r.results[0]["out"].reshape(GRAPHS, N, D)
```
